# Optimizing a Trainium2 kernel written in Bass

```python
import numpy as np
import jax
import jax.numpy as jnp

def _softmax(x, axis=-1):
    return jax.nn.softmax(x, axis=axis)

def _gelu(x):
    return jax.nn.gelu(x, approximate=True)

def _silu(x):
    return jax.nn.silu(x)

def _sigmoid(x):
    return jax.nn.sigmoid(x)

def _layernorm(x, axis=-1, eps=1e-05):
    m = jnp.mean(x, axis=axis, keepdims=True)
    v = jnp.var(x, axis=axis, keepdims=True)
    return (x - m) / jnp.sqrt(v + eps)

def _scatter_add(tgt, idx, src, axis=0):
    return tgt.at[idx].add(src)

def _segment_sum(src, seg, n):
    return jax.ops.segment_sum(src, seg, n)
kernel_name = 'mk_conv_seq_d1_conv_nchw256_r2_a9ddb2'

def setup_inputs(seed: int=0):
    np.random.seed(seed)
    _w = jnp.asarray

    def _rec_inputs():
        import jax
        import jax.numpy as jnp
        _gk = jax.random.key(seed)
        x = -0.0009896 + 1 * jax.random.normal(jax.random.fold_in(_gk, 1), (2, 128, 56, 56), jnp.float32)
        return x
    x = _rec_inputs()

    def _L0_conv_setup():
        import jax, jax.numpy as jnp
        import numpy as np
        from jax import lax
        DIM, HEADS, BS, TOPK, WIN = (128, 8, 8, 4, 7)
        HID = 2 * DIM
        B, H, W = (2, 56, 56)

        def _lin(x, w, b=None):
            y = jnp.einsum('...c,oc->...o', x, w)
            return y if b is None else y + b

        def _ln(x, w, b, eps=1e-06):
            mu = jnp.mean(x, -1, keepdims=True)
            var = jnp.mean((x - mu) ** 2, -1, keepdims=True)
            return (x - mu) * lax.rsqrt(var + eps) * w + b

        def _mha(Q, K, V, wq_w, wq_b, wk_w, wk_b, wv_w, wv_b, p_w, p_b):
            Bq, Nq, C = Q.shape
            h, d = (HEADS, C // HEADS)
            scale = d ** (-0.5)
            q = _lin(Q, wq_w, wq_b).reshape(Bq, Nq, h, d)
            k = _lin(K, wk_w, wk_b).reshape(Bq, -1, h, d)
            v = _lin(V, wv_w, wv_b).reshape(Bq, -1, h, d)
            attn = jax.nn.softmax(jnp.einsum('bnhd,bmhd->bhnm', q, k) * scale, axis=-1)
            out = jnp.einsum('bhnm,bmhd->bnhd', attn, v).reshape(Bq, Nq, C)
            return _lin(out, p_w, p_b)

        def _forward(x, pos_w, pos_b, n1_w, n1_b, n2_w, n2_b, wq_w, wq_b, wk_w, wk_b, wv_w, wv_b, pj_w, pj_b, s1_w, s1_b, s2_w, s2_b, g_w, g_b, pin_w, dw_w, pout_w):
            Bx, C, Hx, Wx = x.shape
            pos = lax.conv_general_dilated(x, pos_w, (1, 1), 'SAME', dimension_numbers=('NCHW', 'OIHW', 'NCHW'), feature_group_count=C)
            x = x + pos + pos_b[None, :, None, None] * 0 + pos_b[None, :, None, None]
            feat = jnp.transpose(x, (0, 2, 3, 1))
            Nq = Hx * Wx
            Q = feat.reshape(Bx, Nq, C)
            nH, nW = (Hx // BS, Wx // BS)
            nB = nH * nW
            blk = feat.reshape(Bx, nH, BS, nW, BS, C).transpose(0, 1, 3, 2, 4, 5)
            blk = blk.reshape(Bx, nB, BS * BS, C).mean(axis=2)
            hsc = jax.nn.gelu(_lin(blk, s1_w, s1_b), approximate=False)
            scores = _lin(hsc, s2_w, s2_b)[..., 0]
            topk = min(TOPK, nB)
            _, idx = lax.top_k(scores, topk)
            K_sel = jnp.take_along_axis(blk, idx[:, :, None], axis=1)
            y_cmp = _mha(Q, blk, blk, wq_w[0], wq_b[0], wk_w[0], wk_b[0], wv_w[0], wv_b[0], pj_w[0], pj_b[0])
            y_sel = _mha(Q, K_sel, K_sel, wq_w[1], wq_b[1], wk_w[1], wk_b[1], wv_w[1], wv_b[1], pj_w[1], pj_b[1])
            pad = WIN // 2
            padded = jnp.pad(feat, ((0, 0), (pad, pad), (pad, pad), (0, 0)), mode='edge')
            patches = jnp.stack([padded[:, dy:dy + Hx, dx:dx + Wx, :] for dy in range(WIN) for dx in range(WIN)], axis=3)
            patches = patches.reshape(Bx, Nq, WIN * WIN, C)
            h, d = (HEADS, C // HEADS)
            scale = d ** (-0.5)
            q = _lin(Q, wq_w[2], wq_b[2]).reshape(Bx, Nq, h, d)
            k = _lin(patches, wk_w[2], wk_b[2]).reshape(Bx, Nq, WIN * WIN, h, d)
            v = _lin(patches, wv_w[2], wv_b[2]).reshape(Bx, Nq, WIN * WIN, h, d)
            attn = jax.nn.softmax(jnp.einsum('bnhd,bnwhd->bnhw', q, k) * scale, axis=-1)
            y_win = jnp.einsum('bnhw,bnwhd->bnhd', attn, v).reshape(Bx, Nq, C)
            y_win = _lin(y_win, pj_w[2], pj_b[2])
            qn = _ln(Q, n1_w, n1_b)
            g = jax.nn.softmax(_lin(qn, g_w, g_b), axis=-1)
            y = g[..., 0:1] * y_cmp + g[..., 1:2] * y_sel + g[..., 2:3] * y_win + Q
            ym = y.reshape(Bx, Hx, Wx, C)
            t = _lin(ym, pin_w)
            t = lax.conv_general_dilated(t, dw_w, (1, 1), 'SAME', dimension_numbers=('NHWC', 'HWIO', 'NHWC'), feature_group_count=2 * HID)
            x1, x2 = jnp.split(t, 2, axis=-1)
            mlp = _lin(jax.nn.gelu(x1, approximate=False) * x2, pout_w)
            ym = _ln(ym + mlp, n2_w, n2_b)
            return jnp.transpose(ym, (0, 3, 1, 2))
        key = jax.random.key(seed)
        ks = jax.random.split(key, 16)
        s = 0.02
        C = DIM
        inp = {'x': jax.random.normal(ks[0], (B, C, H, W), jnp.float32), 'pos_w': jax.random.normal(ks[1], (C, 1, 3, 3), jnp.float32) * s, 'pos_b': jnp.zeros((C,), jnp.float32), 'n1_w': jnp.ones((C,), jnp.float32), 'n1_b': jnp.zeros((C,), jnp.float32), 'n2_w': jnp.ones((C,), jnp.float32), 'n2_b': jnp.zeros((C,), jnp.float32), 'wq_w': jax.random.normal(ks[2], (3, C, C), jnp.float32) * s, 'wq_b': jnp.zeros((3, C), jnp.float32), 'wk_w': jax.random.normal(ks[3], (3, C, C), jnp.float32) * s, 'wk_b': jnp.zeros((3, C), jnp.float32), 'wv_w': jax.random.normal(ks[4], (3, C, C), jnp.float32) * s, 'wv_b': jnp.zeros((3, C), jnp.float32), 'pj_w': jax.random.normal(ks[5], (3, C, C), jnp.float32) * s, 'pj_b': jnp.zeros((3, C), jnp.float32), 's1_w': jax.random.normal(ks[6], (C // 2, C), jnp.float32) * s, 's1_b': jnp.zeros((C // 2,), jnp.float32), 's2_w': jax.random.normal(ks[7], (1, C // 2), jnp.float32) * s, 's2_b': jnp.zeros((1,), jnp.float32), 'g_w': jax.random.normal(ks[8], (3, C), jnp.float32) * s, 'g_b': jnp.zeros((3,), jnp.float32), 'pin_w': jax.random.normal(ks[9], (2 * HID, C), jnp.float32) * s, 'dw_w': jax.random.normal(ks[10], (3, 3, 1, 2 * HID), jnp.float32) * s, 'pout_w': jax.random.normal(ks[11], (C, HID), jnp.float32) * s}
        return inp
    _L0_conv_all = _L0_conv_setup()
    _L0_conv_in = {k: v for k, v in _L0_conv_all.items() if k in ('pos_w', 'pos_b', 'n1_w', 'n1_b', 'n2_w', 'n2_b', 'wq_w', 'wq_b', 'wk_w', 'wk_b', 'wv_w', 'wv_b', 'pj_w', 'pj_b', 's1_w', 's1_b', 's2_w', 's2_b', 'g_w', 'g_b', 'pin_w', 'dw_w', 'pout_w')}
    del _L0_conv_all
    return {'x': x, 'L0_conv_pos_w': _L0_conv_in['pos_w'], 'L0_conv_pos_b': _L0_conv_in['pos_b'], 'L0_conv_n1_w': _L0_conv_in['n1_w'], 'L0_conv_n1_b': _L0_conv_in['n1_b'], 'L0_conv_n2_w': _L0_conv_in['n2_w'], 'L0_conv_n2_b': _L0_conv_in['n2_b'], 'L0_conv_wq_w': _L0_conv_in['wq_w'], 'L0_conv_wq_b': _L0_conv_in['wq_b'], 'L0_conv_wk_w': _L0_conv_in['wk_w'], 'L0_conv_wk_b': _L0_conv_in['wk_b'], 'L0_conv_wv_w': _L0_conv_in['wv_w'], 'L0_conv_wv_b': _L0_conv_in['wv_b'], 'L0_conv_pj_w': _L0_conv_in['pj_w'], 'L0_conv_pj_b': _L0_conv_in['pj_b'], 'L0_conv_s1_w': _L0_conv_in['s1_w'], 'L0_conv_s1_b': _L0_conv_in['s1_b'], 'L0_conv_s2_w': _L0_conv_in['s2_w'], 'L0_conv_s2_b': _L0_conv_in['s2_b'], 'L0_conv_g_w': _L0_conv_in['g_w'], 'L0_conv_g_b': _L0_conv_in['g_b'], 'L0_conv_pin_w': _L0_conv_in['pin_w'], 'L0_conv_dw_w': _L0_conv_in['dw_w'], 'L0_conv_pout_w': _L0_conv_in['pout_w']}

def reference(x, L0_conv_pos_w, L0_conv_pos_b, L0_conv_n1_w, L0_conv_n1_b, L0_conv_n2_w, L0_conv_n2_b, L0_conv_wq_w, L0_conv_wq_b, L0_conv_wk_w, L0_conv_wk_b, L0_conv_wv_w, L0_conv_wv_b, L0_conv_pj_w, L0_conv_pj_b, L0_conv_s1_w, L0_conv_s1_b, L0_conv_s2_w, L0_conv_s2_b, L0_conv_g_w, L0_conv_g_b, L0_conv_pin_w, L0_conv_dw_w, L0_conv_pout_w):
    import jax
    import jax.numpy as jnp

    def _L0_conv_ref(x, pos_w, pos_b, n1_w, n1_b, n2_w, n2_b, wq_w, wq_b, wk_w, wk_b, wv_w, wv_b, pj_w, pj_b, s1_w, s1_b, s2_w, s2_b, g_w, g_b, pin_w, dw_w, pout_w):
        import jax, jax.numpy as jnp
        import numpy as np
        from jax import lax
        DIM, HEADS, BS, TOPK, WIN = (128, 8, 8, 4, 7)
        HID = 2 * DIM
        B, H, W = (2, 56, 56)

        def _lin(x, w, b=None):
            y = jnp.einsum('...c,oc->...o', x, w)
            return y if b is None else y + b

        def _ln(x, w, b, eps=1e-06):
            mu = jnp.mean(x, -1, keepdims=True)
            var = jnp.mean((x - mu) ** 2, -1, keepdims=True)
            return (x - mu) * lax.rsqrt(var + eps) * w + b

        def _mha(Q, K, V, wq_w, wq_b, wk_w, wk_b, wv_w, wv_b, p_w, p_b):
            Bq, Nq, C = Q.shape
            h, d = (HEADS, C // HEADS)
            scale = d ** (-0.5)
            q = _lin(Q, wq_w, wq_b).reshape(Bq, Nq, h, d)
            k = _lin(K, wk_w, wk_b).reshape(Bq, -1, h, d)
            v = _lin(V, wv_w, wv_b).reshape(Bq, -1, h, d)
            attn = jax.nn.softmax(jnp.einsum('bnhd,bmhd->bhnm', q, k) * scale, axis=-1)
            out = jnp.einsum('bhnm,bmhd->bnhd', attn, v).reshape(Bq, Nq, C)
            return _lin(out, p_w, p_b)

        def _forward(x, pos_w, pos_b, n1_w, n1_b, n2_w, n2_b, wq_w, wq_b, wk_w, wk_b, wv_w, wv_b, pj_w, pj_b, s1_w, s1_b, s2_w, s2_b, g_w, g_b, pin_w, dw_w, pout_w):
            Bx, C, Hx, Wx = x.shape
            pos = lax.conv_general_dilated(x, pos_w, (1, 1), 'SAME', dimension_numbers=('NCHW', 'OIHW', 'NCHW'), feature_group_count=C)
            x = x + pos + pos_b[None, :, None, None] * 0 + pos_b[None, :, None, None]
            feat = jnp.transpose(x, (0, 2, 3, 1))
            Nq = Hx * Wx
            Q = feat.reshape(Bx, Nq, C)
            nH, nW = (Hx // BS, Wx // BS)
            nB = nH * nW
            blk = feat.reshape(Bx, nH, BS, nW, BS, C).transpose(0, 1, 3, 2, 4, 5)
            blk = blk.reshape(Bx, nB, BS * BS, C).mean(axis=2)
            hsc = jax.nn.gelu(_lin(blk, s1_w, s1_b), approximate=False)
            scores = _lin(hsc, s2_w, s2_b)[..., 0]
            topk = min(TOPK, nB)
            _, idx = lax.top_k(scores, topk)
            K_sel = jnp.take_along_axis(blk, idx[:, :, None], axis=1)
            y_cmp = _mha(Q, blk, blk, wq_w[0], wq_b[0], wk_w[0], wk_b[0], wv_w[0], wv_b[0], pj_w[0], pj_b[0])
            y_sel = _mha(Q, K_sel, K_sel, wq_w[1], wq_b[1], wk_w[1], wk_b[1], wv_w[1], wv_b[1], pj_w[1], pj_b[1])
            pad = WIN // 2
            padded = jnp.pad(feat, ((0, 0), (pad, pad), (pad, pad), (0, 0)), mode='edge')
            patches = jnp.stack([padded[:, dy:dy + Hx, dx:dx + Wx, :] for dy in range(WIN) for dx in range(WIN)], axis=3)
            patches = patches.reshape(Bx, Nq, WIN * WIN, C)
            h, d = (HEADS, C // HEADS)
            scale = d ** (-0.5)
            q = _lin(Q, wq_w[2], wq_b[2]).reshape(Bx, Nq, h, d)
            k = _lin(patches, wk_w[2], wk_b[2]).reshape(Bx, Nq, WIN * WIN, h, d)
            v = _lin(patches, wv_w[2], wv_b[2]).reshape(Bx, Nq, WIN * WIN, h, d)
            attn = jax.nn.softmax(jnp.einsum('bnhd,bnwhd->bnhw', q, k) * scale, axis=-1)
            y_win = jnp.einsum('bnhw,bnwhd->bnhd', attn, v).reshape(Bx, Nq, C)
            y_win = _lin(y_win, pj_w[2], pj_b[2])
            qn = _ln(Q, n1_w, n1_b)
            g = jax.nn.softmax(_lin(qn, g_w, g_b), axis=-1)
            y = g[..., 0:1] * y_cmp + g[..., 1:2] * y_sel + g[..., 2:3] * y_win + Q
            ym = y.reshape(Bx, Hx, Wx, C)
            t = _lin(ym, pin_w)
            t = lax.conv_general_dilated(t, dw_w, (1, 1), 'SAME', dimension_numbers=('NHWC', 'HWIO', 'NHWC'), feature_group_count=2 * HID)
            x1, x2 = jnp.split(t, 2, axis=-1)
            mlp = _lin(jax.nn.gelu(x1, approximate=False) * x2, pout_w)
            ym = _ln(ym + mlp, n2_w, n2_b)
            return jnp.transpose(ym, (0, 3, 1, 2))
        return _forward(x, pos_w, pos_b, n1_w, n1_b, n2_w, n2_b, wq_w, wq_b, wk_w, wk_b, wv_w, wv_b, pj_w, pj_b, s1_w, s1_b, s2_w, s2_b, g_w, g_b, pin_w, dw_w, pout_w)

    def _gn(v, G=32, eps=1e-05):
        B_, C_, H_, W_ = v.shape
        g = v.reshape(B_, G, C_ // G, H_, W_)
        m = jnp.mean(g, axis=(2, 3, 4), keepdims=True)
        s = jnp.var(g, axis=(2, 3, 4), keepdims=True)
        return ((g - m) / jnp.sqrt(s + eps)).reshape(v.shape)

    def _ln_c(v, eps=1e-06):
        m = jnp.mean(v, axis=1, keepdims=True)
        s = jnp.var(v, axis=1, keepdims=True)
        return (v - m) / jnp.sqrt(s + eps)

    def _ln_t(v, eps=1e-05):
        m = jnp.mean(v, axis=-1, keepdims=True)
        s = jnp.var(v, axis=-1, keepdims=True)
        return (v - m) / jnp.sqrt(s + eps)

    def _to_tokens(v):
        B_, C_, H_, W_ = v.shape
        return v.reshape(B_, C_, H_ * W_).transpose(0, 2, 1)

    def _from_tokens(t, like):
        B_, C_, H_, W_ = like.shape
        return t.transpose(0, 2, 1).reshape(B_, C_, H_, W_)
    x = _L0_conv_ref(x, L0_conv_pos_w, L0_conv_pos_b, L0_conv_n1_w, L0_conv_n1_b, L0_conv_n2_w, L0_conv_n2_b, L0_conv_wq_w, L0_conv_wq_b, L0_conv_wk_w, L0_conv_wk_b, L0_conv_wv_w, L0_conv_wv_b, L0_conv_pj_w, L0_conv_pj_b, L0_conv_s1_w, L0_conv_s1_b, L0_conv_s2_w, L0_conv_s2_b, L0_conv_g_w, L0_conv_g_b, L0_conv_pin_w, L0_conv_dw_w, L0_conv_pout_w)
    return x

_drawn_inputs = setup_inputs


def setup_inputs(seed=0):
    import zlib

    import numpy as np

    out = dict(_drawn_inputs(seed))
    spreads = {'L0_conv_pos_b': (0.0, 0.1),
     'L0_conv_n1_w': (1.0, 0.6),
     'L0_conv_n1_b': (0.0, 0.8),
     'L0_conv_n2_w': (1.0, 0.2),
     'L0_conv_n2_b': (0.0, 0.1),
     'L0_conv_wq_b': (0.0, 0.8),
     'L0_conv_wk_b': (0.0, 0.8),
     'L0_conv_wv_b': (0.0, 0.602),
     'L0_conv_pj_b': (0.0, 0.1),
     'L0_conv_s1_b': (0.0, 0.8),
     'L0_conv_g_b': (0.0, 0.8)}
    factors = {'L0_conv_wq_w': 8.0,
     'L0_conv_wk_w': 8.0,
     'L0_conv_wv_w': 8.0,
     'L0_conv_pj_w': 4.095,
     'L0_conv_s1_w': 8.0,
     'L0_conv_s2_w': 8.0,
     'L0_conv_g_w': 5.748,
     'L0_conv_pin_w': 8.0,
     'L0_conv_dw_w': 8.0,
     'L0_conv_pout_w': 8.0}
    for name, (base, spread) in spreads.items():
        noise = np.random.default_rng([zlib.crc32(name.encode()), seed]).standard_normal(out[name].shape)
        drawn = base * np.exp(spread * noise) if base else spread * noise
        out[name] = jnp.asarray(drawn.astype(out[name].dtype))
    for name, factor in factors.items():
        out[name] = (out[name] * factor).astype(out[name].dtype)
    return out
```

```python
from contextlib import ExitStack

import numpy as np

import concourse.bass as bass
from concourse import mybir

F32 = mybir.dt.float32
BF16 = mybir.dt.bfloat16
U32 = mybir.dt.uint32
ALU = mybir.AluOpType
ACT = mybir.ActivationFunctionType
AX = mybir.AxisListType
ds = bass.ds

C = 128
IMAGES = 2
SIDE = 56
PIX = SIDE * SIDE
HEADS, DH = 8, 16
BLOCK = 8
NBS = SIDE // BLOCK
NBLK = NBS * NBS
TOPK = 4
WIN = 7
PAD = WIN // 2
PSIDE = SIDE + 2 * PAD
PPIX = PSIDE * PSIDE
BANDS = SIDE // BLOCK
BAND = BLOCK * SIDE
SUBC = 7
SUB = BLOCK * SUBC
SUBS = SIDE // SUBC
TILE = 2 * SUB
TILES = SUBS // 2
KROWS = BLOCK + WIN - 1
KCOLS = SUBC + WIN - 1
HCOLS = (7, KCOLS - 7)
HKEYS = [n * KROWS for n in HCOLS]
KEYS = max(HKEYS)
KBAND = KROWS * PSIDE
TCOLS = 2 * SUBC + WIN - 1
PAIRS = HEADS // 2
VCOLS = 2 * DH + 1
KC = 2 * NBLK + 2 * TOPK
SC = PAIRS * KC
TERMS = ((0, 0), (0, 1), (1, 0), (1, 1), (0, 2), (2, 0))
MASK0 = len(TERMS) * DH
SHIFT0 = 126
HID = 2 * C
SCALE = float(DH) ** -0.5
EPS = 1e-6
BIG = 2.0 ** 99

WNAMES = ("wq0", "wq1", "wq2", "wk0", "wk1", "wk2", "wv0", "wv1", "wv2", "pj0", "pj1", "pj2")
WCOL = {n: C * k for k, n in enumerate(WNAMES)}
WCOL["s1"] = C * len(WNAMES)
WCOL["pin"] = WCOL["s1"] + C // 2
WCOL["pout"] = WCOL["pin"] + 2 * HID
NW = WCOL["pout"] + HID
V_POSW, V_POSB, V_N1W, V_N1B, V_N2W, V_N2B, V_BQ, V_BK, V_DW, V_S1B, V_S2, V_GW = 0, 9, 10, 11, 12, 13, 14, 17, 20, 56, 57, 58
NV = 61
R_BV, R_GB, R_S2B, NR = 0, 3 * C, 3 * C + 3, 3 * C + 4
CI, CH, CSEL, CVM, CIO, CM, CEM, CE = 0, 128, 136, 192, 260, 261, 264, 266
NC32 = CE + SC
TAPS = [(dy, dx) for dy in (-1, 0, 1) for dx in (-1, 0, 1)]
SIDE_TAPS = [t for t in range(9) if t != 4]


def shape_constants():
    c = np.zeros((128, NC32), np.float32)
    c[:, CI:CI + 128] = np.eye(128)
    c[:, CH:CH + HEADS] = np.arange(128)[:, None] // DH == np.arange(HEADS)
    for e in range(2):
        c[e * SUB:(e + 1) * SUB, CSEL:CSEL + SUB] = np.eye(SUB)
        c[e * SUB:(e + 1) * SUB, CEM + e] = 1
        for rows, o in ((slice(e * NBLK, (e + 1) * NBLK), 0), (slice(2 * NBLK + e * TOPK, 2 * NBLK + (e + 1) * TOPK), 1)):
            c[rows, CVM + o * 32 + e * DH:CVM + o * 32 + (e + 1) * DH] = 1
            c[rows, CVM + 64 + 2 * o + e] = 1
            for j in range(PAIRS):
                for part in range(2):
                    c[16 * part + 8 * o + 2 * j + e, CE + j * KC + rows.start:CE + j * KC + rows.stop] = 1
    c[:, CIO] = np.arange(128)
    for part in range(3):
        c[32 + part, CM + part] = 1
    ck = np.zeros((32, PSIDE, KROWS), np.float32)
    cq = np.zeros((32, SUBS, BLOCK, SUBC), np.float32)
    X, x = np.arange(PSIDE).reshape(-1, 1), np.arange(SIDE).reshape(SUBS, 1, SUBC)
    r = np.arange(BLOCK).reshape(1, BLOCK, 1)
    for j in range(14):
        ck[j, :, j] = 1
        cq[j] = np.where((j >= r) & (j < r + WIN), 0, -BIG)
        ck[14 + j] = X % 14 == j
        cq[14 + j] = np.where((j - x) % 14 < WIN, 0, -BIG)
    ck[28] = X % 28 < 6
    ck[29] = (X % 28 >= 14) & (X % 28 < 20)
    tile, rel = x // 14, x % 14
    cq[28] = np.where(tile % 2 == 0, np.where(rel >= 6, -BIG, 0), np.where(rel <= 7, -BIG, 0))
    cq[29] = np.where(tile % 2 == 1, np.where(rel >= 6, -BIG, 0), np.where(rel <= 7, -BIG, 0))
    ck[30:] = 1
    return c, np.concatenate([ck.reshape(32, -1), cq.reshape(32, -1)], 1)


def bc(ap, shape):
    return ap.broadcast_to(shape)


def build(nc, x, wts, vecs, rows, pjb, c32, cmask, out):
    ctx = ExitStack()
    with ctx:
        def sb(name, shape, dt=F32, stack=ctx):
            return stack.enter_context(nc.sbuf_tensor(name, shape, dt))

        sems = {}

        def sem(name):
            if name not in sems:
                sems[name] = ctx.enter_context(nc.semaphore(name))
            return sems[name]

        q_dram = nc.dram_tensor("q_parts", [3, C, IMAGES, PIX], BF16, kind="Internal").ap()
        k_dram = nc.dram_tensor("k_parts", [3, C, IMAGES, BANDS * KBAND], BF16, kind="Internal").ap()
        v_dram = nc.dram_tensor("v_rows", [IMAGES, PSIDE, PSIDE, PAIRS * VCOLS], F32, kind="Internal").ap()
        v_flat = v_dram.rearrange("i r c v -> i (r c) v")

        PS = ctx.enter_context(nc.psum_tensor("banks", [128, 8, 512], F32))

        W = sb("W", [128, NW])
        vec = sb("vec", [128, NV])
        row = sb("row", [1, NR])
        pjrow = sb("pjrow", [3, C])
        cst = sb("cst", [128, NC32])
        identb = sb("identb", [TILE, TILE], BF16)
        ones = sb("ones", [128, 128])
        meanw = sb("meanw", [128, 128])
        epsc = sb("epsc", [128, 1])
        X = sb("X", [128, IMAGES, PIX])
        G = sb("G", [TILE, IMAGES, BANDS, 12, 4])

        att = ctx.enter_context(ExitStack())
        FP = sb("FP", [128, IMAGES, PSIDE, PSIDE], F32, att)
        XT = sb("XT", [128, IMAGES, PIX], F32, att)
        XH = sb("XH", [128, IMAGES, PIX], BF16, att)
        XL = sb("XL", [128, IMAGES, PIX], BF16, att)
        bs1 = sb("bs1", [128, IMAGES, SIDE, NBS], F32, att)
        Af = [sb(f"Af{m}", [128, SC], F32, att) for m in range(IMAGES)]
        Ah = [sb(f"Ah{m}", [128, SC], BF16, att) for m in range(IMAGES)]
        Al = [sb(f"Al{m}", [128, SC], BF16, att) for m in range(IMAGES)]
        ES = [sb(f"ES{m}", [35, SC], BF16, att) for m in range(IMAGES)]
        VB = [sb(f"VB{m}", [KC, PAIRS, 68], F32, att) for m in range(IMAGES)]
        c1 = sb("c1", [128, 8], F32, att)
        BV2 = sb("BV2", [124, C], F32, att)

        def xt(img):
            return XT[:, img, :]

        with ExitStack() as s1:
            blk = sb("blk", [128, IMAGES, NBLK], F32, s1)
            hs = sb("hs", [64, IMAGES * NBLK], F32, s1)
            score = sb("score", [1, IMAGES, NBLK], F32, s1)
            top = sb("top", [1, IMAGES, 8], F32, s1)
            topi = sb("topi", [1, IMAGES, 8], U32, s1)
            topf = sb("topf", [1, IMAGES, 8], F32, s1)
            onehot = sb("onehot", [NBLK, IMAGES, 8], F32, s1)
            blkT = sb("blkT", [NBLK, IMAGES, C], F32, s1)
            R = sb("R", [128, IMAGES, KC], F32, s1)
            k0 = sb("k0", [128, NBLK], F32, s1)
            k1 = sb("k1", [128, TOPK], F32, s1)
            KM = sb("KM", [128, PAIRS, KC], F32, s1)
            bq35 = sb("bq35", [128, 2, 35], F32, s1)
            cs = sb("cs", [35, SC], F32, s1)
            ch = [sb(f"ch{n}", [35, SC], F32, s1) for n in range(3)]
            chb = sb("chb", [35, SC], BF16, s1)
            pk = [sb(f"pk{n}", [128, 3, 512], BF16, s1) for n in range(2)]
            pf = [sb(f"pf{n}", [128, 512], F32, s1) for n in range(2)]
            pr = sb("pr", [128, 512], F32, s1)
            pq = sb("pq", [128, 512], F32, s1)
            vst = [sb(f"vst{n}", [124, 4, PAIRS * VCOLS], F32, s1) for n in range(2)]
            gl = sb("gl", [128, 2, 4], F32, s1)
            n1rep = sb("n1rep", [128, TILE], F32, s1)
            cg = sb("cg", [TILE, 3], F32, s1)
            xc = [sb(f"xc{n}", [128, BAND], F32, s1) for n in range(2)]
            sq = [sb(f"sq{n}", [128, BAND], F32, s1) for n in range(2)]
            ls = [sb(f"ls{n}", [4, BAND], F32, s1) for n in range(2)]
            ls2 = [sb(f"ls2{n}", [4, SUBS, 2, SUB], F32, s1) for n in range(2)]
            NG = IMAGES * BANDS * 12
            gst = sb("gst", [TILE, NG], F32, s1)
            gmx = sb("gmx", [TILE, NG], F32, s1)
        with ExitStack() as s2:
            nm = sb("nm", [TILE, 16], F32, s2)
            nmb = [sb(f"nmb{n}", [TILE, 32], BF16, s2) for n in range(2)]
            cst35 = sb("cst35", [35, TILE], BF16, s2)
            MV = [sb(f"MV{n}", [35, TILE], BF16, s2) for n in range(2)]
            PC = [sb(f"PC{n}", [KC, PAIRS * TILE], F32, s2) for n in range(2)]
            rd = sb("rd", [TILE, 2, PAIRS, 2], F32, s2)
            rg = sb("rg", [TILE, 2, PAIRS, 2], F32, s2)
            oc = [sb(f"oc{n}", [TILE, 260], F32, s2) for n in range(2)]
            ot = [sb(f"ot{n}", [128, 3 * TILE], F32, s2) for n in range(2)]
        with ExitStack() as s3:
            K = [sb(f"K{m}", [128, HEADS, KBAND], BF16, s3) for m in range(IMAGES)]
            Q = [sb(f"Q{m}", [128, HEADS, BAND], BF16, s3) for m in range(IMAGES)]
            Vw = [sb(f"Vw{n}", [KEYS, 2, PAIRS * VCOLS], F32, s3) for n in range(4)]
            P = [sb(f"P{n}", [KEYS, HEADS * SUB], F32, s3) for n in range(4)]
            wn = [sb(f"wn{n}", [TILE, HEADS], F32, s3) for n in range(2)]
            wnb = [sb(f"wnb{n}", [TILE, 2, HEADS], BF16, s3) for n in range(2)]
            nT = [sb(f"nT{n}", [2 * HEADS, TILE], BF16, s3) for n in range(2)]
            gm = sb("gm", [TILE, 2], F32, s3)
            wr = sb("wr", [TILE, PAIRS], F32, s3)
            wr2 = sb("wr2", [TILE, PAIRS, 2], F32, s3)
            tw = [sb(f"tw{n}", [TILE, C], F32, s3) for n in range(4)]
            ow = [sb(f"ow{n}", [128, BAND], F32, s3) for n in range(2)]
            stage = sb("stage", [128, KROWS * PSIDE + BAND], F32, s3)
        att.close()
        with ExitStack() as s4:
            T = [sb(f"T{n}", [128, PIX], F32, s4) for n in range(2)]
            AC = [sb(f"AC{n}", [128, PIX], F32, s4) for n in range(2)]
            U = [sb(f"U{n}", [128, PIX], F32, s4) for n in range(2)]
            zc = [sb(f"zc{n}", [128, BAND], F32, s4) for n in range(2)]
            zq = [sb(f"zq{n}", [128, BAND], F32, s4) for n in range(2)]
            sd = [sb(f"sd{n}", [128, BAND], F32, s4) for n in range(2)]
            zo = [sb(f"zo{n}", [128, BAND], F32, s4) for n in range(2)]

        def w(name, n=C, off=0):
            return W[:, WCOL[name] + off:WCOL[name] + off + n]

        def v(col, n=1, p=128):
            return vec[0:p, col:col + n]

        LOADS = 6
        block = ctx.enter_context(nc.Block())

        pjobs = [(m, "k", h * KBAND // 2, KBAND // 2) for m in range(IMAGES) for h in range(2 * BANDS)]
        pjobs += [(m, "q", b * BAND, BAND) for m in range(IMAGES) for b in range(BANDS)]
        NPJ = len(pjobs)
        vjobs = [(m, g, min(4, 31 - 4 * g)) for m in range(IMAGES) for g in range(8)]
        NVJ = len(vjobs)
        gjobs = [(m, b) for m in range(IMAGES) for b in range(BANDS)]
        NGJ = len(gjobs)

        CT = IMAGES * BANDS * TILES
        CB = IMAGES * TILES
        CLAG = 5

        def each_tile(i, last, emit):
            for k in range(CLAG if last else CB):
                emit(i, k)

        def at(i, k, lag, per, total):
            turn, place = divmod(k - lag, per)
            if isinstance(i, int):
                n = per * i + k - lag
                if n < 0 or n >= total:
                    return None
            return per * i + (k - lag), i + turn, place

        def run_loop(eng, body, turns, tail):
            body(0, False)
            with eng.Fori(1, turns) as i:
                body(i, False)
            if tail:
                body(turns, True)

        STEPJ = 2 * SUBS
        WB = IMAGES * STEPJ
        WT = WB * BANDS
        NTAIL = 8
        LEAD = 8

        def pa_jobs(k):
            jobs = [("A", k + LEAD)]
            if k % 4 == 1:
                jobs.append(("S", (k + 3) // 4))
            if k % 4 == 3:
                jobs.append(("T", (k - 7) // 4))
            if k % 16 == 5:
                jobs.append(("Y", (k - 21) // 16))
            return jobs

        PER = {"A": WB, "S": WB // 4, "T": WB // 4, "Y": WB // 16}
        TOT = {"A": WT, "S": WT // 4, "T": WT // 4, "Y": WT // 16}

        def pa_real(kind, i, n):
            a = PER[kind] * i + n
            return 0 <= a < TOT[kind]

        PAPER = sum(len(pa_jobs(k)) for k in range(WB))
        assert PAPER % 2 == 0
        PRE = LEAD

        pa_table, used, local = {}, {0: 0, 1: 0}, -sum(len(pa_jobs(k)) for k in range(-PRE, 0))
        done = 0
        for q in range(-PRE, WB * (BANDS + 1)):
            for kind, n in pa_jobs(q):
                if pa_real(kind, 0, n):
                    pa_table[q, kind] = (local % 2, done, used[local % 2])
                    done += 1
                    used[local % 2] = done
                local += 1

        def pa_list(i, ks):
            res = []
            for k in ks:
                for kind, n in pa_jobs(k):
                    if not isinstance(i, int):
                        slot, before, last_use = pa_table[WB + k, kind]
                        assert last_use == before - 1
                        res.append((k, kind, n, slot, PAPER * i + (before - PAPER), PAPER * i + (last_use - PAPER)))
                    elif (i * WB + k, kind) in pa_table:
                        res.append((k, kind, n, *pa_table[i * WB + k, kind]))
            return res

        def turn_of(i, n, per):
            d, r = divmod(n, per)
            return i + d, r

        def window_places(i, kind):
            if kind == "head":
                return range(-PRE, 0)
            return range(0, NTAIL + 16) if kind == "tail" else range(0, WB)

        def run_window(eng, body):
            body(0, range(-PRE, WB))
            with eng.Fori(1, BANDS - 1) as i:
                body(i, range(0, WB))
            body(BANDS - 1, range(0, WB))
            body(BANDS, range(0, 24))

        def wjob(i, n, per=WB, total=WT):
            if isinstance(i, int) and not 0 <= per * i + n < total:
                return None
            t, r = turn_of(i, n, per)
            return per * i + n, t, r

        def kband(i, img):
            return (i, img)

        @block.sync
        def _(sp):
            sp.dma_start(X[:, 0, :], x[0]).then_inc(sem("x0_loaded"), 16)
            sp.dma_start(vec[:], vecs).then_inc(sem("loaded"), 16)
            sp.dma_start(W[:], wts).then_inc(sem("loaded"), 16)
            sp.dma_start(X[:, 1, :], x[1]).then_inc(sem("x1_loaded"), 16)
            sp.dma_start(row[:], rows).then_inc(sem("loaded"), 16)
            sp.dma_start(pjrow[:], pjb).then_inc(sem("loaded"), 16)
            sp.dma_start(cst[:], c32).then_inc(sem("loaded"), 16)

            for n, (m, which, at0, cols) in enumerate(pjobs):
                sp.wait_ge(sem("parts_ready"), n + 1)
                dst = (k_dram if which == "k" else q_dram)[:, :, m, at0:at0 + cols]
                sp.dma_start(dst.rearrange("t c n -> c t n"), pk[n % 2][:, :, 0:cols]).then_inc(sem(f"parts_stored{n % 2}"), 16)
            for n, (m, g, k) in enumerate(vjobs):
                sp.wait_ge(sem("v_ready"), n + 1)
                dst = v_flat[m, 496 * g:496 * g + 124 * k, :].rearrange("(t p) v -> p t v", p=124)
                sp.dma_start(dst, vst[n % 2][:, 0:k, :]).then_inc(sem(f"v_stored{n % 2}"), 16)

            sp.wait_ge(sem("c_added"), CT)
            for n in range(2):
                sp.wait_ge(sem(f"parts_stored{n}"), 16 * (NPJ // 2))
                sp.wait_ge(sem(f"v_stored{n}"), 16 * (NVJ // 2))
            sp.dma_start(stage[96:128, :], cmask).then_inc(sem("stage_loaded"), 16)

            def load_band(i, img):
                for t, (a, b) in enumerate(TERMS):
                    qsrc = q_dram[a, :, img, ds(i * BAND, BAND)].rearrange("(h d) n -> d h n", h=HEADS)
                    sp.dma_start(Q[img][DH * t:DH * (t + 1), :, :], qsrc).then_inc(sem(f"band_loaded{img}"), 16)
                    ksrc = k_dram[b, :, img, ds(i * KBAND, KBAND)].rearrange("(h d) n -> d h n", h=HEADS)
                    sp.dma_start(K[img][DH * t:DH * (t + 1), :, :], ksrc).then_inc(sem(f"band_loaded{img}"), 16)

            def body(i, ks):
                for k in ks:
                    if k % 16 == 0:
                        nj = wjob(i, k // 16 + 1, 2, 2 * BANDS)
                        if nj is not None:
                            prev = wjob(i, k - 1)
                            if prev is not None:
                                sp.wait_ge(sem("w_scores"), prev[0] + 1)
                            load_band(nj[1], nj[2])
                    if k % 2 == 0:
                        s = wjob(i, k // 2 + 3, WB // 2, WT // 2)
                        if s is not None:
                            num, t, r = s
                            img, c = divmod(r, SUBS)
                            old = wjob(i, k // 2 - 1, WB // 2, WT // 2)
                            if old is not None:
                                sp.wait_ge(sem("w_products"), 2 * old[0] + 2)
                            for h in range(2):
                                c0 = SUBC * c + HCOLS[0] * h
                                src = v_dram[img, ds(t * BLOCK, KROWS), c0:c0 + HCOLS[h], :].rearrange("r c v -> c r v")
                                sp.dma_start(Vw[r % 4][0:HKEYS[h], h, :], src).then_inc(sem(f"w_values{r % 4}"), 16)
                    if k % 4 == 2:
                        s = wjob(i, (k + 2) // 4, WB // 4, WT // 4)
                        if s is not None:
                            num, t, r = s
                            img, c = divmod(r, TILES)
                            sp.wait_ge(sem("w_shiftT"), num + 1)
                            dst = Q[img][SHIFT0:SHIFT0 + 2, :, c * TILE:(c + 1) * TILE]
                            sp.dma_start(dst, nT[r % 2][:]).then_inc(sem(f"w_shift{r % 2}"), 16)

            load_band(0, 0)
            sp.wait_ge(sem("stacks"), 4)
            run_window(sp, body)

            for n in range(IMAGES * BANDS):
                m, b = divmod(n, BANDS)
                sp.wait_ge(sem("z_ready"), n + 1)
                sp.dma_start(out[m, :, b * BAND:(b + 1) * BAND], zo[n % 2][:]).then_inc(sem(f"z_stored{n % 2}"), 16)
            for n in range(2):
                sp.wait_ge(sem(f"z_stored{n}"), 16 * (IMAGES * BANDS // 2))

        @block.gpsimd
        def _(pool):
            g = nc.gpsimd
            g.memset(ones[:], 1.0).then_inc(sem("consts"), 1)
            g.memset(meanw[:], 1.0 / C).then_inc(sem("consts"), 1)
            g.memset(epsc[:], EPS).then_inc(sem("consts"), 1)
            for n in range(2):
                g.memset(vst[n][:], 1.0).then_inc(sem("consts"), 1)
            for m in range(IMAGES):
                pool.wait_ge(sem("conv_done"), m + 1)
                mid = slice(PAD, PAD + SIDE)
                g.tensor_copy(FP[:, m, mid, 0:PAD], bc(FP[:, m, mid, PAD:PAD + 1], [128, SIDE, PAD])).then_inc(sem("sides"), 1)
                g.tensor_copy(FP[:, m, mid, PAD + SIDE:PSIDE], bc(FP[:, m, mid, PAD + SIDE - 1:PAD + SIDE], [128, SIDE, PAD])).then_inc(sem("sides"), 1)
                pool.wait_ge(sem("sides"), 2 * m + 2)
                g.tensor_copy(FP[:, m, 0:PAD, :], bc(FP[:, m, PAD:PAD + 1, :], [128, PAD, PSIDE])).then_inc(sem("padded"), 1)
                g.tensor_copy(FP[:, m, PAD + SIDE:PSIDE, :], bc(FP[:, m, PAD + SIDE - 1:PAD + SIDE, :], [128, PAD, PSIDE])).then_inc(sem("padded"), 1)
            pool.wait_ge(sem("setup_done"), 2)
            for n in range(2):
                pool.wait_ge(sem(f"parts_stored{n}"), 16 * (NPJ // 2))
                pool.wait_ge(sem(f"v_stored{n}"), 16 * (NVJ // 2))
            g.memset(cst35[:], 0.0).then_inc(sem("c_consts0"), 1)
            pool.wait_ge(sem("c_consts0"), 1)
            g.memset(cst35[32:35, :], 1.0).then_inc(sem("c_consts"), 1)
            for n in range(2):
                pool.wait_ge(sem("c_consts"), n + 1)
                g.memset(MV[n][32:35, :], 1.0).then_inc(sem("c_consts"), 1)


        @block.tensor
        def _(pe):
            mm = nc.tensor.matmul
            tr = nc.tensor.transpose
            ident = cst[:, CI:CI + 128]

            def bank(b, p=128, n=512, at0=0):
                return PS[0:p, b, at0:at0 + n]

            pe.wait_ge(sem("loaded"), 16 * 5)
            pe.wait_ge(sem("consts"), 5)
            pe.wait_ge(sem("blk_ready"), 1)
            blk2 = blk[:].rearrange("p i n -> p (i n)")
            mm(bank(0, 64, 98), w("s1", 64), blk2, start=True, stop=True).then_inc(sem("p_hid"), 1)
            for m in range(IMAGES):
                last = tr(bank(1, NBLK, C, C * m), blk[:, m, :], ident)
            last.then_inc(sem("p_blkT"), 1)
            pe.wait_ge(sem("hid"), 1)
            mm(bank(0, 1, 98, 128), v(V_S2, 1, 64), hs[:], start=True, stop=True).then_inc(sem("p_score"), 1)
            pe.wait_ge(sem("topf"), 1)
            mm(bank(0, NBLK, 16, 256), ones[0:1, 0:NBLK], topf[:].rearrange("p i n -> p (i n)"), start=True, stop=True).then_inc(sem("p_idx"), 1)
            pe.wait_ge(sem("onehot"), 1)
            pe.wait_ge(sem("blkT"), 1)
            for m in range(IMAGES):
                last = mm(bank(2, C, TOPK, 8 * m), blkT[:, m, :], onehot[:, m, 0:TOPK], start=True, stop=True)
            last.then_inc(sem("p_ksel"), 1)
            pe.wait_ge(sem("rows_ready"), 2)
            for m in range(IMAGES):
                if m:
                    pe.wait_ge(sem("attn_ops"), 4 * m)
                mm(bank(0, C, NBLK), w("wk0"), R[:, m, 0:NBLK], start=True, stop=True)
                mm(bank(0, C, TOPK, 64), w("wk1"), R[:, m, 2 * NBLK:2 * NBLK + TOPK], start=True, stop=True).then_inc(sem("p_keys"), 1)
                for n, name in enumerate(("wv0", "wv1")):
                    mm(bank(1, KC, C, C * n), R[:, m, :], w(name), start=True, stop=False)
                    last = mm(bank(1, KC, C, C * n), ones[0:1, 0:KC], row[0:1, C * n:C * (n + 1)], start=False, stop=True)
                last.then_inc(sem("p_vals"), 1)
                pe.wait_ge(sem("km_ready"), m + 1)
                a4 = bank(2, C, SC).rearrange("p (j k) -> p j k", j=PAIRS)
                b4 = bank(3, 35, SC).rearrange("p (j k) -> p j k", j=PAIRS)
                mm(a4[:, :, 0:2 * NBLK], w("wq0"), KM[:, :, 0:2 * NBLK], start=True, stop=True)
                mm(a4[:, :, 2 * NBLK:KC], w("wq1"), KM[:, :, 2 * NBLK:KC], start=True, stop=True)
                mm(b4[:, :, 0:2 * NBLK], bq35[:, 0, :], KM[:, :, 0:2 * NBLK], start=True, stop=True)
                mm(b4[:, :, 2 * NBLK:KC], bq35[:, 1, :], KM[:, :, 2 * NBLK:KC], start=True, stop=True).then_inc(sem("p_fold"), 1)
            mm(bank(4, 124, C), ones[0:1, 0:124], row[0:1, 2 * C:3 * C], start=True, stop=True)
            mm(bank(4, TILE, 3, 256), n1rep[:], v(V_GW, 3), start=True, stop=False)
            mm(bank(4, TILE, 3, 256), ones[0:1, 0:TILE], row[0:1, R_GB:R_GB + 3], start=False, stop=True).then_inc(sem("p_rows"), 1)

            pe.wait_ge(sem("padded"), 4)
            pe.wait_ge(sem("tile_order"), IMAGES * BANDS)
            for n, (m, which, at0, cols) in enumerate(pjobs):
                if n >= 2:
                    pe.wait_ge(sem("proj_read"), n - 1)
                if which == "k":
                    b, h = divmod(at0 // (KBAND // 2), 2)
                    src = FP[:, m, BLOCK * b:BLOCK * b + KROWS, PSIDE // 2 * h:PSIDE // 2 * (h + 1)].rearrange("p r c -> p c r")
                    dst = bank(5 + n % 2, C, cols).rearrange("p (c r) -> p c r", r=KROWS)
                else:
                    src, dst = xt(m)[:, at0:at0 + cols], bank(5 + n % 2, C, cols)
                mm(dst, w("wk2" if which == "k" else "wq2"), src, start=True, stop=True).then_inc(sem("proj"), 1)
            for n, (m, g, k) in enumerate(vjobs):
                if n >= 1:
                    pe.wait_ge(sem("v_ready"), n)
                for t in range(k):
                    pos = FP[:, m, 8 * g + 2 * t:8 * g + 2 * t + 2, :].rearrange("p r c -> p (r c)")
                    last = mm(bank(7, 124, C, C * t), pos, w("wv2"), start=True, stop=True)
                last.then_inc(sem("vals"), 1)
            for n in range(NGJ + 1):
                if n < NGJ:
                    m, b = gjobs[n]
                    if n >= 1:
                        pe.wait_ge(sem("g_centred"), n)
                    mm(bank(0, C, BAND), meanw[:], xt(m)[:, b * BAND:(b + 1) * BAND], start=True, stop=True).then_inc(sem("g_mean"), 1)
                if n >= 1:
                    q = n - 1
                    pe.wait_ge(sem("g_square"), q + 1)
                    pe.wait_ge(sem("g_centred"), q + 1)
                    if q >= 1:
                        pe.wait_ge(sem("g_logits_read"), q)
                    mm(bank(1, 4, BAND), gl[:, 0, :], xc[q % 2][:], start=True, stop=False)
                    mm(bank(1, 4, BAND), gl[:, 1, :], sq[q % 2][:], start=False, stop=True).then_inc(sem("g_logits"), 1)
                    pe.wait_ge(sem("g_logits_read"), q + 1)
                    if q >= 1:
                        pe.wait_ge(sem("g_stored"), q)
                    for s in range(SUBS):
                        tr(bank(2, TILE, 4, 4 * s), ls2[q % 2][:, s, :, :].rearrange("p a n -> p (a n)"), ident[0:4, 0:4])
                    for s in range(TILES):
                        last = tr(bank(2, TILE, 4, 32 + 4 * s), ls[q % 2][:, s * TILE:(s + 1) * TILE], ident[0:4, 0:4])
                    last.then_inc(sem("g_byquery"), 1)

            pe.wait_ge(sem("split"), 2)
            pe.wait_ge(sem("c_consts"), 3)
            pe.wait_ge(sem("gates"), 1)

            def c_body(i, tail):
                for k in range(CLAG if tail else CB):
                    a = at(i, k, 0, CB, CT)
                    if a:
                        num, t, r = a
                        img, c = divmod(r, TILES)
                        if not (isinstance(num, int) and num < 2):
                            pe.wait_ge(sem("c_maxed"), num - 1)
                        xs = ds(t * BAND + c * TILE, TILE)
                        s = bank(r % 2, TILE, SC)
                        mm(s, XH[:, img, xs], Ah[img][:], start=True, stop=False)
                        mm(s, XL[:, img, xs], Ah[img][:], start=False, stop=False)
                        mm(s, XH[:, img, xs], Al[img][:], start=False, stop=False)
                        mm(s, cst35[:], ES[img][:], start=False, stop=True).then_inc(sem("c_sa"), 1)
                    a = at(i, k, 1, CB, CT)
                    if a:
                        num, t, r = a
                        pe.wait_ge(sem("c_shift"), num + 1)
                        if not (isinstance(num, int) and num < 1):
                            pe.wait_ge(sem("c_shift_used"), num)
                        tr(PS[0:32, 2, 0:TILE // 2].bitcast(BF16), nmb[r % 2][:], identb[:]).then_inc(sem("c_shiftT"), 1)
                    a = at(i, k, 2, CB, CT)
                    if a:
                        num, t, r = a
                        img, c = divmod(r, TILES)
                        pe.wait_ge(sem("c_shift_used"), num + 1)
                        if not (isinstance(num, int) and num < 2):
                            pe.wait_ge(sem("c_exp"), num - 1)
                        for j in range(PAIRS):
                            s = bank(3 + r % 2, KC, TILE, TILE * j)
                            mm(s, Af[img][:, KC * j:KC * (j + 1)], XT[:, img, ds(t * BAND + c * TILE, TILE)], start=True, stop=False)
                            last = mm(s, ES[img][:, KC * j:KC * (j + 1)], MV[r % 2][:], start=False, stop=True)
                        last.then_inc(sem("c_sb"), 1)
                    a = at(i, k, 3, CB, CT)
                    if a:
                        num, t, r = a
                        img = r // TILES
                        pe.wait_ge(sem("c_exp"), num + 1)
                        if not (isinstance(num, int) and num < 1):
                            pe.wait_ge(sem("c_norm"), num)
                        for j in range(PAIRS):
                            last = mm(bank(5, TILE, 68, 68 * j), PC[r % 2][:, TILE * j:TILE * (j + 1)], VB[img][:, j, :], start=True, stop=True)
                        last.then_inc(sem("c_pv"), 1)
                    a = at(i, k, 4, CB, CT)
                    if a:
                        num, t, r = a
                        pe.wait_ge(sem("c_norm"), num + 1)
                        if not (isinstance(num, int) and num < 1):
                            pe.wait_ge(sem("c_ot"), 2 * num)
                        for ty in range(2):
                            tr(bank(6, C, TILE, TILE * ty), oc[r % 2][:, C * ty:C * (ty + 1)], ident[0:TILE, 0:TILE])
                        tr(bank(6, 3, TILE, 2 * TILE), oc[r % 2][:, 256:259], ident[0:TILE, 0:TILE]).then_inc(sem("c_tr"), 1)
                    a = at(i, k, 5, CB, CT)
                    if a:
                        num, t, r = a
                        pe.wait_ge(sem("c_ot"), 2 * num + 2)
                        if not (isinstance(num, int) and num < 1):
                            pe.wait_ge(sem("c_added"), num)
                        y = bank(7, C, TILE)
                        mm(y, w("pj0"), ot[r % 2][:, 0:TILE], start=True, stop=False)
                        mm(y, w("pj1"), ot[r % 2][:, TILE:2 * TILE], start=False, stop=False)
                        mm(y, pjrow[:], ot[r % 2][0:3, 2 * TILE:3 * TILE], start=False, stop=True).then_inc(sem("c_y"), 1)

            run_loop(pe, c_body, BANDS, True)

            pe.wait_ge(sem("c_added"), CT)
            pe.wait_ge(sem("stacks"), 4)

            def pslot(s, p=128):
                return PS[0:p, 2 * s:2 * s + 2, :]

            def w_body(i, ks):
                lst = pa_list(i, ks)
                for k in ks:
                    mine = [e for e in lst if e[0] == k]

                    def slot_free(last_use):
                        if not (isinstance(last_use, int) and last_use < 1):
                            pe.wait_ge(sem("w_slot_read"), last_use)

                    for _, kind, n, slot, before, last_use in mine:
                        if kind == "A":
                            num, t, r = wjob(i, n)
                            img, q = divmod(r, STEPJ)
                            c, hp = divmod(q, 4)
                            if q == 0:
                                pe.wait_ge(sem(f"band_loaded{img}"), (t + 1) * (16 * 2 * len(TERMS)))
                            slot_free(last_use)
                            for e in range(2):
                                h = 2 * hp + e
                                last = mm(pslot(slot, TILE)[:, e, 0:KROWS * TCOLS], Q[img][0:SHIFT0, h, c * TILE:(c + 1) * TILE],
                                          K[img][0:SHIFT0, h, 14 * c * KROWS:(14 * c + TCOLS) * KROWS], start=True, stop=True)
                            last.then_inc(sem("w_slot"), 1)
                        if kind == "S":
                            num, t, r = wjob(i, n, WB // 4, WT // 4)
                            pe.wait_ge(sem("w_split"), num + 1)
                            slot_free(last_use)
                            dst = PS[0:2 * HEADS, 2 * slot, 0:TILE // 2].bitcast(BF16)
                            tr(dst, wnb[r % 2][:].rearrange("p a h -> p (a h)"), identb[:]).then_inc(sem("w_slot"), 1)
                    jb = wjob(i, k)
                    if jb:
                        num, t, r = jb
                        img, q = divmod(r, STEPJ)
                        c, h2 = divmod(q, 2)
                        if q % 4 == 0:
                            tl = (num // 4) if isinstance(num, int) else (t * (WB // 4) + r // 4)
                            par = (r // 4) % 2
                            pe.wait_ge(sem(f"w_shift{par}"), (t * (WB // 8) + (r // 8) + 1) * 16)
                        if not (isinstance(num, int) and num < 2):
                            pe.wait_ge(sem("w_exp"), num - 1)
                        for h in range(HEADS):
                            k0_ = (SUBC * c + HCOLS[0] * h2) * KROWS
                            last = mm(PS[0:HKEYS[h2], 4 + r % 2, h * SUB:(h + 1) * SUB],
                                      K[img][:, h, k0_:k0_ + HKEYS[h2]],
                                      Q[img][:, h, c * SUB:(c + 1) * SUB], start=True, stop=True)
                        last.then_inc(sem("w_scores"), 1)
                    jb = wjob(i, k - 2)
                    if jb:
                        num, t, r = jb
                        s = r // 2
                        pe.wait_ge(sem("w_exp"), num + 1)
                        if r % 2 == 0:
                            pe.wait_ge(sem(f"w_values{s % 4}"), (t * (WB // 8) + s // 4 + 1) * 32)
                            if not (isinstance(num, int) and num < 4):
                                pe.wait_ge(sem("w_norm"), t * (WB // 2) + s - 1)
                        for j in range(PAIRS):
                            last = mm(PS[0:TILE, 6 + s % 2, VCOLS * j:VCOLS * (j + 1)], P[r % 4][0:HKEYS[r % 2], TILE * j:TILE * (j + 1)],
                                      Vw[s % 4][0:HKEYS[r % 2], r % 2, VCOLS * j:VCOLS * (j + 1)], start=(r % 2 == 0 and j == 0),
                                      stop=(r % 2 == 1 and j == PAIRS - 1), skip_group_check=True)
                        last.then_inc(sem("w_products"), 1)
                    for _, kind, n, slot, before, last_use in mine:
                        if kind == "T":
                            num, t, r = wjob(i, n, WB // 4, WT // 4)
                            pe.wait_ge(sem("w_norm"), 2 * num + 2)
                            slot_free(last_use)
                            for e in range(2):
                                last = mm(PS[:, 2 * slot, e * SUB:(e + 1) * SUB], tw[(2 * r + e) % 4][:], cst[0:TILE, CSEL:CSEL + SUB], start=True, stop=True)
                            last.then_inc(sem("w_slot"), 1)
                        if kind == "Y":
                            num, t, r = wjob(i, n, 2, 2 * BANDS)
                            pe.wait_ge(sem("w_ot"), 4 * num + 4)
                            slot_free(last_use)
                            mm(PS[:, 2 * slot, 0:BAND], w("pj2"), ow[r % 2][:], start=True, stop=True).then_inc(sem("w_slot"), 1)

            run_window(pe, w_body)

            job = 0
            pe.wait_ge(sem("w_y"), 2 * BANDS)
            for m in range(IMAGES):
                for pair in range(2):
                    for half in range(2):
                        q = 4 * m + 2 * pair + half
                        grp = pair + 2 * half
                        for b in range(BANDS):
                            if job >= 2:
                                pe.wait_ge(sem("t_read"), job - 1)
                            mm(bank(job % 2, C, BAND), w("pin", C, C * grp), X[:, m, b * BAND:(b + 1) * BAND], start=True, stop=True).then_inc(sem("t_proj"), 1)
                            job += 1
                pe.wait_ge(sem("hidden"), 2 * m + 2)
                for b in range(BANDS):
                    n = m * BANDS + b
                    if n >= 2:
                        pe.wait_ge(sem("z_sum"), n - 1)
                    for g2 in range(2):
                        last = mm(bank(2 + n % 2, C, BAND), w("pout", C, C * g2), U[g2][:, b * BAND:(b + 1) * BAND], start=(g2 == 0), stop=(g2 == 1))
                    last.then_inc(sem("z_proj"), 1)
            for n in range(IMAGES * BANDS + 1):
                if n < IMAGES * BANDS:
                    m, b = divmod(n, BANDS)
                    pe.wait_ge(sem("z_sum"), n + 1)
                    if n >= 2:
                        pe.wait_ge(sem("z_centred"), n - 1)
                    mm(bank(4 + n % 2, C, BAND), meanw[:], X[:, m, b * BAND:(b + 1) * BAND], start=True, stop=True).then_inc(sem("z_mean"), 1)
                if n >= 1:
                    q = n - 1
                    pe.wait_ge(sem("z_square"), q + 1)
                    if q >= 2:
                        pe.wait_ge(sem("z_std"), q - 1)
                    mm(bank(6 + q % 2, C, BAND), meanw[:], zq[q % 2][:], start=True, stop=True).then_inc(sem("z_var"), 1)

        @block.scalar
        def _(act):
            a = nc.scalar.activation
            act.wait_ge(sem("loaded"), 16 * 5)
            act.wait_ge(sem("p_hid"), 1)
            a(hs[:], PS[0:64, 0, 0:98], ACT.Gelu, bias=v(V_S1B, 1, 64)).then_inc(sem("hid"), 1)
            a(identb[:], cst[0:TILE, CI:CI + TILE], ACT.Copy).then_inc(sem("identb"), 1)
            for m in range(IMAGES):
                act.wait_ge(sem("conv_done"), m + 1)
                for b in range(BANDS):
                    src = FP[:, m, PAD + BLOCK * b:PAD + BLOCK * (b + 1), PAD:PAD + SIDE].rearrange("p r (s c) -> p s r c", c=SUBC)
                    dst = XT[:, m, b * BAND:(b + 1) * BAND].rearrange("p (s r c) -> p s r c", s=SUBS, c=SUBC)
                    a(dst, src, ACT.Copy).then_inc(sem("tile_order"), 1)
            for m in range(IMAGES):
                act.wait_ge(sem("tile_order"), BANDS * (m + 1))
                a(XH[:, m, :], xt(m), ACT.Copy).then_inc(sem("high"), 1)
            for n, (m, which, at0, cols) in enumerate(pjobs):
                act.wait_ge(sem("proj"), n + 1)
                if n >= 2:
                    act.wait_ge(sem("parts_ready"), n - 1)
                    act.wait_ge(sem(f"parts_stored{n % 2}"), 16 * (n // 2))
                ps = PS[:, 5 + n % 2, 0:cols]
                if n == 0:
                    act.wait_ge(sem("c1"), 3)
                bias = v(V_BK + 2) if which == "k" else c1[:, 2:3]
                sc = 1.0 if which == "k" else SCALE
                a(pf[n % 2][:, 0:cols], ps, ACT.Identity, bias=bias, scale=sc).then_inc(sem("proj_full"), 1)
                a(pk[n % 2][:, 0, 0:cols], ps, ACT.Identity, bias=bias, scale=sc).then_inc(sem("proj_read"), 1)
            for n in range(NGJ):
                act.wait_ge(sem("g_centred"), n + 1)
                if n >= 2:
                    act.wait_ge(sem("g_logits"), n - 1)
                a(sq[n % 2][:], xc[n % 2][:], ACT.Square).then_inc(sem("g_square"), 1)
            act.wait_ge(sem("g_stored"), NGJ)
            g4 = G[:].rearrange("p i b s k -> p (i b s) k")
            a(gst[:], g4[:, :, 3], ACT.Sqrt, bias=epsc[0:TILE, :]).then_inc(sem("g_std"), 1)
            act.wait_ge(sem("g_shifted"), 1)
            a(g4[:, :, 0:3], g4[:, :, 0:3], ACT.Exp).then_inc(sem("g_exp"), 1)

            def c_body(i, tail):
                for k in range(CLAG if tail else CB):
                    s = at(i, k, 2, CB, CT)
                    if s:
                        num, t, r = s
                        act.wait_ge(sem("c_sb"), num + 1)
                        if not (isinstance(num, int) and num < 2):
                            act.wait_ge(sem("c_pv"), num - 1)
                        a(PC[r % 2][:], PS[0:KC, 3 + r % 2, 0:PAIRS * TILE], ACT.Exp).then_inc(sem("c_exp"), 1)
                    s = at(i, k, 4, CB, CT)
                    if s:
                        num, t, r = s
                        act.wait_ge(sem("c_tr"), num + 1)
                        if not (isinstance(num, int) and num < 2):
                            act.wait_ge(sem("c_y"), num - 1)
                        a(ot[r % 2][:, 0:2 * TILE], PS[:, 6, 0:2 * TILE], ACT.Copy).then_inc(sem("c_ot"), 1)
                        a(ot[r % 2][0:3, 2 * TILE:3 * TILE], PS[0:3, 6, 2 * TILE:3 * TILE], ACT.Copy).then_inc(sem("c_ot"), 1)

            act.wait_ge(sem("setup_done"), 2)
            run_loop(act, c_body, BANDS, True)

            act.wait_ge(sem("c_added"), CT)
            act.wait_ge(sem("stage_loaded"), 16)
            NK = KROWS * PSIDE
            for m in range(IMAGES):
                kd = K[m][MASK0:128, :, :]
                a(kd, bc(stage[MASK0:128, 0:NK].unsqueeze(1), [32, HEADS, NK]), ACT.Copy).then_inc(sem("stacks"), 1)
                a(Q[m][MASK0:128, :, :], bc(stage[MASK0:128, NK:NK + BAND].unsqueeze(1), [32, HEADS, BAND]), ACT.Copy).then_inc(sem("stacks"), 1)

            def w_body(i, ks):
                for k in ks:
                    jb = wjob(i, k)
                    if jb:
                        num, t, r = jb
                        act.wait_ge(sem("w_scores"), num + 1)
                        if not (isinstance(num, int) and num < 4):
                            act.wait_ge(sem("w_products"), num - 3)
                        kn = HKEYS[r % 2]
                        a(P[r % 4][0:kn, :], PS[0:kn, 4 + r % 2, 0:HEADS * SUB], ACT.Exp).then_inc(sem("w_exp"), 1)

            run_window(act, w_body)

            job = 0
            act.wait_ge(sem("w_y"), 2 * BANDS)
            for m in range(IMAGES):
                for pair in range(2):
                    for half in range(2):
                        q = 4 * m + 2 * pair + half
                        grp = pair + 2 * half
                        if q >= 2:
                            act.wait_ge(sem("conv2"), q - 1)
                            act.wait_ge(sem("hidden"), q // 2 if half == 0 else (q - 1) // 2)
                        for b in range(BANDS):
                            act.wait_ge(sem("t_proj"), job + 1)
                            cols = slice(b * BAND, (b + 1) * BAND)
                            a(T[q % 2][:, cols], PS[:, job % 2, 0:BAND], ACT.Copy).then_inc(sem("t_full"), 1)
                            a(AC[q % 2][:, cols], PS[:, job % 2, 0:BAND], ACT.Copy, scale=v(V_DW + 9 * grp + 4)).then_inc(sem("t_read"), 1)
                            job += 1
                        if half == 1:
                            act.wait_ge(sem("conv2"), q)
                            a(AC[0][:], AC[0][:], ACT.Gelu).then_inc(sem("gelu"), 1)
            for n in range(IMAGES * BANDS + 1):
                if n < IMAGES * BANDS:
                    act.wait_ge(sem("z_centred"), n + 1)
                    if n >= 2:
                        act.wait_ge(sem("z_var"), n - 1)
                    a(zq[n % 2][:], zc[n % 2][:], ACT.Square).then_inc(sem("z_square"), 1)
                if n >= 1:
                    q = n - 1
                    act.wait_ge(sem("z_var"), q + 1)
                    if q >= 2:
                        act.wait_ge(sem("z_rstd"), q - 1)
                    a(sd[q % 2][:], PS[:, 6 + q % 2, 0:BAND], ACT.Sqrt, bias=epsc[:]).then_inc(sem("z_std"), 1)

        @block.vector
        def _(dve):
            ve = nc.vector
            chain = [0]

            def link(ins):
                chain[0] += 1
                ins.then_inc(sem("v_chain"), 1)
                dve.wait_ge(sem("v_chain"), chain[0])

            dve.wait_ge(sem("loaded"), 16 * 5)
            ve.tensor_scalar(c1[:, 0:1], v(V_POSW + 4), 1.0, None, ALU.add).then_inc(sem("c1"), 1)
            ve.memset(gl[:], 0.0).then_inc(sem("c1"), 1)
            ve.tensor_scalar(c1[:, 2:3], v(V_BQ + 2), SCALE, None, ALU.mult).then_inc(sem("c1"), 1)
            dve.wait_ge(sem("c1"), 3)

            def conv(src, dst, wcol, first):
                for t in SIDE_TAPS:
                    dy, dx = TAPS[t]
                    ro, rn = max(0, -dy), SIDE - abs(dy)
                    co, cn = max(0, -dx), SIDE - abs(dx)
                    o = dst(ro, rn, co, cn)
                    link(ve.scalar_tensor_tensor(out=o, in0=src(ro + dy, rn, co + dx, cn), scalar=v(wcol + t), in1=o, op0=ALU.mult, op1=ALU.add))

            for m in range(IMAGES):
                dve.wait_ge(sem(f"x{m}_loaded"), 16)
                xi = X[:, m, :].rearrange("p (r c) -> p r c", c=SIDE)
                inner = FP[:, m, PAD:PAD + SIDE, PAD:PAD + SIDE]
                link(ve.tensor_scalar(inner, xi, c1[:, 0:1], v(V_POSB), ALU.mult, ALU.add))
                conv(lambda r, rn, c, cn: xi[:, r:r + rn, c:c + cn], lambda r, rn, c, cn: inner[:, r:r + rn, c:c + cn], V_POSW, m)
                ve.tensor_reduce(bs1[:, m, :, :], inner.rearrange("p r (b c) -> p r b c", c=BLOCK), AX.X, ALU.add).then_inc(sem("conv_done"), 1)
            for m in range(IMAGES):
                dve.wait_ge(sem("conv_done"), m + 1)
                src = bs1[:, m, :, :].rearrange("p (y r) b -> p y b r", r=BLOCK)
                link(ve.tensor_reduce(blk[:, m, :].rearrange("p (y b) -> p y b", b=NBS), src, AX.X, ALU.add))
            ve.tensor_scalar(blk[:], blk[:], 1.0 / BLOCK ** 2, None, ALU.mult).then_inc(sem("blk_ready"), 1)
            dve.wait_ge(sem("p_blkT"), 1)
            ve.tensor_copy(blkT[:], PS[0:NBLK, 1, 0:2 * C].rearrange("p (i c) -> p i c", i=IMAGES)).then_inc(sem("blkT"), 1)
            dve.wait_ge(sem("p_score"), 1)
            link(ve.tensor_scalar(score[:], PS[0:1, 0, 128:128 + 98].rearrange("p (i n) -> p i n", i=IMAGES), row[0:1, R_S2B:R_S2B + 1], None, ALU.add))
            for m in range(IMAGES):
                link(ve.max(top[:, m, :], score[:, m, :]))
            for m in range(IMAGES):
                link(ve.max_index(topi[:, m, :], top[:, m, :], score[:, m, :]))
            ve.tensor_copy(topf[:], topi[:]).then_inc(sem("topf"), 1)
            dve.wait_ge(sem("p_idx"), 1)
            ve.tensor_scalar(onehot[:], PS[0:NBLK, 0, 256:272].rearrange("p (i n) -> p i n", i=IMAGES), cst[0:NBLK, CIO:CIO + 1], None, ALU.is_equal).then_inc(sem("onehot"), 1)
            ve.tensor_scalar(gl[:, 0, 0:3], v(V_GW, 3), v(V_N1W), None, ALU.mult).then_inc(sem("c1"), 1)
            ve.memset(gl[:, 1, 3:4], 1.0 / C).then_inc(sem("c1"), 1)
            link(ve.tensor_copy(n1rep[:], bc(v(V_N1B), [128, TILE])))
            for n in range(2):
                link(ve.tensor_copy(bq35[:, n, :], bc(v(V_BQ + n), [128, 35])))
            r4 = R[:, :, 0:2 * NBLK].rearrange("p i (e n) -> p i e n", e=2)
            for e in range(2):
                link(ve.tensor_copy(r4[:, :, e, :], blk[:]))
            dve.wait_ge(sem("p_ksel"), 1)
            for e in range(2):
                ve.tensor_copy(R[:, :, 2 * NBLK + TOPK * e:2 * NBLK + TOPK * (e + 1)],
                               PS[:, 2, 0:16].rearrange("p (i n) -> p i n", i=IMAGES)[:, :, 0:TOPK]).then_inc(sem("rows_ready"), 1)
            for m in range(IMAGES):
                dve.wait_ge(sem("p_keys"), m + 1)
                link(ve.tensor_scalar(k0[:], PS[:, 0, 0:NBLK], v(V_BK), SCALE, ALU.add, ALU.mult))
                link(ve.tensor_scalar(k1[:], PS[:, 0, 64:64 + TOPK], v(V_BK + 1), SCALE, ALU.add, ALU.mult))
                hm = cst[:, CH:CH + HEADS].rearrange("p (j e) -> p j e", e=2)
                for e in range(2):
                    for kk, o, n in ((k0, NBLK * e, NBLK), (k1, 2 * NBLK + TOPK * e, TOPK)):
                        last = ve.tensor_tensor(KM[:, :, o:o + n], bc(kk[:].unsqueeze(1), [128, PAIRS, n]), bc(hm[:, :, e:e + 1], [128, PAIRS, n]), ALU.mult)
                        if (e, n) != (1, TOPK):
                            link(last)
                last.then_inc(sem("km_ready"), 1)
                dve.wait_ge(sem("p_vals"), m + 1)
                for n in range(2):
                    vf = PS[0:KC, 1, C * n:C * (n + 1)].rearrange("p (j d) -> p j d", j=PAIRS)
                    vm = cst[0:KC, CVM + 32 * n:CVM + 32 * (n + 1)]
                    ve.tensor_tensor(VB[m][:, :, 32 * n:32 * (n + 1)], vf, bc(vm.unsqueeze(1), [KC, PAIRS, 32]), ALU.mult).then_inc(sem("attn_ops"), 1)
                ve.tensor_copy(VB[m][:, :, 64:68], bc(cst[0:KC, CVM + 64:CVM + 68].unsqueeze(1), [KC, PAIRS, 4])).then_inc(sem("attn_ops"), 1)
                dve.wait_ge(sem("p_fold"), m + 1)
                link(ve.tensor_copy(Af[m][:], PS[:, 2, 0:SC]))
                link(ve.tensor_copy(Ah[m][:], Af[m][:]))
                link(ve.tensor_tensor(Al[m][:], Af[m][:], Ah[m][:], ALU.subtract))
                link(ve.tensor_copy(cs[:], PS[0:35, 3, 0:SC]))
                prev = cst[0:35, CE:CE + SC]
                for part in range(3):
                    link(ve.tensor_copy(chb[:], cs[:]))
                    dst = ES[m] if part == 2 else ch[part]
                    link(ve.scalar_tensor_tensor(out=dst[:], in0=chb[:], scalar=cst[0:35, CM + part:CM + part + 1], in1=prev, op0=ALU.mult, op1=ALU.add))
                    prev = ch[part][:]
                    if part < 2:
                        link(ve.tensor_tensor(cs[:], cs[:], chb[:], ALU.subtract))
                ve.memset(c1[:, 4 + m:5 + m], 0.0).then_inc(sem("attn_ops"), 1)
            dve.wait_ge(sem("p_rows"), 1)
            link(ve.tensor_copy(BV2[:], PS[0:124, 4, 0:C]))
            link(ve.tensor_copy(cg[:], PS[0:TILE, 4, 256:259]))
            for m in range(IMAGES):
                dve.wait_ge(sem("high"), m + 1)
                ve.tensor_tensor(XL[:, m, :], xt(m), XH[:, m, :], ALU.subtract).then_inc(sem("split"), 1)
            for n, (m, which, at0, cols) in enumerate(pjobs):
                dve.wait_ge(sem("proj_read"), n + 1)
                dve.wait_ge(sem("proj_full"), n + 1)
                if n >= 1:
                    dve.wait_ge(sem("parts_ready"), n)
                p, f = pk[n % 2], pf[n % 2]
                link(ve.tensor_tensor(pr[:, 0:cols], f[:, 0:cols], p[:, 0, 0:cols], ALU.subtract))
                link(ve.tensor_copy(p[:, 1, 0:cols], pr[:, 0:cols]))
                ve.tensor_tensor(p[:, 2, 0:cols], pr[:, 0:cols], p[:, 1, 0:cols], ALU.subtract).then_inc(sem("parts_ready"), 1)
            for n, (m, g, k) in enumerate(vjobs):
                dve.wait_ge(sem("vals"), n + 1)
                if n >= 2:
                    dve.wait_ge(sem(f"v_stored{n % 2}"), 16 * (n // 2))
                o = vst[n % 2][:, 0:k, :].rearrange("p t (j d) -> p (t j) d", d=VCOLS)[:, :, 0:2 * DH]
                i0 = PS[0:124, 7, 0:C * k].rearrange("p (t d) -> p t d", d=2 * DH)
                for t in range(k):
                    last = ve.tensor_tensor(o[:, PAIRS * t:PAIRS * (t + 1), :], i0[:, PAIRS * t:PAIRS * (t + 1), :],
                                            BV2[:].rearrange("p (j d) -> p j d", j=PAIRS), ALU.add)
                last.then_inc(sem("v_ready"), 1)
            for n in range(NGJ):
                m, b = gjobs[n]
                dve.wait_ge(sem("g_mean"), n + 1)
                if n >= 2:
                    dve.wait_ge(sem("g_logits"), n - 1)
                ve.tensor_tensor(xc[n % 2][:], xt(m)[:, b * BAND:(b + 1) * BAND], PS[:, 0, 0:BAND], ALU.subtract).then_inc(sem("g_centred"), 1)
                dve.wait_ge(sem("g_logits"), n + 1)
                ve.tensor_copy(ls[n % 2][:], PS[0:4, 1, 0:BAND])
                ve.tensor_copy(ls2[n % 2][:], bc(PS[0:4, 1, 0:BAND].rearrange("p (s n) -> p s n", n=SUB).unsqueeze(2), [4, SUBS, 2, SUB])).then_inc(sem("g_logits_read"), 1)
                dve.wait_ge(sem("g_byquery"), n + 1)
                ve.tensor_copy(G[:, m, b, :, :], PS[0:TILE, 2, 0:48].rearrange("p (s k) -> p s k", k=4)).then_inc(sem("g_stored"), 1)
            g4 = G[:].rearrange("p i b s k -> p (i b s) k")
            g3 = g4[:, :, 0:3]
            dve.wait_ge(sem("g_stored"), NGJ)
            dve.wait_ge(sem("g_std"), 1)
            link(ve.reciprocal(gst[:], gst[:]))
            link(ve.tensor_tensor(g3, g3, bc(gst[:].unsqueeze(2), [TILE, NG, 3]), ALU.mult))
            link(ve.tensor_tensor(g3, g3, bc(cg[:].unsqueeze(1), [TILE, NG, 3]), ALU.add))
            link(ve.tensor_reduce(gmx[:], g3, AX.X, ALU.max))
            ve.tensor_tensor(g3, g3, bc(gmx[:].unsqueeze(2), [TILE, NG, 3]), ALU.subtract).then_inc(sem("g_shifted"), 1)
            dve.wait_ge(sem("g_exp"), 1)
            link(ve.tensor_reduce(gst[:], g3, AX.X, ALU.add))
            link(ve.reciprocal(gmx[:], gst[:]))
            link(ve.tensor_tensor(g3, g3, bc(gmx[:].unsqueeze(2), [TILE, NG, 3]), ALU.mult))
            ve.memset(c1[:, 6:7], 0.0).then_inc(sem("gates"), 1)
            ve.memset(c1[:, 7:8], 0.0).then_inc(sem("setup_done"), 2)

            def c_body(i, tail):
                for k in range(CLAG if tail else CB):
                    s = at(i, k, 0, CB, CT)
                    if s:
                        num, t, r = s
                        dve.wait_ge(sem("c_sa"), num + 1)
                        if not (isinstance(num, int) and num < 1):
                            dve.wait_ge(sem("c_shift"), num)
                        s4 = PS[0:TILE, r % 2, 0:SC].rearrange("p (j k) -> p j k", j=PAIRS)
                        o = nm[:].rearrange("p (t j e) -> p t j e", t=2, e=2)
                        ve.tensor_reduce(o[:, 0, :, :], s4[:, :, 0:2 * NBLK].rearrange("p j (e n) -> p j e n", e=2), AX.X, ALU.max, negate=True).then_inc(sem("c_max1"), 1)
                        ve.tensor_reduce(o[:, 1, :, :], s4[:, :, 2 * NBLK:KC].rearrange("p j (e n) -> p j e n", e=2), AX.X, ALU.max, negate=True).then_inc(sem("c_maxed"), 1)
                        dve.wait_ge(sem("c_maxed"), num + 1)
                        dve.wait_ge(sem("c_max1"), num + 1)
                        if not (isinstance(num, int) and num < 2):
                            dve.wait_ge(sem("c_shiftT"), num - 1)
                        ve.tensor_copy(nmb[r % 2][:, 0:16], nm[:]).then_inc(sem("c_high"), 1)
                        dve.wait_ge(sem("c_high"), num + 1)
                        ve.tensor_tensor(nmb[r % 2][:, 16:32], nm[:], nmb[r % 2][:, 0:16], ALU.subtract).then_inc(sem("c_shift"), 1)
                    s = at(i, k, 1, CB, CT)
                    if s:
                        num, t, r = s
                        dve.wait_ge(sem("c_shiftT"), num + 1)
                        if not (isinstance(num, int) and num < 2):
                            dve.wait_ge(sem("c_sb"), num - 1)
                        ve.tensor_copy(MV[r % 2][0:32, :], PS[0:32, 2, 0:TILE // 2].bitcast(BF16)).then_inc(sem("c_shift_used"), 1)
                    s = at(i, k, 3, CB, CT)
                    if s:
                        num, t, r = s
                        img, c = divmod(r, TILES)
                        dve.wait_ge(sem("c_pv"), num + 1)
                        if not (isinstance(num, int) and num < 1):
                            dve.wait_ge(sem("c_norm"), num)
                        if not (isinstance(num, int) and num < 2):
                            dve.wait_ge(sem("c_tr"), num - 1)
                        pv = PS[0:TILE, 5, 0:68 * PAIRS].rearrange("p (j k) -> p j k", j=PAIRS)
                        gg = G[:, img, ds(t, 1), 8 + c, 0:2] if not isinstance(t, int) else G[:, img, t:t + 1, 8 + c, 0:2]
                        ve.reciprocal(rd[:].rearrange("p a j e -> p j a e"), pv[:, :, 64:68].rearrange("p j (a e) -> p j a e", e=2)).then_inc(sem("c_recip"), 1)
                        dve.wait_ge(sem("c_recip"), num + 1)
                        for ty in range(2):
                            ve.tensor_scalar(rg[:, ty, :, :], rd[:, ty, :, :], gg[:, 0, ty:ty + 1], None, ALU.mult).then_inc(sem("c_gated"), 1)
                        dve.wait_ge(sem("c_gated"), 2 * num + 2)
                        ve.tensor_scalar(oc[r % 2][:, 256:259], G[:, img, ds(t, 1), 8 + c, 0:3].rearrange("p a k -> p (a k)") if not isinstance(t, int) else G[:, img, t, 8 + c, 0:3], 1.0, None, ALU.mult).then_inc(sem("c_gcol"), 1)
                        dve.wait_ge(sem("c_gcol"), num + 1)
                        for ty in range(2):
                            o = oc[r % 2][:, C * ty:C * (ty + 1)].rearrange("p (j e d) -> p j e d", e=2, d=DH)
                            last = ve.tensor_tensor(o, pv[:, :, 32 * ty:32 * (ty + 1)].rearrange("p j (e d) -> p j e d", e=2),
                                                    bc(rg[:, ty, :, :].unsqueeze(3), [TILE, PAIRS, 2, DH]), ALU.mult)
                        last.then_inc(sem("c_norm"), 1)
                    s = at(i, k, 5, CB, CT)
                    if s:
                        num, t, r = s
                        img, c = divmod(r, TILES)
                        dve.wait_ge(sem("c_y"), num + 1)
                        xs = XT[:, img, ds(t * BAND + c * TILE, TILE)]
                        ve.tensor_tensor(xs, PS[:, 7, 0:TILE], xs, ALU.add).then_inc(sem("c_added"), 1)

            run_loop(dve, c_body, BANDS, True)

            dve.wait_ge(sem("c_added"), CT)

            def w_body(i, ks):
                lst = pa_list(i, ks)
                for k in ks:
                    mine = [e for e in lst if e[0] == k]

                    def paj(kinds):
                        for _, kind, n, slot, before, last_use in mine:
                            if kind not in kinds:
                                continue
                            dve.wait_ge(sem("w_slot"), before + 1)
                            if kind == "A":
                                num, t, r = wjob(i, n)
                                tl, hp = divmod(r, 4)
                                if hp == 0 and not (isinstance(num, int) and num < 8):
                                    dve.wait_ge(sem("w_split"), t * (WB // 4) + tl - 1)
                                src = PS[0:TILE, 2 * slot:2 * slot + 2, 0:KROWS * TCOLS]
                                ve.tensor_reduce(wn[tl % 2][:, 2 * hp:2 * hp + 2], src, AX.X, ALU.max, negate=True).then_inc(sem("w_slot_read"), 1)
                                if hp == 3:
                                    dve.wait_ge(sem("w_slot_read"), before + 1)
                                    if not (isinstance(num, int) and num < 8):
                                        dve.wait_ge(sem("w_shiftT"), t * (WB // 4) + tl - 1)
                                    ve.tensor_copy(wnb[tl % 2][:, 0, :], wn[tl % 2][:]).then_inc(sem("w_high"), 1)
                                    dve.wait_ge(sem("w_high"), t * (WB // 4) + tl + 1)
                                    ve.tensor_tensor(wnb[tl % 2][:, 1, :], wn[tl % 2][:], wnb[tl % 2][:, 0, :], ALU.subtract).then_inc(sem("w_split"), 1)
                            if kind == "S":
                                num, t, r = wjob(i, n, WB // 4, WT // 4)
                                if not (isinstance(num, int) and num < 2):
                                    dve.wait_ge(sem(f"w_shift{r % 2}"), (t * (WB // 8) + r // 2) * 16)
                                src = PS[0:2 * HEADS, 2 * slot, 0:TILE // 2].bitcast(BF16)
                                ve.tensor_copy(nT[r % 2][:], src).then_inc(sem("w_shiftT"), 1)
                                dve.wait_ge(sem("w_shiftT"), num + 1)
                                ve.memset(c1[0:1, 0:1], 0.0).then_inc(sem("w_slot_read"), 1)
                            if kind == "T":
                                num, t, r = wjob(i, n, WB // 4, WT // 4)
                                img, c = divmod(r, TILES)
                                ve.tensor_copy(ow[img][:, c * TILE:(c + 1) * TILE], PS[:, 2 * slot, 0:TILE]).then_inc(sem("w_ot"), 1)
                                dve.wait_ge(sem("w_ot"), num + 1)
                                ve.memset(c1[0:1, 0:1], 0.0).then_inc(sem("w_slot_read"), 1)
                            if kind == "Y":
                                num, t, r = wjob(i, n, 2, 2 * BANDS)
                                o = X[:, r, ds(t * BAND, BAND)].rearrange("p (r s c) -> p s r c", s=SUBS, c=SUBC)
                                xs = XT[:, r, ds(t * BAND, BAND)].rearrange("p (s r c) -> p s r c", s=SUBS, c=SUBC)
                                ve.tensor_tensor(o, PS[:, 2 * slot, 0:BAND].rearrange("p (s r c) -> p s r c", s=SUBS, c=SUBC), xs, ALU.add).then_inc(sem("w_y"), 1)
                                dve.wait_ge(sem("w_y"), num + 1)
                                ve.memset(c1[0:1, 0:1], 0.0).then_inc(sem("w_slot_read"), 1)

                    paj("AS")
                    if k % 2 == 1:
                        s = wjob(i, (k - 3) // 2, WB // 2, WT // 2)
                        if s:
                            num, t, r = s
                            img, c = divmod(r, SUBS)
                            dve.wait_ge(sem("w_products"), 2 * num + 2)
                            if not (isinstance(num, int) and num < 1):
                                dve.wait_ge(sem("w_norm"), num)
                            if not (isinstance(num, int) and num < 4):
                                dve.wait_ge(sem("w_ot"), t * (WB // 4) + r // 2 - 1)
                            po = PS[0:TILE, 6 + r % 2, 0:PAIRS * VCOLS].rearrange("p (j k) -> p j k", k=VCOLS)
                            gt = (G[:, img, ds(t, 1), c, 2:3].rearrange("p a k -> p (a k)")) if not isinstance(t, int) else G[:, img, t, c, 2:3]
                            ve.tensor_scalar(gm[:], cst[0:TILE, CEM:CEM + 2], gt, None, ALU.mult).then_inc(sem("w_n1"), 1)
                            ve.reciprocal(wr[:], po[:, :, 2 * DH]).then_inc(sem("w_n1"), 1)
                            dve.wait_ge(sem("w_n1"), 2 * num + 2)
                            ve.tensor_tensor(wr2[:], bc(wr[:].unsqueeze(2), [TILE, PAIRS, 2]), bc(gm[:].unsqueeze(1), [TILE, PAIRS, 2]), ALU.mult).then_inc(sem("w_n2"), 1)
                            dve.wait_ge(sem("w_n2"), num + 1)
                            ve.tensor_tensor(tw[r % 4][:].rearrange("p (j e d) -> p j e d", e=2, d=DH), po[:, :, 0:2 * DH].rearrange("p j (e d) -> p j e d", e=2),
                                             bc(wr2[:].unsqueeze(3), [TILE, PAIRS, 2, DH]), ALU.mult).then_inc(sem("w_norm"), 1)
                    paj("TY")

            run_window(dve, w_body)

            cq = chain
            for m in range(IMAGES):
                for pair in range(2):
                    for half in range(2):
                        q = 4 * m + 2 * pair + half
                        grp = pair + 2 * half
                        dve.wait_ge(sem("t_read"), BANDS * (q + 1))
                        dve.wait_ge(sem("t_full"), BANDS * (q + 1))
                        ti = T[q % 2][:].rearrange("p (r c) -> p r c", c=SIDE)
                        ai = AC[q % 2][:].rearrange("p (r c) -> p r c", c=SIDE)
                        conv(lambda r, rn, c, cn: ti[:, r:r + rn, c:c + cn], lambda r, rn, c, cn: ai[:, r:r + rn, c:c + cn], V_DW + 9 * grp, m)
                        ve.memset(c1[0:1, 0:1], 0.0).then_inc(sem("conv2"), 1)
                    dve.wait_ge(sem("gelu"), 2 * m + pair + 1)
                    if m and pair == 0:
                        dve.wait_ge(sem("z_proj"), BANDS * m)
                    ve.tensor_tensor(U[pair][:], AC[0][:], AC[1][:], ALU.mult).then_inc(sem("hidden"), 1)
                for b in range(BANDS):
                    n = m * BANDS + b
                    dve.wait_ge(sem("z_proj"), n + 1)
                    xs = X[:, m, b * BAND:(b + 1) * BAND]
                    ve.tensor_tensor(xs, PS[:, 2 + n % 2, 0:BAND], xs, ALU.add).then_inc(sem("z_sum"), 1)
            for n in range(IMAGES * BANDS + 1):
                if n < IMAGES * BANDS:
                    m, b = divmod(n, BANDS)
                    dve.wait_ge(sem("z_mean"), n + 1)
                    if n >= 2:
                        dve.wait_ge(sem("z_scaled"), n - 1)
                    ve.tensor_tensor(zc[n % 2][:], X[:, m, b * BAND:(b + 1) * BAND], PS[:, 4 + n % 2, 0:BAND], ALU.subtract).then_inc(sem("z_centred"), 1)
                if n >= 1:
                    q = n - 1
                    dve.wait_ge(sem("z_std"), q + 1)
                    ve.reciprocal(sd[q % 2][:], sd[q % 2][:]).then_inc(sem("z_rstd"), 1)
                    dve.wait_ge(sem("z_rstd"), q + 1)
                    if q >= 2:
                        dve.wait_ge(sem(f"z_stored{q % 2}"), 16 * (q // 2))
                    ve.tensor_tensor(sd[q % 2][:], zc[q % 2][:], sd[q % 2][:], ALU.mult).then_inc(sem("z_scaled"), 1)
                    dve.wait_ge(sem("z_scaled"), q + 1)
                    ve.tensor_scalar(zo[q % 2][:], sd[q % 2][:], v(V_N2W), v(V_N2B), ALU.mult, ALU.add).then_inc(sem("z_ready"), 1)


_OUT = (IMAGES, C, SIDE, SIDE)


def kernel(**inputs):
    import concourse.bacc as _bacc
    from concourse.bass_utils import run_bass_kernel_spmd as _run

    a = {n.replace("L0_conv_", ""): np.ascontiguousarray(t) for n, t in inputs.items()}
    wts = np.concatenate(
        [a["wq_w"][0], a["wq_w"][1], a["wq_w"][2].T, a["wk_w"][0].T, a["wk_w"][1].T, a["wk_w"][2].T,
         a["wv_w"][0].T, a["wv_w"][1].T, a["wv_w"][2].T, a["pj_w"][0].T, a["pj_w"][1].T, a["pj_w"][2].T,
         a["s1_w"].T, a["pin_w"].T, a["pout_w"].T[0:C], a["pout_w"].T[C:]], 1)
    vecs = np.zeros((128, NV), np.float32)
    vecs[:, V_POSW:V_POSW + 9] = a["pos_w"].reshape(C, 9)
    for col, name in ((V_POSB, "pos_b"), (V_N1W, "n1_w"), (V_N1B, "n1_b"), (V_N2W, "n2_w"), (V_N2B, "n2_b")):
        vecs[:, col] = a[name]
    vecs[:, V_BQ:V_BQ + 3] = a["wq_b"].T
    vecs[:, V_BK:V_BK + 3] = a["wk_b"].T
    for g in range(4):
        vecs[:, V_DW + 9 * g:V_DW + 9 * (g + 1)] = a["dw_w"].reshape(9, 2 * HID)[:, C * g:C * (g + 1)].T
    vecs[0:64, V_S1B] = a["s1_b"]
    vecs[0:64, V_S2] = a["s2_w"][0]
    vecs[:, V_GW:V_GW + 3] = a["g_w"].T
    rows = np.concatenate([a["wv_b"].reshape(-1), a["g_b"], a["s2_b"]])[None]
    c32, cmask = shape_constants()
    arrays = {"x": a["x"].reshape(IMAGES, C, PIX), "wts": wts, "vecs": vecs, "rows": rows, "pjb": a["pj_b"], "c32": c32, "cmask": cmask}
    nc = _bacc.Bacc("TRN2", target_bir_lowering=False, num_devices=1)
    args = {n: nc.dram_tensor(f"in_{n}", t.shape, mybir.dt.from_np(t.dtype), kind="ExternalInput").ap() for n, t in arrays.items()}
    out = nc.dram_tensor("out_y", (IMAGES, C, PIX), F32, kind="ExternalOutput").ap()
    build(nc, out=out, **args)
    r = _run(nc, [{f"in_{n}": np.ascontiguousarray(t) for n, t in arrays.items()}], core_ids=[0])
    return r.results[0]["out_y"].reshape(_OUT)
```

```python
from contextlib import ExitStack

import numpy as np

import concourse.bass as bass
from concourse import mybir

F32 = mybir.dt.float32
BF16 = mybir.dt.bfloat16
U32 = mybir.dt.uint32
ALU = mybir.AluOpType
ACT = mybir.ActivationFunctionType
AX = mybir.AxisListType
ds = bass.ds

C = 128
IMAGES = 2
SIDE = 56
PIX = SIDE * SIDE
HEADS, DH = 8, 16
BLOCK = 8
NBS = SIDE // BLOCK
NBLK = NBS * NBS
TOPK = 4
WIN = 7
PAD = WIN // 2
PSIDE = SIDE + 2 * PAD
PPIX = PSIDE * PSIDE
BANDS = SIDE // BLOCK
BAND = BLOCK * SIDE
SUBC = 7
SUB = BLOCK * SUBC
SUBS = SIDE // SUBC
TILE = 2 * SUB
TILES = SUBS // 2
KROWS = BLOCK + WIN - 1
KCOLS = SUBC + WIN - 1
HCOLS = (7, KCOLS - 7)
HKEYS = [n * KROWS for n in HCOLS]
KEYS = max(HKEYS)
KBAND = KROWS * PSIDE
TCOLS = 2 * SUBC + WIN - 1
PAIRS = HEADS // 2
VH = DH + 1
VROW = HEADS * VH
QUAD = 32
KC = 2 * NBLK + 2 * TOPK
SC = PAIRS * KC
TERMS = ((0, 0), (0, 1), (1, 0), (1, 1), (0, 2), (2, 0))
MASK0 = len(TERMS) * DH
SHIFT0 = 126
HID = 2 * C
SCALE = float(DH) ** -0.5
EPS = 1e-6
BIG = 2.0 ** 99

WNAMES = ("wq0", "wq1", "wq2", "wk0", "wk1", "wk2", "wv0", "wv1", "wv2", "pj0", "pj1")
WCOL = {n: C * k for k, n in enumerate(WNAMES)}
WCOL["s1"] = C * len(WNAMES)
WCOL["pin"] = WCOL["s1"] + C // 2
WCOL["pout"] = WCOL["pin"] + 2 * HID
WCOL["pj2"] = WCOL["pout"] + HID
NW = WCOL["pj2"] + 2 * C
V_POSW, V_POSB, V_N1W, V_N1B, V_N2W, V_N2B, V_BQ, V_BK, V_DW, V_S1B, V_S2, V_GW = 0, 9, 10, 11, 12, 13, 14, 17, 20, 56, 57, 58
NV = 61
R_BV, R_GB, R_S2B, NR = 0, 3 * C, 3 * C + 3, 3 * C + 4
CI, CH, CVM, CIO, CM, CD, CG, CE = 0, 128, 136, 204, 205, 208, 336, 464
NC32 = CE + SC
TAPS = [(dy, dx) for dy in (-1, 0, 1) for dx in (-1, 0, 1)]
SIDE_TAPS = [t for t in range(9) if t != 4]


def shape_constants():
    c = np.zeros((128, NC32), np.float32)
    c[:, CI:CI + 128] = np.eye(128)
    c[:, CH:CH + HEADS] = np.arange(128)[:, None] // DH == np.arange(HEADS)
    for e in range(2):
        for rows, o in ((slice(e * NBLK, (e + 1) * NBLK), 0), (slice(2 * NBLK + e * TOPK, 2 * NBLK + (e + 1) * TOPK), 1)):
            c[rows, CVM + o * 32 + e * DH:CVM + o * 32 + (e + 1) * DH] = 1
            c[rows, CVM + 64 + 2 * o + e] = 1
            for j in range(PAIRS):
                for part in range(2):
                    c[16 * part + 8 * o + 2 * j + e, CE + j * KC + rows.start:CE + j * KC + rows.stop] = 1
    c[:, CIO] = np.arange(128)
    for m in range(128):
        c[QUAD * (m // QUAD) + DH, CD + m] = 1
    c[2, CG:CG + 128] = 1
    for part in range(3):
        c[32 + part, CM + part] = 1
    ck = np.zeros((32, PSIDE, KROWS), np.float32)
    cq = np.zeros((32, SUBS, BLOCK, SUBC), np.float32)
    X, x = np.arange(PSIDE).reshape(-1, 1), np.arange(SIDE).reshape(SUBS, 1, SUBC)
    r = np.arange(BLOCK).reshape(1, BLOCK, 1)
    for j in range(14):
        ck[j, :, j] = 1
        cq[j] = np.where((j >= r) & (j < r + WIN), 0, -BIG)
        ck[14 + j] = X % 14 == j
        cq[14 + j] = np.where((j - x) % 14 < WIN, 0, -BIG)
    ck[28] = X % 28 < 6
    ck[29] = (X % 28 >= 14) & (X % 28 < 20)
    tile, rel = x // 14, x % 14
    cq[28] = np.where(tile % 2 == 0, np.where(rel >= 6, -BIG, 0), np.where(rel <= 7, -BIG, 0))
    cq[29] = np.where(tile % 2 == 1, np.where(rel >= 6, -BIG, 0), np.where(rel <= 7, -BIG, 0))
    ck[30:] = 1
    return c, np.concatenate([ck.reshape(32, -1), cq.reshape(32, -1)], 1)


def bc(ap, shape):
    return ap.broadcast_to(shape)


def build(nc, x, wts, vecs, rows, pjb, c32, cmask, out):
    ctx = ExitStack()
    with ctx:
        def sb(name, shape, dt=F32, stack=ctx):
            return stack.enter_context(nc.sbuf_tensor(name, shape, dt))

        sems = {}

        def sem(name):
            if name not in sems:
                sems[name] = ctx.enter_context(nc.semaphore(name))
            return sems[name]

        q_dram = nc.dram_tensor("q_parts", [3, C, IMAGES, PIX], BF16, kind="Internal").ap()
        k_dram = nc.dram_tensor("k_parts", [3, C, IMAGES, BANDS * KBAND], BF16, kind="Internal").ap()
        v_dram = nc.dram_tensor("v_rows", [IMAGES, PSIDE, PSIDE, VROW], F32, kind="Internal").ap()
        v_flat = v_dram.rearrange("i r c v -> i (r c) v")

        PS = ctx.enter_context(nc.psum_tensor("banks", [128, 8, 512], F32))

        W = sb("W", [128, NW])
        vec = sb("vec", [128, NV])
        row = sb("row", [1, NR])
        pjrow = sb("pjrow", [3, C])
        cst = sb("cst", [128, NC32])
        identb = sb("identb", [TILE, TILE], BF16)
        ones = sb("ones", [128, 128])
        meanw = sb("meanw", [128, 128])
        epsc = sb("epsc", [128, 1])
        X = sb("X", [128, IMAGES, PIX])
        G = sb("G", [TILE, IMAGES, BANDS, 12, 4])

        c1 = sb("c1", [128, 8])

        att = ctx.enter_context(ExitStack())
        FP = sb("FP", [128, IMAGES, PSIDE, PSIDE], F32, att)
        XT = sb("XT", [128, IMAGES, PIX], F32, att)
        GB = FP[:].rearrange("p i r c -> p (i r c)")[:, 0:IMAGES * PIX].rearrange("p (i n) -> p i n", i=IMAGES)
        early = ctx.enter_context(ExitStack())
        XH = sb("XH", [128, IMAGES, PIX], BF16, early)
        XL = sb("XL", [128, IMAGES, PIX], BF16, early)
        bs1 = sb("bs1", [128, IMAGES, SIDE, NBS], F32, early)
        Af = [sb(f"Af{m}", [128, SC], F32, early) for m in range(IMAGES)]
        Ah = [sb(f"Ah{m}", [128, SC], BF16, early) for m in range(IMAGES)]
        Al = [sb(f"Al{m}", [128, SC], BF16, early) for m in range(IMAGES)]
        ES = [sb(f"ES{m}", [35, SC], BF16, early) for m in range(IMAGES)]
        VB = [sb(f"VB{m}", [KC, PAIRS, 68], F32, early) for m in range(IMAGES)]
        BV2 = sb("BV2", [124, C], F32, early)

        def xt(img):
            return XT[:, img, :]

        with ExitStack() as s1:
            blk = sb("blk", [128, IMAGES, NBLK], F32, s1)
            hs = sb("hs", [64, IMAGES * NBLK], F32, s1)
            score = sb("score", [1, IMAGES, NBLK], F32, s1)
            top = sb("top", [1, IMAGES, 8], F32, s1)
            topi = sb("topi", [1, IMAGES, 8], U32, s1)
            topf = sb("topf", [1, IMAGES, 8], F32, s1)
            onehot = sb("onehot", [NBLK, IMAGES, 8], F32, s1)
            blkT = sb("blkT", [NBLK, IMAGES, C], F32, s1)
            R = sb("R", [128, IMAGES, KC], F32, s1)
            k0 = sb("k0", [128, NBLK], F32, s1)
            k1 = sb("k1", [128, TOPK], F32, s1)
            KM = sb("KM", [128, PAIRS, KC], F32, s1)
            bq35 = sb("bq35", [128, 2, 35], F32, s1)
            cs = sb("cs", [35, SC], F32, s1)
            ch = [sb(f"ch{n}", [35, SC], F32, s1) for n in range(3)]
            chb = sb("chb", [35, SC], BF16, s1)
            pk = [sb(f"pk{n}", [128, 3, 512], BF16, s1) for n in range(2)]
            pf = [sb(f"pf{n}", [128, 512], F32, s1) for n in range(2)]
            pr = sb("pr", [128, 512], F32, s1)
            pq = sb("pq", [128, 512], F32, s1)
            vst = [sb(f"vst{n}", [124, 4, VROW], F32, s1) for n in range(2)]
            gl = sb("gl", [128, 2, 4], F32, s1)
            n1rep = sb("n1rep", [128, TILE], F32, s1)
            cg = sb("cg", [TILE, 3], F32, s1)
            xc = [sb(f"xc{n}", [128, BAND], F32, s1) for n in range(2)]
            sq = [sb(f"sq{n}", [128, BAND], F32, s1) for n in range(2)]
            ls = [sb(f"ls{n}", [4, BAND], F32, s1) for n in range(2)]
            ls2 = [sb(f"ls2{n}", [4, SUBS, 2, SUB], F32, s1) for n in range(2)]
            NG = IMAGES * BANDS * 12
            gst = sb("gst", [TILE, NG], F32, s1)
            gmx = sb("gmx", [TILE, NG], F32, s1)
        with ExitStack() as s2:
            nm = sb("nm", [TILE, 16], F32, s2)
            nmb = [sb(f"nmb{n}", [TILE, 32], BF16, s2) for n in range(2)]
            cst35 = sb("cst35", [35, TILE], BF16, s2)
            MV = [sb(f"MV{n}", [35, TILE], BF16, s2) for n in range(2)]
            PC = [sb(f"PC{n}", [KC, PAIRS * TILE], F32, s2) for n in range(2)]
            rd = sb("rd", [TILE, 2, PAIRS, 2], F32, s2)
            rg = sb("rg", [TILE, 2, PAIRS, 2], F32, s2)
            oc = [sb(f"oc{n}", [TILE, 260], F32, s2) for n in range(2)]
            ot = [sb(f"ot{n}", [128, 3 * TILE], F32, s2) for n in range(2)]
        early.close()
        with ExitStack() as s3:
            K = [sb(f"K{m}", [128, HEADS * KBAND + 64], BF16, s3) for m in range(IMAGES)]
            Q = [sb(f"Q{m}", [128, HEADS, BAND], BF16, s3) for m in range(IMAGES)]
            Vw = [sb(f"Vw{n}", [KEYS, 2, VROW], F32, s3) for n in range(4)]
            P = [sb(f"P{n}", [KEYS, HEADS * SUB], F32, s3) for n in range(4)]
            wn = [sb(f"wn{n}", [TILE, HEADS], F32, s3) for n in range(2)]
            wnb = [sb(f"wnb{n}", [TILE, 2, HEADS], BF16, s3) for n in range(2)]
            nT = [sb(f"nT{n}", [2 * HEADS, TILE], BF16, s3) for n in range(2)]
            OB = [sb(f"OB{n}", [128, 2, BAND], F32, s3) for n in range(2)]
            RD = sb("RD", [128, 2, BAND], F32, s3)
            ON = [sb(f"ON{n}", [128, 2, BAND], F32, s3) for n in range(2)]
            yt = sb("yt", [128, BAND], F32, s3)
            stage = sb("stage", [128, KBAND + BAND], F32, s3)
        att.close()
        with ExitStack() as s4:
            T = [sb(f"T{n}", [128, PIX], F32, s4) for n in range(2)]
            AC = [sb(f"AC{n}", [128, PIX], F32, s4) for n in range(2)]
            U = [sb(f"U{n}", [128, PIX], F32, s4) for n in range(2)]
            zc = [sb(f"zc{n}", [128, BAND], F32, s4) for n in range(2)]
            zq = [sb(f"zq{n}", [128, BAND], F32, s4) for n in range(2)]
            sd = [sb(f"sd{n}", [128, BAND], F32, s4) for n in range(2)]
            zo = [sb(f"zo{n}", [128, BAND], F32, s4) for n in range(2)]

        def w(name, n=C, off=0):
            return W[:, WCOL[name] + off:WCOL[name] + off + n]

        def v(col, n=1, p=128):
            return vec[0:p, col:col + n]

        LOADS = 6
        block = ctx.enter_context(nc.Block())

        pjobs = [(m, "k", h * KBAND // 2, KBAND // 2) for m in range(IMAGES) for h in range(2 * BANDS)]
        pjobs += [(m, "q", b * BAND, BAND) for m in range(IMAGES) for b in range(BANDS)]
        NPJ = len(pjobs)
        vjobs = [(m, g, min(4, 31 - 4 * g)) for m in range(IMAGES) for g in range(8)]
        NVJ = len(vjobs)
        gjobs = [(m, b) for m in range(IMAGES) for b in range(BANDS)]
        NGJ = len(gjobs)

        CT = IMAGES * BANDS * TILES
        CB = IMAGES * TILES
        CLAG = 5

        def each_tile(i, last, emit):
            for k in range(CLAG if last else CB):
                emit(i, k)

        def at(i, k, lag, per, total):
            turn, place = divmod(k - lag, per)
            if isinstance(i, int):
                n = per * i + k - lag
                if n < 0 or n >= total:
                    return None
            return per * i + (k - lag), i + turn, place

        def run_loop(eng, body, turns, tail):
            body(0, False)
            with eng.Fori(1, turns) as i:
                body(i, False)
            if tail:
                body(turns, True)

        STEPJ = 2 * SUBS
        WB = IMAGES * STEPJ
        WT = WB * BANDS
        NTAIL = 8
        LEAD = 10

        def pa_jobs(k):
            jobs = [("A", k + LEAD)]
            if k % 4 == 3:
                jobs.append(("S", (k + 5) // 4))
            if k % 16 == 3:
                jobs.append(("D", (k - 19) // 16))
            if k % 16 == 9:
                jobs.append(("Y", (k - 25) // 16))
            return jobs

        PER = {"A": WB, "S": WB // 4, "D": WB // 16, "Y": WB // 16}
        TOT = {"A": WT, "S": WT // 4, "D": WT // 16, "Y": WT // 16}

        def pa_real(kind, i, n):
            a = PER[kind] * i + n
            return 0 <= a < TOT[kind]

        PAPER = sum(len(pa_jobs(k)) for k in range(WB))
        assert PAPER % 2 == 0
        PRE = LEAD

        pa_table, used, local = {}, {0: 0, 1: 0}, -sum(len(pa_jobs(k)) for k in range(-PRE, 0))
        done = 0
        for q in range(-PRE, WB * (BANDS + 1)):
            for kind, n in pa_jobs(q):
                if pa_real(kind, 0, n):
                    pa_table[q, kind] = (local % 2, done, used[local % 2])
                    done += 1
                    used[local % 2] = done
                local += 1

        def jobs_before_turn(i):
            if isinstance(i, int):
                return sum(q < WB * i for q, _ in pa_table)
            return PAPER * i + (sum(q < WB for q, _ in pa_table) - PAPER)

        def pa_list(i, ks):
            res = []
            for k in ks:
                for kind, n in pa_jobs(k):
                    if not isinstance(i, int):
                        slot, before, last_use = pa_table[WB + k, kind]
                        assert last_use == before - 1
                        res.append((k, kind, n, slot, PAPER * i + (before - PAPER), PAPER * i + (last_use - PAPER)))
                    elif (i * WB + k, kind) in pa_table:
                        res.append((k, kind, n, *pa_table[i * WB + k, kind]))
            return res

        def turn_of(i, n, per):
            d, r = divmod(n, per)
            return i + d, r

        def window_places(i, kind):
            if kind == "head":
                return range(-PRE, 0)
            return range(0, NTAIL + 16) if kind == "tail" else range(0, WB)

        def run_window(eng, body):
            body(0, range(-PRE, WB))
            with eng.Fori(1, BANDS - 1) as i:
                body(i, range(0, WB))
            body(BANDS - 1, range(0, WB))
            body(BANDS, range(0, 28))

        def wjob(i, n, per=WB, total=WT):
            if isinstance(i, int) and not 0 <= per * i + n < total:
                return None
            t, r = turn_of(i, n, per)
            return per * i + n, t, r

        def kband(i, img):
            return (i, img)

        @block.sync
        def _(sp):
            sp.dma_start(X[:, 0, :], x[0]).then_inc(sem("x0_loaded"), 16)
            sp.dma_start(vec[:], vecs).then_inc(sem("loaded"), 16)
            sp.dma_start(W[:], wts).then_inc(sem("loaded"), 16)
            sp.dma_start(X[:, 1, :], x[1]).then_inc(sem("x1_loaded"), 16)
            sp.dma_start(row[:], rows).then_inc(sem("loaded"), 16)
            sp.dma_start(pjrow[:], pjb).then_inc(sem("loaded"), 16)
            sp.dma_start(cst[:], c32).then_inc(sem("loaded"), 16)

            for n, (m, which, at0, cols) in enumerate(pjobs):
                sp.wait_ge(sem("parts_ready"), n + 1)
                dst = (k_dram if which == "k" else q_dram)[:, :, m, at0:at0 + cols]
                sp.dma_start(dst.rearrange("t c n -> c t n"), pk[n % 2][:, :, 0:cols]).then_inc(sem(f"parts_stored{n % 2}"), 16)
            for n, (m, g, k) in enumerate(vjobs):
                sp.wait_ge(sem("v_ready"), n + 1)
                dst = v_flat[m, 496 * g:496 * g + 124 * k, :].rearrange("(t p) v -> p t v", p=124)
                sp.dma_start(dst, vst[n % 2][:, 0:k, :]).then_inc(sem(f"v_stored{n % 2}"), 16)

            sp.wait_ge(sem("c_added"), CT)
            for n in range(2):
                sp.wait_ge(sem(f"parts_stored{n}"), 16 * (NPJ // 2))
                sp.wait_ge(sem(f"v_stored{n}"), 16 * (NVJ // 2))
            sp.dma_start(stage[96:128, :], cmask).then_inc(sem("stage_loaded"), 16)

            def load_band(i, img):
                done = sem(f"band_loaded{img}")
                kb, qb = ds(i * KBAND, KBAND), ds(i * BAND, BAND)
                kd = K[img][:, 0:HEADS * KBAND].rearrange("p (h n) -> p h n", h=HEADS)
                for t, (a, b) in enumerate(TERMS):
                    sp.dma_start(kd[DH * t:DH * (t + 1), :, :], k_dram[b, :, img, kb].rearrange("(h d) n -> d h n", h=HEADS)).then_inc(done, 16)
                    sp.dma_start(Q[img][DH * t:DH * (t + 1), :, :], q_dram[a, :, img, qb].rearrange("(h d) n -> d h n", h=HEADS)).then_inc(done, 16)

            def body(i, ks):
                smax = {k: before for k, kind, n, slot, before, last_use in pa_list(i, range(ks.start, ks.stop)) if kind == "S"}
                for k in ks:
                    if k - 1 in smax or (k % 4 == 0 and k == ks.start):
                        s = wjob(i, (k + 4) // 4, WB // 4, WT // 4)
                        if s is not None:
                            num, t, r = s
                            img, c = divmod(r, TILES)
                            if k - 1 in smax:
                                before = smax[k - 1]
                            else:
                                before = jobs_before_turn(i) - 1
                            sp.wait_ge(sem("w_slot_read"), before + 1)
                            dst = Q[img][SHIFT0:SHIFT0 + 2, :, c * TILE:(c + 1) * TILE]
                            sp.dma_start(dst, nT[r % 2][:]).then_inc(sem(f"w_shift{r % 2}"), 16)
                    if k % 2 == 0:
                        s = wjob(i, k // 2 + 2, WB // 2, WT // 2)
                        if s is not None:
                            num, t, r = s
                            img, c = divmod(r, SUBS)
                            old = wjob(i, k // 2 - 2, WB // 2, WT // 2)
                            if old is not None:
                                sp.wait_ge(sem("w_products"), 2 * old[0] + 2)
                            for h in range(2):
                                c0 = SUBC * c + HCOLS[0] * h
                                src = v_dram[img, ds(t * BLOCK, KROWS), c0:c0 + HCOLS[h], :].rearrange("r c v -> c r v")
                                sp.dma_start(Vw[r % 4][0:HKEYS[h], h, :], src).then_inc(sem(f"w_values{r % 4}"), 16)
                    if k % 16 == 0:
                        nj = wjob(i, k // 16 + 1, 2, 2 * BANDS)
                        if nj is not None:
                            prev = wjob(i, k - 1)
                            if prev is not None:
                                sp.wait_ge(sem("w_scores"), prev[0] + 1)
                            load_band(nj[1], nj[2])

            load_band(0, 0)
            sp.wait_ge(sem("stacks"), 4)
            run_window(sp, body)

            for n in range(IMAGES * BANDS):
                m, b = divmod(n, BANDS)
                sp.wait_ge(sem("z_ready"), n + 1)
                sp.dma_start(out[m, :, b * BAND:(b + 1) * BAND], zo[n % 2][:]).then_inc(sem(f"z_stored{n % 2}"), 16)
            for n in range(2):
                sp.wait_ge(sem(f"z_stored{n}"), 16 * (IMAGES * BANDS // 2))

        @block.gpsimd
        def _(pool):
            g = nc.gpsimd
            g.memset(ones[:], 1.0).then_inc(sem("consts"), 1)
            g.memset(meanw[:], 1.0 / C).then_inc(sem("consts"), 1)
            g.memset(epsc[:], EPS).then_inc(sem("consts"), 1)
            for n in range(2):
                g.memset(vst[n][:], 1.0).then_inc(sem("consts"), 1)
            for m in range(IMAGES):
                pool.wait_ge(sem("conv_done"), m + 1)
                mid = slice(PAD, PAD + SIDE)
                g.tensor_copy(FP[:, m, mid, 0:PAD], bc(FP[:, m, mid, PAD:PAD + 1], [128, SIDE, PAD])).then_inc(sem("sides"), 1)
                g.tensor_copy(FP[:, m, mid, PAD + SIDE:PSIDE], bc(FP[:, m, mid, PAD + SIDE - 1:PAD + SIDE], [128, SIDE, PAD])).then_inc(sem("sides"), 1)
                pool.wait_ge(sem("sides"), 2 * m + 2)
                g.tensor_copy(FP[:, m, 0:PAD, :], bc(FP[:, m, PAD:PAD + 1, :], [128, PAD, PSIDE])).then_inc(sem("padded"), 1)
                g.tensor_copy(FP[:, m, PAD + SIDE:PSIDE, :], bc(FP[:, m, PAD + SIDE - 1:PAD + SIDE, :], [128, PAD, PSIDE])).then_inc(sem("padded"), 1)
            pool.wait_ge(sem("setup_done"), 2)
            for n in range(2):
                pool.wait_ge(sem(f"parts_stored{n}"), 16 * (NPJ // 2))
                pool.wait_ge(sem(f"v_stored{n}"), 16 * (NVJ // 2))
            g.memset(cst35[:], 0.0).then_inc(sem("c_consts0"), 1)
            pool.wait_ge(sem("c_consts0"), 1)
            g.memset(cst35[32:35, :], 1.0).then_inc(sem("c_consts"), 1)
            for n in range(2):
                pool.wait_ge(sem("c_consts"), n + 1)
                g.memset(MV[n][32:35, :], 1.0).then_inc(sem("c_consts"), 1)

            pool.wait_ge(sem("c_added"), CT)
            for m in range(IMAGES):
                g.memset(K[m][:, HEADS * KBAND:], 0.0).then_inc(sem("w_pad"), 1)
            pool.wait_ge(sem("w_pad"), 2)
            g.memset(c1[:, 3:4], 0.0).then_inc(sem("w_zeroed"), 1)

            def w_body(i, ks):
                for k, kind, n, slot, before, last_use in pa_list(i, ks):
                    if kind == "D":
                        num, t, r = wjob(i, n, 2, 2 * BANDS)
                        pool.wait_ge(sem("w_slot_read"), before + 1)
                        if not (isinstance(num, int) and num < 2):
                            pool.wait_ge(sem("w_y"), num - 1)
                        g.tensor_tensor(ON[r][:], OB[r][:], RD[:], ALU.mult).then_inc(sem("w_norm"), 1)

            run_window(pool, w_body)

        @block.tensor
        def _(pe):
            mm = nc.tensor.matmul
            tr = nc.tensor.transpose
            ident = cst[:, CI:CI + 128]

            def bank(b, p=128, n=512, at0=0):
                return PS[0:p, b, at0:at0 + n]

            pe.wait_ge(sem("loaded"), 16 * 5)
            pe.wait_ge(sem("consts"), 5)
            pe.wait_ge(sem("blk_ready"), 1)
            blk2 = blk[:].rearrange("p i n -> p (i n)")
            mm(bank(0, 64, 98), w("s1", 64), blk2, start=True, stop=True).then_inc(sem("p_hid"), 1)
            for m in range(IMAGES):
                last = tr(bank(1, NBLK, C, C * m), blk[:, m, :], ident)
            last.then_inc(sem("p_blkT"), 1)
            pe.wait_ge(sem("hid"), 1)
            mm(bank(0, 1, 98, 128), v(V_S2, 1, 64), hs[:], start=True, stop=True).then_inc(sem("p_score"), 1)
            pe.wait_ge(sem("topf"), 1)
            mm(bank(0, NBLK, 16, 256), ones[0:1, 0:NBLK], topf[:].rearrange("p i n -> p (i n)"), start=True, stop=True).then_inc(sem("p_idx"), 1)
            pe.wait_ge(sem("onehot"), 1)
            pe.wait_ge(sem("blkT"), 1)
            for m in range(IMAGES):
                last = mm(bank(2, C, TOPK, 8 * m), blkT[:, m, :], onehot[:, m, 0:TOPK], start=True, stop=True)
            last.then_inc(sem("p_ksel"), 1)
            pe.wait_ge(sem("rows_ready"), 2)
            for m in range(IMAGES):
                if m:
                    pe.wait_ge(sem("attn_ops"), 4 * m)
                mm(bank(0, C, NBLK), w("wk0"), R[:, m, 0:NBLK], start=True, stop=True)
                mm(bank(0, C, TOPK, 64), w("wk1"), R[:, m, 2 * NBLK:2 * NBLK + TOPK], start=True, stop=True).then_inc(sem("p_keys"), 1)
                for n, name in enumerate(("wv0", "wv1")):
                    mm(bank(1, KC, C, C * n), R[:, m, :], w(name), start=True, stop=False)
                    last = mm(bank(1, KC, C, C * n), ones[0:1, 0:KC], row[0:1, C * n:C * (n + 1)], start=False, stop=True)
                last.then_inc(sem("p_vals"), 1)
                pe.wait_ge(sem("km_ready"), m + 1)
                a4 = bank(2, C, SC).rearrange("p (j k) -> p j k", j=PAIRS)
                b4 = bank(3, 35, SC).rearrange("p (j k) -> p j k", j=PAIRS)
                mm(a4[:, :, 0:2 * NBLK], w("wq0"), KM[:, :, 0:2 * NBLK], start=True, stop=True)
                mm(a4[:, :, 2 * NBLK:KC], w("wq1"), KM[:, :, 2 * NBLK:KC], start=True, stop=True)
                mm(b4[:, :, 0:2 * NBLK], bq35[:, 0, :], KM[:, :, 0:2 * NBLK], start=True, stop=True)
                mm(b4[:, :, 2 * NBLK:KC], bq35[:, 1, :], KM[:, :, 2 * NBLK:KC], start=True, stop=True).then_inc(sem("p_fold"), 1)
            mm(bank(4, 124, C), ones[0:1, 0:124], row[0:1, 2 * C:3 * C], start=True, stop=True)
            mm(bank(4, TILE, 3, 256), n1rep[:], v(V_GW, 3), start=True, stop=False)
            mm(bank(4, TILE, 3, 256), ones[0:1, 0:TILE], row[0:1, R_GB:R_GB + 3], start=False, stop=True).then_inc(sem("p_rows"), 1)

            pe.wait_ge(sem("padded"), 4)
            pe.wait_ge(sem("tile_order"), IMAGES * BANDS)
            for n, (m, which, at0, cols) in enumerate(pjobs):
                if n >= 2:
                    pe.wait_ge(sem("proj_read"), n - 1)
                if which == "k":
                    b, h = divmod(at0 // (KBAND // 2), 2)
                    src = FP[:, m, BLOCK * b:BLOCK * b + KROWS, PSIDE // 2 * h:PSIDE // 2 * (h + 1)].rearrange("p r c -> p c r")
                    dst = bank(5 + n % 2, C, cols).rearrange("p (c r) -> p c r", r=KROWS)
                else:
                    src, dst = xt(m)[:, at0:at0 + cols], bank(5 + n % 2, C, cols)
                mm(dst, w("wk2" if which == "k" else "wq2"), src, start=True, stop=True).then_inc(sem("proj"), 1)
            for n, (m, g, k) in enumerate(vjobs):
                if n >= 1:
                    pe.wait_ge(sem("v_ready"), n)
                for t in range(k):
                    pos = FP[:, m, 8 * g + 2 * t:8 * g + 2 * t + 2, :].rearrange("p r c -> p (r c)")
                    last = mm(bank(7, 124, C, C * t), pos, w("wv2"), start=True, stop=True)
                last.then_inc(sem("vals"), 1)
            for n in range(NGJ + 1):
                if n < NGJ:
                    m, b = gjobs[n]
                    if n >= 1:
                        pe.wait_ge(sem("g_centred"), n)
                    mm(bank(0, C, BAND), meanw[:], xt(m)[:, b * BAND:(b + 1) * BAND], start=True, stop=True).then_inc(sem("g_mean"), 1)
                if n >= 1:
                    q = n - 1
                    pe.wait_ge(sem("g_square"), q + 1)
                    pe.wait_ge(sem("g_centred"), q + 1)
                    if q >= 1:
                        pe.wait_ge(sem("g_logits_read"), q)
                    mm(bank(1, 4, BAND), gl[:, 0, :], xc[q % 2][:], start=True, stop=False)
                    mm(bank(1, 4, BAND), gl[:, 1, :], sq[q % 2][:], start=False, stop=True).then_inc(sem("g_logits"), 1)
                    pe.wait_ge(sem("g_logits_read"), q + 1)
                    if q >= 1:
                        pe.wait_ge(sem("g_stored"), q)
                    for s in range(SUBS):
                        tr(bank(2, TILE, 4, 4 * s), ls2[q % 2][:, s, :, :].rearrange("p a n -> p (a n)"), ident[0:4, 0:4])
                    for s in range(TILES):
                        last = tr(bank(2, TILE, 4, 32 + 4 * s), ls[q % 2][:, s * TILE:(s + 1) * TILE], ident[0:4, 0:4])
                    last.then_inc(sem("g_byquery"), 1)

            pe.wait_ge(sem("split"), 2)
            pe.wait_ge(sem("c_consts"), 3)
            pe.wait_ge(sem("gates"), 1)

            def c_body(i, tail):
                for k in range(CLAG if tail else CB):
                    a = at(i, k, 0, CB, CT)
                    if a:
                        num, t, r = a
                        img, c = divmod(r, TILES)
                        if not (isinstance(num, int) and num < 2):
                            pe.wait_ge(sem("c_maxed"), num - 1)
                        xs = ds(t * BAND + c * TILE, TILE)
                        s = bank(r % 2, TILE, SC)
                        mm(s, XH[:, img, xs], Ah[img][:], start=True, stop=False)
                        mm(s, XL[:, img, xs], Ah[img][:], start=False, stop=False)
                        mm(s, XH[:, img, xs], Al[img][:], start=False, stop=False)
                        mm(s, cst35[:], ES[img][:], start=False, stop=True).then_inc(sem("c_sa"), 1)
                    a = at(i, k, 1, CB, CT)
                    if a:
                        num, t, r = a
                        pe.wait_ge(sem("c_shift"), num + 1)
                        if not (isinstance(num, int) and num < 1):
                            pe.wait_ge(sem("c_shift_used"), num)
                        tr(PS[0:32, 2, 0:TILE // 2].bitcast(BF16), nmb[r % 2][:], identb[:]).then_inc(sem("c_shiftT"), 1)
                    a = at(i, k, 2, CB, CT)
                    if a:
                        num, t, r = a
                        img, c = divmod(r, TILES)
                        pe.wait_ge(sem("c_shift_used"), num + 1)
                        if not (isinstance(num, int) and num < 2):
                            pe.wait_ge(sem("c_exp"), num - 1)
                        for j in range(PAIRS):
                            s = bank(3 + r % 2, KC, TILE, TILE * j)
                            mm(s, Af[img][:, KC * j:KC * (j + 1)], XT[:, img, ds(t * BAND + c * TILE, TILE)], start=True, stop=False)
                            last = mm(s, ES[img][:, KC * j:KC * (j + 1)], MV[r % 2][:], start=False, stop=True)
                        last.then_inc(sem("c_sb"), 1)
                    a = at(i, k, 3, CB, CT)
                    if a:
                        num, t, r = a
                        img = r // TILES
                        pe.wait_ge(sem("c_exp"), num + 1)
                        if not (isinstance(num, int) and num < 1):
                            pe.wait_ge(sem("c_norm"), num)
                        for j in range(PAIRS):
                            last = mm(bank(5, TILE, 68, 68 * j), PC[r % 2][:, TILE * j:TILE * (j + 1)], VB[img][:, j, :], start=True, stop=True)
                        last.then_inc(sem("c_pv"), 1)
                    a = at(i, k, 4, CB, CT)
                    if a:
                        num, t, r = a
                        pe.wait_ge(sem("c_norm"), num + 1)
                        if not (isinstance(num, int) and num < 1):
                            pe.wait_ge(sem("c_ot"), 2 * num)
                        for ty in range(2):
                            tr(bank(6, C, TILE, TILE * ty), oc[r % 2][:, C * ty:C * (ty + 1)], ident[0:TILE, 0:TILE])
                        tr(bank(6, 3, TILE, 2 * TILE), oc[r % 2][:, 256:259], ident[0:TILE, 0:TILE]).then_inc(sem("c_tr"), 1)
                    a = at(i, k, 5, CB, CT)
                    if a:
                        num, t, r = a
                        pe.wait_ge(sem("c_ot"), 2 * num + 2)
                        if not (isinstance(num, int) and num < 1):
                            pe.wait_ge(sem("c_added"), num)
                        y = bank(7, C, TILE)
                        mm(y, w("pj0"), ot[r % 2][:, 0:TILE], start=True, stop=False)
                        mm(y, w("pj1"), ot[r % 2][:, TILE:2 * TILE], start=False, stop=False)
                        mm(y, pjrow[:], ot[r % 2][0:3, 2 * TILE:3 * TILE], start=False, stop=True)
                        mm(bank(7, C, TILE, TILE), cst[0:3, CG:CG + C], ot[r % 2][0:3, 2 * TILE:3 * TILE], start=True, stop=True).then_inc(sem("c_y"), 1)

            run_loop(pe, c_body, BANDS, True)

            pe.wait_ge(sem("c_added"), CT)
            pe.wait_ge(sem("stacks"), 4)
            pe.wait_ge(sem("w_zeroed"), 3)

            def pslot(s, p=128):
                return PS[0:p, 2 * s:2 * s + 2, :]

            def w_body(i, ks):
                lst = pa_list(i, ks)
                for k in ks:
                    mine = [e for e in lst if e[0] == k]

                    def slot_free(last_use):
                        if not (isinstance(last_use, int) and last_use < 1):
                            pe.wait_ge(sem("w_slot_read"), last_use)

                    for _, kind, n, slot, before, last_use in mine:
                        if kind == "A":
                            num, t, r = wjob(i, n)
                            img, q = divmod(r, STEPJ)
                            c, hp = divmod(q, 4)
                            if q == 0:
                                pe.wait_ge(sem(f"band_loaded{img}"), (t + 1) * (16 * 2 * len(TERMS)))
                            slot_free(last_use)
                            for e in range(2):
                                h = 2 * hp + e
                                last = mm(pslot(slot, TILE)[:, e, 0:KROWS * TCOLS], Q[img][0:SHIFT0, h, c * TILE:(c + 1) * TILE],
                                          K[img][0:SHIFT0, h * KBAND + 14 * c * KROWS:h * KBAND + (14 * c + TCOLS) * KROWS], start=True, stop=True)
                            last.then_inc(sem("w_slot"), 1)
                        if kind == "S":
                            num, t, r = wjob(i, n, WB // 4, WT // 4)
                            pe.wait_ge(sem("w_split"), num + 1)
                            slot_free(last_use)
                            dst = PS[0:2 * HEADS, 2 * slot, 0:TILE // 2].bitcast(BF16)
                            tr(dst, wnb[r % 2][:].rearrange("p a h -> p (a h)"), identb[:]).then_inc(sem("w_slot"), 1)
                    jb = wjob(i, k)
                    if jb:
                        num, t, r = jb
                        img, q = divmod(r, STEPJ)
                        c, h2 = divmod(q, 2)
                        if q % 4 == 0:
                            tl = (num // 4) if isinstance(num, int) else (t * (WB // 4) + r // 4)
                            par = (r // 4) % 2
                            pe.wait_ge(sem(f"w_shift{par}"), (t * (WB // 8) + (r // 8) + 1) * 16)
                        if not (isinstance(num, int) and num < 2):
                            pe.wait_ge(sem("w_exp"), num - 1)
                        for h in range(HEADS):
                            first = h * KBAND + (SUBC * c + HCOLS[0] * h2) * KROWS
                            last = mm(PS[:, 4 + r % 2, h * SUB:(h + 1) * SUB], K[img][:, first:first + 128],
                                      Q[img][:, h, c * SUB:(c + 1) * SUB], start=True, stop=True)
                        last.then_inc(sem("w_scores"), 1)
                    jb = wjob(i, k - 2)
                    if jb:
                        num, t, r = jb
                        s = r // 2
                        pe.wait_ge(sem("w_exp"), num + 1)
                        if r % 2 == 0:
                            pe.wait_ge(sem(f"w_values{s % 4}"), (t * (WB // 8) + s // 4 + 1) * 32)
                            if not (isinstance(num, int) and num < 4):
                                pe.wait_ge(sem("w_out"), t * (WB // 2) + s - 1)
                        for h in range(HEADS):
                            u, b = divmod(h, 4)
                            last = mm(PS[QUAD * b:QUAD * b + VH, 6 + s % 2, u * SUB:(u + 1) * SUB], Vw[s % 4][0:HKEYS[r % 2], r % 2, VH * h:VH * (h + 1)],
                                      P[r % 4][0:HKEYS[r % 2], SUB * h:SUB * (h + 1)], start=(r % 2 == 0 and u == 0),
                                      stop=(r % 2 == 1), skip_group_check=True)
                        last.then_inc(sem("w_products"), 1)
                    for _, kind, n, slot, before, last_use in mine:
                        if kind == "D":
                            num, t, r = wjob(i, n, 2, 2 * BANDS)
                            pe.wait_ge(sem("w_out"), SUBS * num + SUBS)
                            slot_free(last_use)
                            for u in range(2):
                                last = mm(PS[:, 2 * slot + u, 0:BAND], cst[:, CD:CD + C], OB[r][:, u, :], start=True, stop=True)
                            last.then_inc(sem("w_slot"), 1)
                        if kind == "Y":
                            num, t, r = wjob(i, n, 2, 2 * BANDS)
                            pe.wait_ge(sem("w_norm"), num + 1)
                            slot_free(last_use)
                            for u in range(2):
                                last = mm(PS[:, 2 * slot, 0:BAND], w("pj2", C, C * u), ON[r][:, u, :], start=(u == 0), stop=(u == 1))
                            last.then_inc(sem("w_slot"), 1)

            run_window(pe, w_body)

            job = 0
            pe.wait_ge(sem("w_y"), 2 * BANDS)
            for m in range(IMAGES):
                for pair in range(2):
                    for half in range(2):
                        q = 4 * m + 2 * pair + half
                        grp = pair + 2 * half
                        for b in range(BANDS):
                            if job >= 2:
                                pe.wait_ge(sem("t_read"), job - 1)
                            mm(bank(job % 2, C, BAND), w("pin", C, C * grp), X[:, m, b * BAND:(b + 1) * BAND], start=True, stop=True).then_inc(sem("t_proj"), 1)
                            job += 1
                pe.wait_ge(sem("hidden"), 2 * m + 2)
                for b in range(BANDS):
                    n = m * BANDS + b
                    if n >= 2:
                        pe.wait_ge(sem("z_sum"), n - 1)
                    for g2 in range(2):
                        last = mm(bank(2 + n % 2, C, BAND), w("pout", C, C * g2), U[g2][:, b * BAND:(b + 1) * BAND], start=(g2 == 0), stop=(g2 == 1))
                    last.then_inc(sem("z_proj"), 1)
            for n in range(IMAGES * BANDS + 1):
                if n < IMAGES * BANDS:
                    m, b = divmod(n, BANDS)
                    pe.wait_ge(sem("z_sum"), n + 1)
                    if n >= 2:
                        pe.wait_ge(sem("z_centred"), n - 1)
                    mm(bank(4 + n % 2, C, BAND), meanw[:], X[:, m, b * BAND:(b + 1) * BAND], start=True, stop=True).then_inc(sem("z_mean"), 1)
                if n >= 1:
                    q = n - 1
                    pe.wait_ge(sem("z_square"), q + 1)
                    if q >= 2:
                        pe.wait_ge(sem("z_std"), q - 1)
                    mm(bank(6 + q % 2, C, BAND), meanw[:], zq[q % 2][:], start=True, stop=True).then_inc(sem("z_var"), 1)

        @block.scalar
        def _(act):
            a = nc.scalar.activation
            act.wait_ge(sem("loaded"), 16 * 5)
            act.wait_ge(sem("p_hid"), 1)
            a(hs[:], PS[0:64, 0, 0:98], ACT.Gelu, bias=v(V_S1B, 1, 64)).then_inc(sem("hid"), 1)
            a(identb[:], cst[0:TILE, CI:CI + TILE], ACT.Copy).then_inc(sem("identb"), 1)
            for m in range(IMAGES):
                act.wait_ge(sem("conv_done"), m + 1)
                for b in range(BANDS):
                    src = FP[:, m, PAD + BLOCK * b:PAD + BLOCK * (b + 1), PAD:PAD + SIDE].rearrange("p r (s c) -> p s r c", c=SUBC)
                    dst = XT[:, m, b * BAND:(b + 1) * BAND].rearrange("p (s r c) -> p s r c", s=SUBS, c=SUBC)
                    a(dst, src, ACT.Copy).then_inc(sem("tile_order"), 1)
            for m in range(IMAGES):
                act.wait_ge(sem("tile_order"), BANDS * (m + 1))
                a(XH[:, m, :], xt(m), ACT.Copy).then_inc(sem("high"), 1)
            for n, (m, which, at0, cols) in enumerate(pjobs):
                act.wait_ge(sem("proj"), n + 1)
                if n >= 2:
                    act.wait_ge(sem("parts_ready"), n - 1)
                    act.wait_ge(sem(f"parts_stored{n % 2}"), 16 * (n // 2))
                ps = PS[:, 5 + n % 2, 0:cols]
                if n == 0:
                    act.wait_ge(sem("c1"), 3)
                bias = v(V_BK + 2) if which == "k" else c1[:, 2:3]
                sc = 1.0 if which == "k" else SCALE
                a(pf[n % 2][:, 0:cols], ps, ACT.Identity, bias=bias, scale=sc).then_inc(sem("proj_full"), 1)
                a(pk[n % 2][:, 0, 0:cols], ps, ACT.Identity, bias=bias, scale=sc).then_inc(sem("proj_read"), 1)
            for n in range(NGJ):
                act.wait_ge(sem("g_centred"), n + 1)
                if n >= 2:
                    act.wait_ge(sem("g_logits"), n - 1)
                a(sq[n % 2][:], xc[n % 2][:], ACT.Square).then_inc(sem("g_square"), 1)
            act.wait_ge(sem("g_stored"), NGJ)
            g4 = G[:].rearrange("p i b s k -> p (i b s) k")
            a(gst[:], g4[:, :, 3], ACT.Sqrt, bias=epsc[0:TILE, :]).then_inc(sem("g_std"), 1)
            act.wait_ge(sem("g_shifted"), 1)
            a(g4[:, :, 0:3], g4[:, :, 0:3], ACT.Exp).then_inc(sem("g_exp"), 1)

            def c_body(i, tail):
                for k in range(CLAG if tail else CB):
                    s = at(i, k, 2, CB, CT)
                    if s:
                        num, t, r = s
                        act.wait_ge(sem("c_sb"), num + 1)
                        if not (isinstance(num, int) and num < 2):
                            act.wait_ge(sem("c_pv"), num - 1)
                        a(PC[r % 2][:], PS[0:KC, 3 + r % 2, 0:PAIRS * TILE], ACT.Exp).then_inc(sem("c_exp"), 1)
                    s = at(i, k, 4, CB, CT)
                    if s:
                        num, t, r = s
                        act.wait_ge(sem("c_tr"), num + 1)
                        if not (isinstance(num, int) and num < 2):
                            act.wait_ge(sem("c_y"), num - 1)
                        a(ot[r % 2][:, 0:2 * TILE], PS[:, 6, 0:2 * TILE], ACT.Copy).then_inc(sem("c_ot"), 1)
                        a(ot[r % 2][0:3, 2 * TILE:3 * TILE], PS[0:3, 6, 2 * TILE:3 * TILE], ACT.Copy).then_inc(sem("c_ot"), 1)

            act.wait_ge(sem("setup_done"), 2)
            run_loop(act, c_body, BANDS, True)

            act.wait_ge(sem("c_added"), CT)
            act.wait_ge(sem("stage_loaded"), 16)
            for m in range(IMAGES):
                kd = K[m][MASK0:128, 0:HEADS * KBAND].rearrange("p (h n) -> p h n", h=HEADS)
                a(kd, bc(stage[MASK0:128, 0:KBAND].unsqueeze(1), [32, HEADS, KBAND]), ACT.Copy).then_inc(sem("stacks"), 1)
                a(Q[m][MASK0:128, :, :], bc(stage[MASK0:128, KBAND:KBAND + BAND].unsqueeze(1), [32, HEADS, BAND]), ACT.Copy).then_inc(sem("stacks"), 1)

            def w_body(i, ks):
                for k in ks:
                    jb = wjob(i, k)
                    if jb:
                        num, t, r = jb
                        act.wait_ge(sem("w_scores"), num + 1)
                        if not (isinstance(num, int) and num < 4):
                            act.wait_ge(sem("w_products"), num - 3)
                        kn = HKEYS[r % 2]
                        a(P[r % 4][0:kn, :], PS[0:kn, 4 + r % 2, 0:HEADS * SUB], ACT.Exp).then_inc(sem("w_exp"), 1)
                    if k % 2 == 0:
                        s = wjob(i, k // 2 - 2, WB // 2, WT // 2)
                        if s:
                            num, t, r = s
                            img, c = divmod(r, SUBS)
                            act.wait_ge(sem("w_products"), 2 * num + 2)
                            if c == 0 and not (isinstance(num, int) and num < WB // 2):
                                act.wait_ge(sem("w_norm"), 2 * t + img - 1)
                            src = PS[:, 6 + r % 2, 0:2 * SUB].rearrange("p (u n) -> p u n", u=2)
                            a(OB[img][:, :, c * SUB:(c + 1) * SUB], src, ACT.Copy).then_inc(sem("w_out"), 1)

            run_window(act, w_body)

            job = 0
            act.wait_ge(sem("w_y"), 2 * BANDS)
            for m in range(IMAGES):
                for pair in range(2):
                    for half in range(2):
                        q = 4 * m + 2 * pair + half
                        grp = pair + 2 * half
                        if q >= 2:
                            act.wait_ge(sem("conv2"), q - 1)
                            act.wait_ge(sem("hidden"), q // 2 if half == 0 else (q - 1) // 2)
                        for b in range(BANDS):
                            act.wait_ge(sem("t_proj"), job + 1)
                            cols = slice(b * BAND, (b + 1) * BAND)
                            a(T[q % 2][:, cols], PS[:, job % 2, 0:BAND], ACT.Copy).then_inc(sem("t_full"), 1)
                            a(AC[q % 2][:, cols], PS[:, job % 2, 0:BAND], ACT.Copy, scale=v(V_DW + 9 * grp + 4)).then_inc(sem("t_read"), 1)
                            job += 1
                        if half == 1:
                            act.wait_ge(sem("conv2"), q)
                            a(AC[0][:], AC[0][:], ACT.Gelu).then_inc(sem("gelu"), 1)
            for n in range(IMAGES * BANDS + 1):
                if n < IMAGES * BANDS:
                    act.wait_ge(sem("z_centred"), n + 1)
                    if n >= 2:
                        act.wait_ge(sem("z_var"), n - 1)
                    a(zq[n % 2][:], zc[n % 2][:], ACT.Square).then_inc(sem("z_square"), 1)
                if n >= 1:
                    q = n - 1
                    act.wait_ge(sem("z_var"), q + 1)
                    if q >= 2:
                        act.wait_ge(sem("z_rstd"), q - 1)
                    a(sd[q % 2][:], PS[:, 6 + q % 2, 0:BAND], ACT.Sqrt, bias=epsc[:]).then_inc(sem("z_std"), 1)

        @block.vector
        def _(dve):
            ve = nc.vector
            chain = [0]

            def link(ins):
                chain[0] += 1
                ins.then_inc(sem("v_chain"), 1)
                dve.wait_ge(sem("v_chain"), chain[0])

            dve.wait_ge(sem("loaded"), 16 * 5)
            ve.tensor_scalar(c1[:, 0:1], v(V_POSW + 4), 1.0, None, ALU.add).then_inc(sem("c1"), 1)
            ve.memset(gl[:], 0.0).then_inc(sem("c1"), 1)
            ve.tensor_scalar(c1[:, 2:3], v(V_BQ + 2), SCALE, None, ALU.mult).then_inc(sem("c1"), 1)
            dve.wait_ge(sem("c1"), 3)

            def conv(src, dst, wcol, first):
                for t in SIDE_TAPS:
                    dy, dx = TAPS[t]
                    ro, rn = max(0, -dy), SIDE - abs(dy)
                    co, cn = max(0, -dx), SIDE - abs(dx)
                    o = dst(ro, rn, co, cn)
                    link(ve.scalar_tensor_tensor(out=o, in0=src(ro + dy, rn, co + dx, cn), scalar=v(wcol + t), in1=o, op0=ALU.mult, op1=ALU.add))

            for m in range(IMAGES):
                dve.wait_ge(sem(f"x{m}_loaded"), 16)
                xi = X[:, m, :].rearrange("p (r c) -> p r c", c=SIDE)
                inner = FP[:, m, PAD:PAD + SIDE, PAD:PAD + SIDE]
                link(ve.tensor_scalar(inner, xi, c1[:, 0:1], v(V_POSB), ALU.mult, ALU.add))
                conv(lambda r, rn, c, cn: xi[:, r:r + rn, c:c + cn], lambda r, rn, c, cn: inner[:, r:r + rn, c:c + cn], V_POSW, m)
                ve.tensor_reduce(bs1[:, m, :, :], inner.rearrange("p r (b c) -> p r b c", c=BLOCK), AX.X, ALU.add).then_inc(sem("conv_done"), 1)
            for m in range(IMAGES):
                dve.wait_ge(sem("conv_done"), m + 1)
                src = bs1[:, m, :, :].rearrange("p (y r) b -> p y b r", r=BLOCK)
                link(ve.tensor_reduce(blk[:, m, :].rearrange("p (y b) -> p y b", b=NBS), src, AX.X, ALU.add))
            ve.tensor_scalar(blk[:], blk[:], 1.0 / BLOCK ** 2, None, ALU.mult).then_inc(sem("blk_ready"), 1)
            dve.wait_ge(sem("p_blkT"), 1)
            ve.tensor_copy(blkT[:], PS[0:NBLK, 1, 0:2 * C].rearrange("p (i c) -> p i c", i=IMAGES)).then_inc(sem("blkT"), 1)
            dve.wait_ge(sem("p_score"), 1)
            link(ve.tensor_scalar(score[:], PS[0:1, 0, 128:128 + 98].rearrange("p (i n) -> p i n", i=IMAGES), row[0:1, R_S2B:R_S2B + 1], None, ALU.add))
            for m in range(IMAGES):
                link(ve.max(top[:, m, :], score[:, m, :]))
            for m in range(IMAGES):
                link(ve.max_index(topi[:, m, :], top[:, m, :], score[:, m, :]))
            ve.tensor_copy(topf[:], topi[:]).then_inc(sem("topf"), 1)
            dve.wait_ge(sem("p_idx"), 1)
            ve.tensor_scalar(onehot[:], PS[0:NBLK, 0, 256:272].rearrange("p (i n) -> p i n", i=IMAGES), cst[0:NBLK, CIO:CIO + 1], None, ALU.is_equal).then_inc(sem("onehot"), 1)
            ve.tensor_scalar(gl[:, 0, 0:3], v(V_GW, 3), v(V_N1W), None, ALU.mult).then_inc(sem("c1"), 1)
            ve.memset(gl[:, 1, 3:4], 1.0 / C).then_inc(sem("c1"), 1)
            link(ve.tensor_copy(n1rep[:], bc(v(V_N1B), [128, TILE])))
            for n in range(2):
                link(ve.tensor_copy(bq35[:, n, :], bc(v(V_BQ + n), [128, 35])))
            r4 = R[:, :, 0:2 * NBLK].rearrange("p i (e n) -> p i e n", e=2)
            for e in range(2):
                link(ve.tensor_copy(r4[:, :, e, :], blk[:]))
            dve.wait_ge(sem("p_ksel"), 1)
            for e in range(2):
                ve.tensor_copy(R[:, :, 2 * NBLK + TOPK * e:2 * NBLK + TOPK * (e + 1)],
                               PS[:, 2, 0:16].rearrange("p (i n) -> p i n", i=IMAGES)[:, :, 0:TOPK]).then_inc(sem("rows_ready"), 1)
            for m in range(IMAGES):
                dve.wait_ge(sem("p_keys"), m + 1)
                link(ve.tensor_scalar(k0[:], PS[:, 0, 0:NBLK], v(V_BK), SCALE, ALU.add, ALU.mult))
                link(ve.tensor_scalar(k1[:], PS[:, 0, 64:64 + TOPK], v(V_BK + 1), SCALE, ALU.add, ALU.mult))
                hm = cst[:, CH:CH + HEADS].rearrange("p (j e) -> p j e", e=2)
                for e in range(2):
                    for kk, o, n in ((k0, NBLK * e, NBLK), (k1, 2 * NBLK + TOPK * e, TOPK)):
                        last = ve.tensor_tensor(KM[:, :, o:o + n], bc(kk[:].unsqueeze(1), [128, PAIRS, n]), bc(hm[:, :, e:e + 1], [128, PAIRS, n]), ALU.mult)
                        if (e, n) != (1, TOPK):
                            link(last)
                last.then_inc(sem("km_ready"), 1)
                dve.wait_ge(sem("p_vals"), m + 1)
                for n in range(2):
                    vf = PS[0:KC, 1, C * n:C * (n + 1)].rearrange("p (j d) -> p j d", j=PAIRS)
                    vm = cst[0:KC, CVM + 32 * n:CVM + 32 * (n + 1)]
                    ve.tensor_tensor(VB[m][:, :, 32 * n:32 * (n + 1)], vf, bc(vm.unsqueeze(1), [KC, PAIRS, 32]), ALU.mult).then_inc(sem("attn_ops"), 1)
                ve.tensor_copy(VB[m][:, :, 64:68], bc(cst[0:KC, CVM + 64:CVM + 68].unsqueeze(1), [KC, PAIRS, 4])).then_inc(sem("attn_ops"), 1)
                dve.wait_ge(sem("p_fold"), m + 1)
                link(ve.tensor_copy(Af[m][:], PS[:, 2, 0:SC]))
                link(ve.tensor_copy(Ah[m][:], Af[m][:]))
                link(ve.tensor_tensor(Al[m][:], Af[m][:], Ah[m][:], ALU.subtract))
                link(ve.tensor_copy(cs[:], PS[0:35, 3, 0:SC]))
                prev = cst[0:35, CE:CE + SC]
                for part in range(3):
                    link(ve.tensor_copy(chb[:], cs[:]))
                    dst = ES[m] if part == 2 else ch[part]
                    link(ve.scalar_tensor_tensor(out=dst[:], in0=chb[:], scalar=cst[0:35, CM + part:CM + part + 1], in1=prev, op0=ALU.mult, op1=ALU.add))
                    prev = ch[part][:]
                    if part < 2:
                        link(ve.tensor_tensor(cs[:], cs[:], chb[:], ALU.subtract))
                ve.memset(c1[:, 4 + m:5 + m], 0.0).then_inc(sem("attn_ops"), 1)
            dve.wait_ge(sem("p_rows"), 1)
            link(ve.tensor_copy(BV2[:], PS[0:124, 4, 0:C]))
            link(ve.tensor_copy(cg[:], PS[0:TILE, 4, 256:259]))
            for m in range(IMAGES):
                dve.wait_ge(sem("high"), m + 1)
                ve.tensor_tensor(XL[:, m, :], xt(m), XH[:, m, :], ALU.subtract).then_inc(sem("split"), 1)
            for n, (m, which, at0, cols) in enumerate(pjobs):
                dve.wait_ge(sem("proj_read"), n + 1)
                dve.wait_ge(sem("proj_full"), n + 1)
                if n >= 1:
                    dve.wait_ge(sem("parts_ready"), n)
                p, f = pk[n % 2], pf[n % 2]
                link(ve.tensor_tensor(pr[:, 0:cols], f[:, 0:cols], p[:, 0, 0:cols], ALU.subtract))
                link(ve.tensor_copy(p[:, 1, 0:cols], pr[:, 0:cols]))
                ve.tensor_tensor(p[:, 2, 0:cols], pr[:, 0:cols], p[:, 1, 0:cols], ALU.subtract).then_inc(sem("parts_ready"), 1)
            for n, (m, g, k) in enumerate(vjobs):
                dve.wait_ge(sem("vals"), n + 1)
                if n >= 2:
                    dve.wait_ge(sem(f"v_stored{n % 2}"), 16 * (n // 2))
                o = vst[n % 2][:, 0:k, :].rearrange("p t (j d) -> p (t j) d", d=VH)[:, :, 0:DH]
                i0 = PS[0:124, 7, 0:C * k].rearrange("p (t d) -> p t d", d=DH)
                for t in range(k):
                    last = ve.tensor_tensor(o[:, HEADS * t:HEADS * (t + 1), :], i0[:, HEADS * t:HEADS * (t + 1), :],
                                            BV2[:].rearrange("p (j d) -> p j d", j=HEADS), ALU.add)
                last.then_inc(sem("v_ready"), 1)
            for n in range(NGJ):
                m, b = gjobs[n]
                dve.wait_ge(sem("g_mean"), n + 1)
                if n >= 2:
                    dve.wait_ge(sem("g_logits"), n - 1)
                ve.tensor_tensor(xc[n % 2][:], xt(m)[:, b * BAND:(b + 1) * BAND], PS[:, 0, 0:BAND], ALU.subtract).then_inc(sem("g_centred"), 1)
                dve.wait_ge(sem("g_logits"), n + 1)
                ve.tensor_copy(ls[n % 2][:], PS[0:4, 1, 0:BAND])
                ve.tensor_copy(ls2[n % 2][:], bc(PS[0:4, 1, 0:BAND].rearrange("p (s n) -> p s n", n=SUB).unsqueeze(2), [4, SUBS, 2, SUB])).then_inc(sem("g_logits_read"), 1)
                dve.wait_ge(sem("g_byquery"), n + 1)
                ve.tensor_copy(G[:, m, b, :, :], PS[0:TILE, 2, 0:48].rearrange("p (s k) -> p s k", k=4)).then_inc(sem("g_stored"), 1)
            g4 = G[:].rearrange("p i b s k -> p (i b s) k")
            g3 = g4[:, :, 0:3]
            dve.wait_ge(sem("g_stored"), NGJ)
            dve.wait_ge(sem("g_std"), 1)
            link(ve.reciprocal(gst[:], gst[:]))
            link(ve.tensor_tensor(g3, g3, bc(gst[:].unsqueeze(2), [TILE, NG, 3]), ALU.mult))
            link(ve.tensor_tensor(g3, g3, bc(cg[:].unsqueeze(1), [TILE, NG, 3]), ALU.add))
            link(ve.tensor_reduce(gmx[:], g3, AX.X, ALU.max))
            ve.tensor_tensor(g3, g3, bc(gmx[:].unsqueeze(2), [TILE, NG, 3]), ALU.subtract).then_inc(sem("g_shifted"), 1)
            dve.wait_ge(sem("g_exp"), 1)
            link(ve.tensor_reduce(gst[:], g3, AX.X, ALU.add))
            link(ve.reciprocal(gmx[:], gst[:]))
            link(ve.tensor_tensor(g3, g3, bc(gmx[:].unsqueeze(2), [TILE, NG, 3]), ALU.mult))
            ve.memset(c1[:, 6:7], 0.0).then_inc(sem("gates"), 1)
            ve.memset(c1[:, 7:8], 0.0).then_inc(sem("setup_done"), 2)

            def c_body(i, tail):
                for k in range(CLAG if tail else CB):
                    s = at(i, k, 0, CB, CT)
                    if s:
                        num, t, r = s
                        dve.wait_ge(sem("c_sa"), num + 1)
                        if not (isinstance(num, int) and num < 1):
                            dve.wait_ge(sem("c_shift"), num)
                        s4 = PS[0:TILE, r % 2, 0:SC].rearrange("p (j k) -> p j k", j=PAIRS)
                        o = nm[:].rearrange("p (t j e) -> p t j e", t=2, e=2)
                        ve.tensor_reduce(o[:, 0, :, :], s4[:, :, 0:2 * NBLK].rearrange("p j (e n) -> p j e n", e=2), AX.X, ALU.max, negate=True).then_inc(sem("c_max1"), 1)
                        ve.tensor_reduce(o[:, 1, :, :], s4[:, :, 2 * NBLK:KC].rearrange("p j (e n) -> p j e n", e=2), AX.X, ALU.max, negate=True).then_inc(sem("c_maxed"), 1)
                        dve.wait_ge(sem("c_maxed"), num + 1)
                        dve.wait_ge(sem("c_max1"), num + 1)
                        if not (isinstance(num, int) and num < 2):
                            dve.wait_ge(sem("c_shiftT"), num - 1)
                        ve.tensor_copy(nmb[r % 2][:, 0:16], nm[:]).then_inc(sem("c_high"), 1)
                        dve.wait_ge(sem("c_high"), num + 1)
                        ve.tensor_tensor(nmb[r % 2][:, 16:32], nm[:], nmb[r % 2][:, 0:16], ALU.subtract).then_inc(sem("c_shift"), 1)
                    s = at(i, k, 1, CB, CT)
                    if s:
                        num, t, r = s
                        dve.wait_ge(sem("c_shiftT"), num + 1)
                        if not (isinstance(num, int) and num < 2):
                            dve.wait_ge(sem("c_sb"), num - 1)
                        ve.tensor_copy(MV[r % 2][0:32, :], PS[0:32, 2, 0:TILE // 2].bitcast(BF16)).then_inc(sem("c_shift_used"), 1)
                    s = at(i, k, 3, CB, CT)
                    if s:
                        num, t, r = s
                        img, c = divmod(r, TILES)
                        dve.wait_ge(sem("c_pv"), num + 1)
                        if not (isinstance(num, int) and num < 1):
                            dve.wait_ge(sem("c_norm"), num)
                        if not (isinstance(num, int) and num < 2):
                            dve.wait_ge(sem("c_tr"), num - 1)
                        pv = PS[0:TILE, 5, 0:68 * PAIRS].rearrange("p (j k) -> p j k", j=PAIRS)
                        gg = G[:, img, ds(t, 1), 8 + c, 0:2] if not isinstance(t, int) else G[:, img, t:t + 1, 8 + c, 0:2]
                        ve.reciprocal(rd[:].rearrange("p a j e -> p j a e"), pv[:, :, 64:68].rearrange("p j (a e) -> p j a e", e=2)).then_inc(sem("c_recip"), 1)
                        dve.wait_ge(sem("c_recip"), num + 1)
                        for ty in range(2):
                            ve.tensor_scalar(rg[:, ty, :, :], rd[:, ty, :, :], gg[:, 0, ty:ty + 1], None, ALU.mult).then_inc(sem("c_gated"), 1)
                        dve.wait_ge(sem("c_gated"), 2 * num + 2)
                        ve.tensor_scalar(oc[r % 2][:, 256:259], G[:, img, ds(t, 1), 8 + c, 0:3].rearrange("p a k -> p (a k)") if not isinstance(t, int) else G[:, img, t, 8 + c, 0:3], 1.0, None, ALU.mult).then_inc(sem("c_gcol"), 1)
                        dve.wait_ge(sem("c_gcol"), num + 1)
                        for ty in range(2):
                            o = oc[r % 2][:, C * ty:C * (ty + 1)].rearrange("p (j e d) -> p j e d", e=2, d=DH)
                            last = ve.tensor_tensor(o, pv[:, :, 32 * ty:32 * (ty + 1)].rearrange("p j (e d) -> p j e d", e=2),
                                                    bc(rg[:, ty, :, :].unsqueeze(3), [TILE, PAIRS, 2, DH]), ALU.mult)
                        last.then_inc(sem("c_norm"), 1)
                    s = at(i, k, 5, CB, CT)
                    if s:
                        num, t, r = s
                        img, c = divmod(r, TILES)
                        dve.wait_ge(sem("c_y"), num + 1)
                        xs = XT[:, img, ds(t * BAND + c * TILE, TILE)]
                        ve.tensor_copy(GB[:, img, ds(t * BAND + c * TILE, TILE)], PS[:, 7, TILE:2 * TILE])
                        ve.tensor_tensor(xs, PS[:, 7, 0:TILE], xs, ALU.add).then_inc(sem("c_added"), 1)

            run_loop(dve, c_body, BANDS, True)

            dve.wait_ge(sem("c_added"), CT)
            for b in (6, 7):
                ve.memset(PS[:, b, 0:2 * SUB], 0.0).then_inc(sem("w_zeroed"), 1)

            def w_body(i, ks):
                lst = pa_list(i, ks)
                for k in ks:
                    mine = [e for e in lst if e[0] == k]

                    def paj(kinds):
                        for _, kind, n, slot, before, last_use in mine:
                            if kind not in kinds:
                                continue
                            dve.wait_ge(sem("w_slot"), before + 1)
                            if kind == "A":
                                num, t, r = wjob(i, n)
                                tl, hp = divmod(r, 4)
                                if hp == 0 and not (isinstance(num, int) and num < 8):
                                    dve.wait_ge(sem("w_split"), t * (WB // 4) + tl - 1)
                                src = PS[0:TILE, 2 * slot:2 * slot + 2, 0:KROWS * TCOLS]
                                ve.tensor_reduce(wn[tl % 2][:, 2 * hp:2 * hp + 2], src, AX.X, ALU.max, negate=True).then_inc(sem("w_slot_read"), 1)
                                if hp == 3:
                                    dve.wait_ge(sem("w_slot_read"), before + 1)
                                    if not (isinstance(num, int) and num < 8):
                                        dve.wait_ge(sem("w_slot"), before - 5)
                                    ve.tensor_copy(wnb[tl % 2][:, 0, :], wn[tl % 2][:]).then_inc(sem("w_high"), 1)
                                    dve.wait_ge(sem("w_high"), t * (WB // 4) + tl + 1)
                                    ve.tensor_tensor(wnb[tl % 2][:, 1, :], wn[tl % 2][:], wnb[tl % 2][:, 0, :], ALU.subtract).then_inc(sem("w_split"), 1)
                            if kind == "S":
                                num, t, r = wjob(i, n, WB // 4, WT // 4)
                                if not (isinstance(num, int) and num < 2):
                                    dve.wait_ge(sem(f"w_shift{r % 2}"), (t * (WB // 8) + r // 2) * 16)
                                src = PS[0:2 * HEADS, 2 * slot, 0:TILE // 2].bitcast(BF16)
                                ve.tensor_copy(nT[r % 2][:], src).then_inc(sem("w_slot_read"), 1)
                            if kind == "D":
                                num, t, r = wjob(i, n, 2, 2 * BANDS)
                                if not (isinstance(num, int) and num < 1):
                                    dve.wait_ge(sem("w_norm"), num)
                                ve.reciprocal(RD[:], PS[:, 2 * slot:2 * slot + 2, 0:BAND]).then_inc(sem("w_slot_read"), 1)
                            if kind == "Y":
                                num, t, r = wjob(i, n, 2, 2 * BANDS)
                                if not (isinstance(num, int) and num < 1):
                                    dve.wait_ge(sem("w_y"), num)
                                ve.tensor_tensor(yt[:], PS[:, 2 * slot, 0:BAND], GB[:, r, ds(t * BAND, BAND)], ALU.mult).then_inc(sem("w_slot_read"), 1)
                                o = X[:, r, ds(t * BAND, BAND)].rearrange("p (r s c) -> p s r c", s=SUBS, c=SUBC)
                                xs = XT[:, r, ds(t * BAND, BAND)].rearrange("p (s r c) -> p s r c", s=SUBS, c=SUBC)
                                dve.wait_ge(sem("w_slot_read"), before + 1)
                                ve.tensor_tensor(o, yt[:].rearrange("p (s r c) -> p s r c", s=SUBS, c=SUBC), xs, ALU.add).then_inc(sem("w_y"), 1)

                    paj("ASDY")

            run_window(dve, w_body)

            cq = chain
            for m in range(IMAGES):
                for pair in range(2):
                    for half in range(2):
                        q = 4 * m + 2 * pair + half
                        grp = pair + 2 * half
                        dve.wait_ge(sem("t_read"), BANDS * (q + 1))
                        dve.wait_ge(sem("t_full"), BANDS * (q + 1))
                        ti = T[q % 2][:].rearrange("p (r c) -> p r c", c=SIDE)
                        ai = AC[q % 2][:].rearrange("p (r c) -> p r c", c=SIDE)
                        conv(lambda r, rn, c, cn: ti[:, r:r + rn, c:c + cn], lambda r, rn, c, cn: ai[:, r:r + rn, c:c + cn], V_DW + 9 * grp, m)
                        ve.memset(c1[0:1, 0:1], 0.0).then_inc(sem("conv2"), 1)
                    dve.wait_ge(sem("gelu"), 2 * m + pair + 1)
                    if m and pair == 0:
                        dve.wait_ge(sem("z_proj"), BANDS * m)
                    ve.tensor_tensor(U[pair][:], AC[0][:], AC[1][:], ALU.mult).then_inc(sem("hidden"), 1)
                for b in range(BANDS):
                    n = m * BANDS + b
                    dve.wait_ge(sem("z_proj"), n + 1)
                    xs = X[:, m, b * BAND:(b + 1) * BAND]
                    ve.tensor_tensor(xs, PS[:, 2 + n % 2, 0:BAND], xs, ALU.add).then_inc(sem("z_sum"), 1)
            for n in range(IMAGES * BANDS + 1):
                if n < IMAGES * BANDS:
                    m, b = divmod(n, BANDS)
                    dve.wait_ge(sem("z_mean"), n + 1)
                    if n >= 2:
                        dve.wait_ge(sem("z_scaled"), n - 1)
                    ve.tensor_tensor(zc[n % 2][:], X[:, m, b * BAND:(b + 1) * BAND], PS[:, 4 + n % 2, 0:BAND], ALU.subtract).then_inc(sem("z_centred"), 1)
                if n >= 1:
                    q = n - 1
                    dve.wait_ge(sem("z_std"), q + 1)
                    ve.reciprocal(sd[q % 2][:], sd[q % 2][:]).then_inc(sem("z_rstd"), 1)
                    dve.wait_ge(sem("z_rstd"), q + 1)
                    if q >= 2:
                        dve.wait_ge(sem(f"z_stored{q % 2}"), 16 * (q // 2))
                    ve.tensor_tensor(sd[q % 2][:], zc[q % 2][:], sd[q % 2][:], ALU.mult).then_inc(sem("z_scaled"), 1)
                    dve.wait_ge(sem("z_scaled"), q + 1)
                    ve.tensor_scalar(zo[q % 2][:], sd[q % 2][:], v(V_N2W), v(V_N2B), ALU.mult, ALU.add).then_inc(sem("z_ready"), 1)


_OUT = (IMAGES, C, SIDE, SIDE)


def kernel(**inputs):
    import concourse.bacc as _bacc
    from concourse.bass_utils import run_bass_kernel_spmd as _run

    a = {n.replace("L0_conv_", ""): np.ascontiguousarray(t) for n, t in inputs.items()}
    pj2 = np.zeros((4, QUAD, 2, C), np.float32)
    pj2[:, 0:DH] = a["pj_w"][2].T.reshape(2, 4, DH, C).transpose(1, 2, 0, 3)
    wts = np.concatenate(
        [a["wq_w"][0], a["wq_w"][1], a["wq_w"][2].T, a["wk_w"][0].T, a["wk_w"][1].T, a["wk_w"][2].T,
         a["wv_w"][0].T, a["wv_w"][1].T, a["wv_w"][2].T, a["pj_w"][0].T, a["pj_w"][1].T,
         a["s1_w"].T, a["pin_w"].T, a["pout_w"].T[0:C], a["pout_w"].T[C:], pj2.reshape(C, 2 * C)], 1)
    vecs = np.zeros((128, NV), np.float32)
    vecs[:, V_POSW:V_POSW + 9] = a["pos_w"].reshape(C, 9)
    for col, name in ((V_POSB, "pos_b"), (V_N1W, "n1_w"), (V_N1B, "n1_b"), (V_N2W, "n2_w"), (V_N2B, "n2_b")):
        vecs[:, col] = a[name]
    vecs[:, V_BQ:V_BQ + 3] = a["wq_b"].T
    vecs[:, V_BK:V_BK + 3] = a["wk_b"].T
    for g in range(4):
        vecs[:, V_DW + 9 * g:V_DW + 9 * (g + 1)] = a["dw_w"].reshape(9, 2 * HID)[:, C * g:C * (g + 1)].T
    vecs[0:64, V_S1B] = a["s1_b"]
    vecs[0:64, V_S2] = a["s2_w"][0]
    vecs[:, V_GW:V_GW + 3] = a["g_w"].T
    rows = np.concatenate([a["wv_b"].reshape(-1), a["g_b"], a["s2_b"]])[None]
    c32, cmask = shape_constants()
    arrays = {"x": a["x"].reshape(IMAGES, C, PIX), "wts": wts, "vecs": vecs, "rows": rows, "pjb": a["pj_b"], "c32": c32, "cmask": cmask}
    nc = _bacc.Bacc("TRN2", target_bir_lowering=False, num_devices=1)
    args = {n: nc.dram_tensor(f"in_{n}", t.shape, mybir.dt.from_np(t.dtype), kind="ExternalInput").ap() for n, t in arrays.items()}
    out = nc.dram_tensor("out_y", (IMAGES, C, PIX), F32, kind="ExternalOutput").ap()
    build(nc, out=out, **args)
    r = _run(nc, [{f"in_{n}": np.ascontiguousarray(t) for n, t in arrays.items()}], core_ids=[0])
    return r.results[0]["out_y"].reshape(_OUT)
```

```python
from contextlib import ExitStack

import numpy as np

import concourse.bass as bass
from concourse import mybir

F32 = mybir.dt.float32
BF16 = mybir.dt.bfloat16
U32 = mybir.dt.uint32
ALU = mybir.AluOpType
ACT = mybir.ActivationFunctionType
AX = mybir.AxisListType
ds = bass.ds

C = 128
IMAGES = 2
SIDE = 56
PIX = SIDE * SIDE
HEADS, DH = 8, 16
BLOCK = 8
NBS = SIDE // BLOCK
NBLK = NBS * NBS
TOPK = 4
WIN = 7
PAD = WIN // 2
PSIDE = SIDE + 2 * PAD
PPIX = PSIDE * PSIDE
BANDS = SIDE // BLOCK
BAND = BLOCK * SIDE
SUBC = 7
SUB = BLOCK * SUBC
SUBS = SIDE // SUBC
TILE = 2 * SUB
TILES = SUBS // 2
KROWS = BLOCK + WIN - 1
KCOLS = SUBC + WIN - 1
HCOLS = (7, KCOLS - 7)
HKEYS = [n * KROWS for n in HCOLS]
KEYS = max(HKEYS)
KBAND = KROWS * PSIDE
TCOLS = 2 * SUBC + WIN - 1
PAIRS = HEADS // 2
VH = DH + 1
VROW = HEADS * VH
QUAD = 32
KC = 2 * NBLK + 2 * TOPK
SC = PAIRS * KC
SLOT = (1, 0, 2)
TERMS = ((0, 1), (0, 0), (1, 1), (1, 0), (2, 0), (0, 2))
MASK0 = len(TERMS) * DH
SHIFT0 = 126
HID = 2 * C
RING = 4
URING = 9
SCALE = float(DH) ** -0.5
EPS = 1e-6
BIG = 2.0 ** 99

WNAMES = ("wq0", "wq1", "wq2", "wk0", "wk1", "wk2", "wv0", "wv1", "wv2", "pj0", "pj1")
WCOL = {n: C * k for k, n in enumerate(WNAMES)}
WCOL["s1"] = C * len(WNAMES)
WCOL["pin"] = WCOL["s1"] + C // 2
WCOL["pout"] = WCOL["pin"] + 2 * HID
WCOL["pj2"] = WCOL["pout"] + HID
NW = WCOL["pj2"] + 2 * C
V_POSW, V_POSB, V_N1W, V_N1B, V_N2W, V_N2B, V_BQ, V_BK, V_DW, V_S1B, V_S2, V_GW = 0, 9, 10, 11, 12, 13, 14, 17, 20, 56, 57, 58
NV = 61
R_BV, R_GB, R_S2B, NR = 0, 3 * C, 3 * C + 3, 3 * C + 4
CI, CH, CVM, CIO, CM, CD, CG, CE = 0, 128, 136, 204, 205, 208, 336, 464
NC32 = CE + SC
TAPS = [(dy, dx) for dy in (-1, 0, 1) for dx in (-1, 0, 1)]
SIDE_TAPS = [t for t in range(9) if t != 4]


def shape_constants():
    c = np.zeros((128, NC32), np.float32)
    c[:, CI:CI + 128] = np.eye(128)
    c[:, CH:CH + HEADS] = np.arange(128)[:, None] // DH == np.arange(HEADS)
    for e in range(2):
        for rows, o in ((slice(e * NBLK, (e + 1) * NBLK), 0), (slice(2 * NBLK + e * TOPK, 2 * NBLK + (e + 1) * TOPK), 1)):
            c[rows, CVM + o * 32 + e * DH:CVM + o * 32 + (e + 1) * DH] = 1
            c[rows, CVM + 64 + 2 * o + e] = 1
            for j in range(PAIRS):
                for part in range(2):
                    c[16 * part + 8 * o + 2 * j + e, CE + j * KC + rows.start:CE + j * KC + rows.stop] = 1
    c[:, CIO] = np.arange(128)
    for b in range(4):
        c[b, CD + QUAD * b:CD + QUAD * (b + 1)] = 1
    c[2, CG:CG + 128] = 1
    for part in range(3):
        c[32 + part, CM + part] = 1
    ck = np.zeros((32, PSIDE, KROWS), np.float32)
    cq = np.zeros((32, SUBS, BLOCK, SUBC), np.float32)
    X, x = np.arange(PSIDE).reshape(-1, 1), np.arange(SIDE).reshape(SUBS, 1, SUBC)
    r = np.arange(BLOCK).reshape(1, BLOCK, 1)
    for j in range(14):
        ck[j, :, j] = 1
        cq[j] = np.where((j >= r) & (j < r + WIN), 0, -BIG)
        ck[14 + j] = X % 14 == j
        cq[14 + j] = np.where((j - x) % 14 < WIN, 0, -BIG)
    ck[28] = X % 28 < 6
    ck[29] = (X % 28 >= 14) & (X % 28 < 20)
    tile, rel = x // 14, x % 14
    cq[28] = np.where(tile % 2 == 0, np.where(rel >= 6, -BIG, 0), np.where(rel <= 7, -BIG, 0))
    cq[29] = np.where(tile % 2 == 1, np.where(rel >= 6, -BIG, 0), np.where(rel <= 7, -BIG, 0))
    ck[30:] = 1
    return c, np.concatenate([ck.reshape(32, -1), cq.reshape(32, -1)], 1)


def bc(ap, shape):
    return ap.broadcast_to(shape)


def build(nc, x, wts, vecs, rows, pjb, dwr, c32, cmask, out):
    ctx = ExitStack()
    with ctx:
        def sb(name, shape, dt=F32, stack=ctx):
            return stack.enter_context(nc.sbuf_tensor(name, shape, dt))

        sems = {}

        def sem(name):
            if name not in sems:
                sems[name] = ctx.enter_context(nc.semaphore(name))
            return sems[name]

        q_dram = nc.dram_tensor("q_parts", [3, C, IMAGES, PIX], BF16, kind="Internal").ap()
        k_dram = nc.dram_tensor("k_parts", [3, C, IMAGES, BANDS * KBAND], BF16, kind="Internal").ap()
        v_dram = nc.dram_tensor("v_rows", [IMAGES, PSIDE, PSIDE, VROW], F32, kind="Internal").ap()
        v_flat = v_dram.rearrange("i r c v -> i (r c) v")

        PS = ctx.enter_context(nc.psum_tensor("banks", [128, 8, 512], F32))

        W = sb("W", [128, NW])
        vec = sb("vec", [128, NV])
        row = sb("row", [1, NR])
        pjrow = sb("pjrow", [3, C])
        cst = sb("cst", [128, NC32])
        identb = sb("identb", [TILE, TILE], BF16)
        ones = sb("ones", [128, 128])
        meanw = sb("meanw", [128, 128])
        epsc = sb("epsc", [128, 1])
        X = sb("X", [128, IMAGES, PIX])
        G = sb("G", [TILE, IMAGES, BANDS, 12, 4])

        c1 = sb("c1", [128, 8])

        att = ctx.enter_context(ExitStack())
        FP = sb("FP", [128, IMAGES, PSIDE, PSIDE], F32, att)
        XT = sb("XT", [128, IMAGES, PIX], F32, att)
        GB = FP[:].rearrange("p i r c -> p (i r c)")[:, 0:IMAGES * PIX].rearrange("p (i n) -> p i n", i=IMAGES)
        early = ctx.enter_context(ExitStack())
        XH = sb("XH", [128, IMAGES, PIX], BF16, early)
        XL = sb("XL", [128, IMAGES, PIX], BF16, early)
        bs1 = sb("bs1", [128, IMAGES, SIDE, NBS], F32, early)
        Af = [sb(f"Af{m}", [128, SC], F32, early) for m in range(IMAGES)]
        Ah = [sb(f"Ah{m}", [128, SC], BF16, early) for m in range(IMAGES)]
        Al = [sb(f"Al{m}", [128, SC], BF16, early) for m in range(IMAGES)]
        ES = [sb(f"ES{m}", [35, SC], BF16, early) for m in range(IMAGES)]
        VB = [sb(f"VB{m}", [KC, PAIRS, 68], F32, early) for m in range(IMAGES)]
        BV2 = sb("BV2", [124, C], F32, early)

        def xt(img):
            return XT[:, img, :]

        with ExitStack() as s1:
            blk = sb("blk", [128, IMAGES, NBLK], F32, s1)
            hs = sb("hs", [64, IMAGES * NBLK], F32, s1)
            score = sb("score", [1, IMAGES, NBLK], F32, s1)
            top = sb("top", [1, IMAGES, 8], F32, s1)
            topi = sb("topi", [1, IMAGES, 8], U32, s1)
            topf = sb("topf", [1, IMAGES, 8], F32, s1)
            onehot = sb("onehot", [NBLK, IMAGES, 8], F32, s1)
            blkT = sb("blkT", [NBLK, IMAGES, C], F32, s1)
            R = sb("R", [128, IMAGES, KC], F32, s1)
            k0 = sb("k0", [128, NBLK], F32, s1)
            k1 = sb("k1", [128, TOPK], F32, s1)
            KM = sb("KM", [128, PAIRS, KC], F32, s1)
            bq35 = sb("bq35", [128, 2, 35], F32, s1)
            cs = sb("cs", [35, SC], F32, s1)
            ch = [sb(f"ch{n}", [35, SC], F32, s1) for n in range(3)]
            chb = sb("chb", [35, SC], BF16, s1)
            pk = [sb(f"pk{n}", [128, 3, BAND], BF16, s1) for n in range(RING)]
            pf = [sb(f"pf{n}", [128, BAND], F32, s1) for n in range(RING)]
            pr = [sb(f"pr{n}", [128, BAND], F32, s1) for n in range(3)]
            diag = sb("diag", [128, 9, C], F32, s1)
            vst = [sb(f"vst{n}", [124, 4, VROW], F32, s1) for n in range(2)]
            gl = sb("gl", [128, 2, 4], F32, s1)
            n1rep = sb("n1rep", [128, TILE], F32, s1)
            cg = sb("cg", [TILE, 3], F32, s1)
            xc = [sb(f"xc{n}", [128, BAND], F32, s1) for n in range(2)]
            sq = [sb(f"sq{n}", [128, BAND], F32, s1) for n in range(2)]
            ls = [sb(f"ls{n}", [4, BAND], F32, s1) for n in range(2)]
            ls2 = [sb(f"ls2{n}", [4, SUBS, 2, SUB], F32, s1) for n in range(2)]
            NG = IMAGES * BANDS * 12
            gst = sb("gst", [TILE, NG], F32, s1)
            gmx = sb("gmx", [TILE, NG], F32, s1)
        with ExitStack() as s2:
            nm = sb("nm", [TILE, 16], F32, s2)
            nmb = [sb(f"nmb{n}", [TILE, 32], BF16, s2) for n in range(2)]
            cst35 = sb("cst35", [35, TILE], BF16, s2)
            MV = [sb(f"MV{n}", [35, TILE], BF16, s2) for n in range(2)]
            PC = [sb(f"PC{n}", [KC, PAIRS * TILE], F32, s2) for n in range(2)]
            rd = sb("rd", [TILE, 2, PAIRS, 2], F32, s2)
            rg = sb("rg", [TILE, 2, PAIRS, 2], F32, s2)
            oc = [sb(f"oc{n}", [TILE, 260], F32, s2) for n in range(2)]
            ot = [sb(f"ot{n}", [128, 3 * TILE], F32, s2) for n in range(2)]
        early.close()
        with ExitStack() as s3:
            K = [sb(f"K{m}", [128, HEADS * KBAND + 64], BF16, s3) for m in range(IMAGES)]
            Q = [sb(f"Q{m}", [128, HEADS, BAND], BF16, s3) for m in range(IMAGES)]
            Vw = [sb(f"Vw{n}", [KEYS, 2, VROW], F32, s3) for n in range(4)]
            P = [sb(f"P{n}", [KEYS, HEADS * SUB], F32, s3) for n in range(4)]
            wn = [sb(f"wn{n}", [TILE, HEADS], F32, s3) for n in range(2)]
            wnb = [sb(f"wnb{n}", [TILE, 2, HEADS], BF16, s3) for n in range(2)]
            nT = [sb(f"nT{n}", [2 * HEADS, TILE], BF16, s3) for n in range(2)]
            OB = [sb(f"OB{n}", [128, 2, BAND], F32, s3) for n in range(2)]
            SR = [sb(f"SR{n}", [HEADS * SUBS, SUB], F32, s3) for n in range(2)]
            RB = [sb(f"RB{n}", [4, 2, BAND], F32, s3) for n in range(2)]
            ON = [sb(f"ON{n}", [128, 2, BAND], F32, s3) for n in range(2)]
            yt = sb("yt", [128, BAND], F32, s3)
            stage = sb("stage", [128, KBAND + BAND], F32, s3)
        att.close()
        with ExitStack() as s4:
            T = [sb(f"T{n}", [128, PIX], F32, s4) for n in range(2)]
            AC = [sb(f"AC{n}", [128, PIX], F32, s4) for n in range(3)]
            U = [sb(f"U{n}", [128, URING, BAND], F32, s4) for n in range(2)]
            YP = sb("YP", [128, IMAGES, SIDE + 2, SIDE + 2], F32, s4)
            WT = sb("WT", [128, 9, HID], F32, s4)
            zc = [sb(f"zc{n}", [128, BAND], F32, s4) for n in range(2)]
            zq = [sb(f"zq{n}", [128, BAND], F32, s4) for n in range(2)]
            sd = [sb(f"sd{n}", [128, BAND], F32, s4) for n in range(2)]
            zo = [sb(f"zo{n}", [128, BAND], F32, s4) for n in range(2)]

        def w(name, n=C, off=0):
            return W[:, WCOL[name] + off:WCOL[name] + off + n]

        def v(col, n=1, p=128):
            return vec[0:p, col:col + n]

        block = ctx.enter_context(nc.Block())

        pjobs = [(m, "k", h * KBAND // 2, KBAND // 2) for m in range(IMAGES) for h in range(2 * BANDS)]
        pjobs += [(m, "q", b * BAND, BAND) for m in range(IMAGES) for b in range(BANDS)]
        NPJ = len(pjobs)
        vjobs = [(m, g, min(4, 31 - 4 * g)) for m in range(IMAGES) for g in range(8)]
        NVJ = len(vjobs)
        gjobs = [(m, b) for m in range(IMAGES) for b in range(BANDS)]
        NGJ = len(gjobs)
        assert NPJ == 3 * NGJ
        VPLACES = sorted([3 * k + 1 for k in range(NGJ)] + [2, 5])
        assert len(VPLACES) == NVJ
        PEB = 5
        PBANKS = (5, 6, 3)

        CT = IMAGES * BANDS * TILES
        CB = IMAGES * TILES
        CLAG = 5

        def at(i, k, lag, per, total):
            turn, place = divmod(k - lag, per)
            if isinstance(i, int):
                n = per * i + k - lag
                if n < 0 or n >= total:
                    return None
            return per * i + (k - lag), i + turn, place

        def run_loop(eng, body, turns, tail):
            body(0, False)
            with eng.Fori(1, turns) as i:
                body(i, False)
            if tail:
                body(turns, True)

        STEPJ = 2 * SUBS
        WB = IMAGES * STEPJ
        WTOT = WB * BANDS
        LEAD = 8
        LOAD_PLACES = (0, 1, 3)

        def pa_jobs(k):
            jobs = [("A", k + LEAD)]
            if k % 4 == 1:
                jobs.append(("S", (k + 3) // 4))
            if k % 16 == 10:
                jobs.append(("D", (k - 26) // 16))
            if k % 16 == 15:
                jobs.append(("Y", (k - 31) // 16))
            return jobs

        PER = {"A": WB, "S": WB // 4, "D": WB // 16, "Y": WB // 16}
        TOT = {"A": WTOT, "S": WTOT // 4, "D": WTOT // 16, "Y": WTOT // 16}

        def pa_real(kind, i, n):
            a = PER[kind] * i + n
            return 0 <= a < TOT[kind]

        PAPER = sum(len(pa_jobs(k)) for k in range(WB))
        assert PAPER % 2 == 0
        PRE = LEAD

        pa_table, used, local = {}, {0: 0, 1: 0}, -sum(len(pa_jobs(k)) for k in range(-PRE, 0))
        done = 0
        for q in range(-PRE, WB * (BANDS + 1)):
            for kind, n in pa_jobs(q):
                if pa_real(kind, 0, n):
                    pa_table[q, kind] = (local % 2, done, used[local % 2])
                    done += 1
                    used[local % 2] = done
                local += 1

        def pa_list(i, ks):
            res = []
            for k in ks:
                for kind, n in pa_jobs(k):
                    if not isinstance(i, int):
                        slot, before, last_use = pa_table[WB + k, kind]
                        assert last_use == before - 1
                        res.append((k, kind, n, slot, PAPER * i + (before - PAPER), PAPER * i + (last_use - PAPER)))
                    elif (i * WB + k, kind) in pa_table:
                        res.append((k, kind, n, *pa_table[i * WB + k, kind]))
            return res

        def turn_of(i, n, per):
            d, r = divmod(n, per)
            return i + d, r

        def run_window(eng, body):
            body(0, range(-PRE, WB))
            with eng.Fori(1, BANDS - 1) as i:
                body(i, range(0, WB))
            body(BANDS - 1, range(0, WB))
            body(BANDS, range(0, 28))

        ZB = IMAGES * BANDS
        UNITS = 2 * ZB
        PINS = {0: [(0, 0), (0, 1)], 5: [(1, 0)], 14: [(1, 1)]}
        ACID = {(0, 0): 0, (0, 1): 1, (1, 0): 2, (1, 1): 0}
        ZSTEP = {15 + z: z for z in range(UNITS - 15)}
        ZLAST = UNITS - 15
        ZSTEPS = ZB + 3
        GELUS = {8: 0, 21: 1}

        def wjob(i, n, per=WB, total=WTOT):
            if isinstance(i, int) and not 0 <= per * i + n < total:
                return None
            t, r = turn_of(i, n, per)
            return per * i + n, t, r

        @block.sync
        def _(sp):
            sp.dma_start(vec[:], vecs).then_inc(sem("vec_loaded"), 16)
            sp.dma_start(X[:, 0, :], x[0]).then_inc(sem("x0_loaded"), 16)
            sp.dma_start(cst[:], c32).then_inc(sem("cst_loaded"), 16)
            sp.dma_start(X[:, 1, :], x[1]).then_inc(sem("x1_loaded"), 16)
            sp.dma_start(W[:], wts).then_inc(sem("loaded"), 16)
            sp.dma_start(row[:], rows).then_inc(sem("loaded"), 16)
            sp.dma_start(pjrow[:], pjb).then_inc(sem("loaded"), 16)

            for n, (m, which, at0, cols) in enumerate(pjobs):
                if n in VPLACES:
                    j = VPLACES.index(n)
                    vm, g, k = vjobs[j]
                    sp.wait_ge(sem("v_ready"), j + 1)
                    dst = v_flat[vm, 496 * g:496 * g + 124 * k, :].rearrange("(t p) v -> p t v", p=124)
                    sp.dma_start(dst, vst[j % 2][:, 0:k, :]).then_inc(sem(f"v_stored{j % 2}"), 16)
                sp.wait_ge(sem("parts_ready"), n + 1)
                dst = (k_dram if which == "k" else q_dram)[:, :, m, at0:at0 + cols]
                sp.dma_start(dst.rearrange("t c n -> c t n"), pk[n % RING][:, :, 0:cols]).then_inc(sem(f"parts_stored{n % RING}"), 16)

            sp.wait_ge(sem("c_added"), CT)
            for n in range(RING):
                sp.wait_ge(sem(f"parts_stored{n}"), 16 * len(range(n, NPJ, RING)))
            for n in range(2):
                sp.wait_ge(sem(f"v_stored{n}"), 16 * (NVJ // 2))
            sp.dma_start(stage[96:128, :], cmask).then_inc(sem("stage_loaded"), 16)

            def load_band(i, img, pairs=range(len(TERMS) // 2)):
                done = sem(f"band_loaded{img}")
                kb, qb = ds(i * KBAND, KBAND), ds(i * BAND, BAND)
                kd = K[img][:, 0:HEADS * KBAND].rearrange("p (h n) -> p h n", h=HEADS)
                for t, (a, b) in enumerate(TERMS):
                    if t // 2 not in pairs:
                        continue
                    if t % 2 == 0:
                        src = k_dram[SLOT[b]:SLOT[b] + 2, :, img, kb].rearrange("t (d h) n -> (t d) h n", h=HEADS)
                        sp.dma_start(kd[DH * t:DH * (t + 2), :, :], src).then_inc(done, 16)
                    sp.dma_start(Q[img][DH * t:DH * (t + 1), :, :], q_dram[SLOT[a], :, img, qb].rearrange("(d h) n -> d h n", h=HEADS)).then_inc(done, 16)

            def body(i, ks):
                smax = {k: before for k, kind, n, slot, before, last_use in pa_list(i, range(ks.start, ks.stop)) if kind == "S"}
                for k in ks:
                    if k - 1 in smax:
                        s = wjob(i, (k + 2) // 4, WB // 4, WTOT // 4)
                        if s is not None:
                            num, t, r = s
                            img, c = divmod(r, TILES)
                            if isinstance(num, int) and num == TILES:
                                sp.wait_ge(sem("stacks1"), 2)
                            sp.wait_ge(sem("w_slot_read"), smax[k - 1] + 1)
                            dst = Q[img][SHIFT0:SHIFT0 + 2, :, c * TILE:(c + 1) * TILE]
                            sp.dma_start(dst, nT[r % 2][:]).then_inc(sem(f"w_shift{r % 2}"), 16)
                    if k % 2 == 0:
                        s = wjob(i, k // 2 + 2, WB // 2, WTOT // 2)
                        if s is not None:
                            num, t, r = s
                            img, c = divmod(r, SUBS)
                            old = wjob(i, k // 2 - 2, WB // 2, WTOT // 2)
                            if old is not None:
                                sp.wait_ge(sem("w_products"), 2 * old[0] + 2)
                            for h in range(2):
                                c0 = SUBC * c + HCOLS[0] * h
                                src = v_dram[img, ds(t * BLOCK, KROWS), c0:c0 + HCOLS[h], :].rearrange("r c v -> c r v")
                                sp.dma_start(Vw[r % 4][0:HKEYS[h], h, :], src).then_inc(sem(f"w_values{r % 4}"), 16)
                    if k % 16 == 3:
                        s = wjob(i, (k - 19) // 16, 2, 2 * BANDS)
                        if s is not None:
                            num, t, r = s
                            sp.wait_ge(sem("w_out"), SUBS * num + SUBS)
                            sp.dma_start(SR[r][:], OB[r][DH:128:QUAD, :, :]).then_inc(sem(f"w_sums{r}"), 16)
                    if k % 16 == 7:
                        s = wjob(i, (k - 23) // 16, 2, 2 * BANDS)
                        if s is not None:
                            num, t, r = s
                            sp.wait_ge(sem("w_recip"), num + 1)
                            sp.dma_start(RB[r][:], SR[r][:]).then_inc(sem(f"w_recips{r}"), 16)
                    if k % 16 in LOAD_PLACES:
                        nj = wjob(i, k // 16 + 1, 2, 2 * BANDS)
                        if nj is not None:
                            prev = wjob(i, k // 16 * 16 - 1)
                            if prev is not None:
                                sp.wait_ge(sem("w_scores"), prev[0] + 1)
                            load_band(nj[1], nj[2], [LOAD_PLACES.index(k % 16)])

            load_band(0, 0)
            sp.wait_ge(sem("stacks0"), 2)
            run_window(sp, body)

            sp.wait_ge(sem("w_y"), 2 * BANDS)
            sp.dma_start(WT[:].rearrange("p t o -> p (t o)"), bc(dwr, [128, 9 * HID])).then_inc(sem("taps_loaded"), 16)
            for n in range(IMAGES * BANDS):
                m, b = divmod(n, BANDS)
                sp.wait_ge(sem("z_ready"), n + 1)
                sp.dma_start(out[m, :, b * BAND:(b + 1) * BAND], zo[n % 2][:]).then_inc(sem(f"z_stored{n % 2}"), 16)
            for n in range(2):
                sp.wait_ge(sem(f"z_stored{n}"), 16 * (IMAGES * BANDS // 2))

        @block.gpsimd
        def _(pool):
            g = nc.gpsimd
            g.memset(ones[:], 1.0).then_inc(sem("consts"), 1)
            g.memset(meanw[:], 1.0 / C).then_inc(sem("consts"), 1)
            g.memset(epsc[:], EPS).then_inc(sem("consts"), 1)
            for n in range(2):
                g.memset(vst[n][:], 1.0).then_inc(sem("consts"), 1)
            for m in range(IMAGES):
                if m == 0:
                    pool.wait_ge(sem("conv_done"), 1)
                else:
                    pool.wait_ge(sem("pos_read"), PEB)
                    pool.wait_ge(sem("conv_last"), 1)
                mid = slice(PAD, PAD + SIDE)
                g.tensor_copy(FP[:, m, mid, 0:PAD], bc(FP[:, m, mid, PAD:PAD + 1], [128, SIDE, PAD])).then_inc(sem("sides"), 1)
                g.tensor_copy(FP[:, m, mid, PAD + SIDE:PSIDE], bc(FP[:, m, mid, PAD + SIDE - 1:PAD + SIDE], [128, SIDE, PAD])).then_inc(sem("sides"), 1)
                pool.wait_ge(sem("sides"), 2 * m + 2)
                g.tensor_copy(FP[:, m, 0:PAD, :], bc(FP[:, m, PAD:PAD + 1, :], [128, PAD, PSIDE])).then_inc(sem("padded"), 1)
                g.tensor_copy(FP[:, m, PAD + SIDE:PSIDE, :], bc(FP[:, m, PAD + SIDE - 1:PAD + SIDE, :], [128, PAD, PSIDE])).then_inc(sem("padded"), 1)
            for n, (m, which, at0, cols) in enumerate(pjobs):
                pool.wait_ge(sem("second_part"), n + 1)
                p = pk[n % RING]
                g.tensor_tensor(p[:, SLOT[2], 0:cols], pr[n % 3][:, 0:cols], p[:, SLOT[1], 0:cols], ALU.subtract).then_inc(sem("parts_ready"), 1)
                if n % 3 == 2:
                    gm, b = gjobs[n // 3]
                    pool.wait_ge(sem("high"), gm + 1)
                    cols = slice(b * BAND, (b + 1) * BAND)
                    g.tensor_tensor(XL[:, gm, cols], XT[:, gm, cols], XH[:, gm, cols], ALU.subtract).then_inc(sem("split"), 1)
            pool.wait_ge(sem("setup_done"), 2)
            for n in range(RING):
                pool.wait_ge(sem(f"parts_stored{n}"), 16 * len(range(n, NPJ, RING)))
            for n in range(2):
                pool.wait_ge(sem(f"v_stored{n}"), 16 * (NVJ // 2))
            g.memset(cst35[:], 0.0).then_inc(sem("c_consts0"), 1)
            pool.wait_ge(sem("c_consts0"), 1)
            g.memset(cst35[32:35, :], 1.0).then_inc(sem("c_consts"), 1)
            for n in range(2):
                pool.wait_ge(sem("c_consts"), n + 1)
                g.memset(MV[n][32:35, :], 1.0).then_inc(sem("c_consts"), 1)

            pool.wait_ge(sem("c_added"), CT)
            for m in range(IMAGES):
                g.memset(K[m][:, HEADS * KBAND:], 0.0).then_inc(sem("w_pad"), 1)
            pool.wait_ge(sem("w_pad"), 2)
            g.memset(c1[:, 3:4], 0.0).then_inc(sem("w_zeroed"), 1)

            pool.wait_ge(sem("w_y"), 2 * BANDS)
            g.memset(YP[:, :, 0:SIDE + 2:SIDE + 1, :], 0.0).then_inc(sem("y_border"), 1)
            g.memset(YP[:, :, 1:SIDE + 1, 0:SIDE + 2:SIDE + 1], 0.0).then_inc(sem("y_border"), 1)
            for b in range(BANDS):
                xs = X[:, 1, b * BAND:(b + 1) * BAND].rearrange("p (r c) -> p r c", c=SIDE)
                g.tensor_copy(YP[:, 1, 1 + BLOCK * b:1 + BLOCK * (b + 1), 1:1 + SIDE], xs).then_inc(sem("y1_padded"), 1)

        @block.tensor
        def _(pe):
            mm = nc.tensor.matmul
            tr = nc.tensor.transpose
            ident = cst[:, CI:CI + 128]

            def bank(b, p=128, n=512, at0=0):
                return PS[0:p, b, at0:at0 + n]

            pe.wait_ge(sem("x1_loaded"), 16)
            pe.wait_ge(sem("diag"), 9)
            x1r = X[:, 1, :].rearrange("p (r c) -> p r c", c=SIDE)
            for b in range(PEB):
                if b >= 2:
                    pe.wait_ge(sem("pos_read"), b - 1)
                dst = bank(3 + b % 2, C, BAND).rearrange("p (r c) -> p r c", c=SIDE)
                for t in [4] + SIDE_TAPS:
                    dy, dx = TAPS[t]
                    lo, hi = max(BLOCK * b, -dy), min(BLOCK * (b + 1), SIDE - dy)
                    co, cn = max(0, -dx), SIDE - abs(dx)
                    last = mm(dst[:, lo - BLOCK * b:hi - BLOCK * b, co:co + cn], diag[:, t, :], x1r[:, lo + dy:hi + dy, co + dx:co + dx + cn],
                              start=(t == 4), stop=(t == SIDE_TAPS[-1]), skip_group_check=True)
                last.then_inc(sem("pos_conv"), 1)
            pe.wait_ge(sem("loaded"), 16 * 3)
            pe.wait_ge(sem("consts"), 5)
            pe.wait_ge(sem("blk_ready"), 1)
            blk2 = blk[:].rearrange("p i n -> p (i n)")
            mm(bank(0, 64, 98), w("s1", 64), blk2, start=True, stop=True).then_inc(sem("p_hid"), 1)
            for m in range(IMAGES):
                last = tr(bank(1, NBLK, C, C * m), blk[:, m, :], ident)
            last.then_inc(sem("p_blkT"), 1)
            pe.wait_ge(sem("hid"), 1)
            mm(bank(0, 1, 98, 128), v(V_S2, 1, 64), hs[:], start=True, stop=True).then_inc(sem("p_score"), 1)
            pe.wait_ge(sem("topf"), 1)
            mm(bank(0, NBLK, 16, 256), ones[0:1, 0:NBLK], topf[:].rearrange("p i n -> p (i n)"), start=True, stop=True).then_inc(sem("p_idx"), 1)
            pe.wait_ge(sem("onehot"), 1)
            pe.wait_ge(sem("blkT"), 1)
            for m in range(IMAGES):
                last = mm(bank(2, C, TOPK, 8 * m), blkT[:, m, :], onehot[:, m, 0:TOPK], start=True, stop=True)
            last.then_inc(sem("p_ksel"), 1)
            pe.wait_ge(sem("rows_ready"), 2)
            for m in range(IMAGES):
                if m:
                    pe.wait_ge(sem("attn_ops"), 4 * m)
                mm(bank(0, C, NBLK), w("wk0"), R[:, m, 0:NBLK], start=True, stop=True)
                mm(bank(0, C, TOPK, 64), w("wk1"), R[:, m, 2 * NBLK:2 * NBLK + TOPK], start=True, stop=True).then_inc(sem("p_keys"), 1)
                for n, name in enumerate(("wv0", "wv1")):
                    mm(bank(1, KC, C, C * n), R[:, m, :], w(name), start=True, stop=False)
                    last = mm(bank(1, KC, C, C * n), ones[0:1, 0:KC], row[0:1, C * n:C * (n + 1)], start=False, stop=True)
                last.then_inc(sem("p_vals"), 1)
                pe.wait_ge(sem("km_ready"), m + 1)
                a4 = bank(2, C, SC).rearrange("p (j k) -> p j k", j=PAIRS)
                b4 = bank(3, 35, SC).rearrange("p (j k) -> p j k", j=PAIRS)
                mm(a4[:, :, 0:2 * NBLK], w("wq0"), KM[:, :, 0:2 * NBLK], start=True, stop=True)
                mm(a4[:, :, 2 * NBLK:KC], w("wq1"), KM[:, :, 2 * NBLK:KC], start=True, stop=True)
                mm(b4[:, :, 0:2 * NBLK], bq35[:, 0, :], KM[:, :, 0:2 * NBLK], start=True, stop=True)
                mm(b4[:, :, 2 * NBLK:KC], bq35[:, 1, :], KM[:, :, 2 * NBLK:KC], start=True, stop=True).then_inc(sem("p_fold"), 1)
            mm(bank(4, 124, C), ones[0:1, 0:124], row[0:1, 2 * C:3 * C], start=True, stop=True)
            mm(bank(4, TILE, 3, 256), n1rep[:], v(V_GW, 3), start=True, stop=False)
            mm(bank(4, TILE, 3, 256), ones[0:1, 0:TILE], row[0:1, R_GB:R_GB + 3], start=False, stop=True).then_inc(sem("p_rows"), 1)

            pe.wait_ge(sem("padded"), 4)
            pe.wait_ge(sem("tile_order"), IMAGES * BANDS)
            pe.wait_ge(sem("rows_read"), 1)
            def by_query(q):
                pe.wait_ge(sem("g_logits_read"), q + 1)
                if q >= 1:
                    pe.wait_ge(sem("g_stored"), q)
                for s in range(SUBS):
                    tr(bank(2, TILE, 4, 4 * s), ls2[q % 2][:, s, :, :].rearrange("p a n -> p (a n)"), ident[0:4, 0:4])
                for s in range(TILES):
                    last = tr(bank(2, TILE, 4, 32 + 4 * s), ls[q % 2][:, s * TILE:(s + 1) * TILE], ident[0:4, 0:4])
                last.then_inc(sem("g_byquery"), 1)

            for n, (m, which, at0, cols) in enumerate(pjobs):
                if n >= 3:
                    pe.wait_ge(sem("proj_read"), n - 2)
                if which == "k":
                    b, h = divmod(at0 // (KBAND // 2), 2)
                    src = FP[:, m, BLOCK * b:BLOCK * b + KROWS, PSIDE // 2 * h:PSIDE // 2 * (h + 1)].rearrange("p r c -> p c r")
                    dst = bank(PBANKS[n % 3], C, cols).rearrange("p (c r) -> p c r", r=KROWS)
                else:
                    src, dst = xt(m)[:, at0:at0 + cols], bank(PBANKS[n % 3], C, cols)
                mm(dst, w("wk2" if which == "k" else "wq2"), src, start=True, stop=True).then_inc(sem("proj"), 1)
                if n in VPLACES:
                    j = VPLACES.index(n)
                    vm, g, k = vjobs[j]
                    if j >= 1:
                        pe.wait_ge(sem("v_ready"), j)
                    for t in range(k):
                        pos = FP[:, vm, 8 * g + 2 * t:8 * g + 2 * t + 2, :].rearrange("p r c -> p (r c)")
                        last = mm(bank(7, 124, C, C * t), pos, w("wv2"), start=True, stop=True)
                    last.then_inc(sem("vals"), 1)
                q, step = divmod(n, 3)
                gm, b = gjobs[q]
                if step == 0:
                    if q >= 1:
                        pe.wait_ge(sem("g_centred"), q)
                    mm(bank(0, C, BAND), meanw[:], xt(gm)[:, b * BAND:(b + 1) * BAND], start=True, stop=True).then_inc(sem("g_mean"), 1)
                if step == 1:
                    pe.wait_ge(sem("g_square"), q + 1)
                    pe.wait_ge(sem("g_centred"), q + 1)
                    if q >= 1:
                        pe.wait_ge(sem("g_logits_read"), q)
                    mm(bank(1, 4, BAND), gl[:, 0, :], xc[q % 2][:], start=True, stop=False)
                    mm(bank(1, 4, BAND), gl[:, 1, :], sq[q % 2][:], start=False, stop=True).then_inc(sem("g_logits"), 1)
                if step == 0 and q >= 1:
                    by_query(q - 1)
            by_query(NGJ - 1)

            pe.wait_ge(sem("split"), NGJ)
            pe.wait_ge(sem("c_consts"), 3)
            pe.wait_ge(sem("gates"), 1)

            def c_body(i, tail):
                for k in range(CLAG if tail else CB):
                    a = at(i, k, 0, CB, CT)
                    if a:
                        num, t, r = a
                        img, c = divmod(r, TILES)
                        if not (isinstance(num, int) and num < 2):
                            pe.wait_ge(sem("c_maxed"), num - 1)
                        xs = ds(t * BAND + c * TILE, TILE)
                        s = bank(r % 2, TILE, SC)
                        mm(s, XH[:, img, xs], Ah[img][:], start=True, stop=False)
                        mm(s, XL[:, img, xs], Ah[img][:], start=False, stop=False)
                        mm(s, XH[:, img, xs], Al[img][:], start=False, stop=False)
                        mm(s, cst35[:], ES[img][:], start=False, stop=True).then_inc(sem("c_sa"), 1)
                    a = at(i, k, 1, CB, CT)
                    if a:
                        num, t, r = a
                        pe.wait_ge(sem("c_shift"), num + 1)
                        if not (isinstance(num, int) and num < 1):
                            pe.wait_ge(sem("c_shift_used"), num)
                        tr(PS[0:32, 2, 0:TILE // 2].bitcast(BF16), nmb[r % 2][:], identb[:]).then_inc(sem("c_shiftT"), 1)
                    a = at(i, k, 2, CB, CT)
                    if a:
                        num, t, r = a
                        img, c = divmod(r, TILES)
                        pe.wait_ge(sem("c_shift_used"), num + 1)
                        if not (isinstance(num, int) and num < 2):
                            pe.wait_ge(sem("c_exp"), num - 1)
                        for j in range(PAIRS):
                            s = bank(3 + r % 2, KC, TILE, TILE * j)
                            mm(s, Af[img][:, KC * j:KC * (j + 1)], XT[:, img, ds(t * BAND + c * TILE, TILE)], start=True, stop=False)
                            last = mm(s, ES[img][:, KC * j:KC * (j + 1)], MV[r % 2][:], start=False, stop=True)
                        last.then_inc(sem("c_sb"), 1)
                    a = at(i, k, 3, CB, CT)
                    if a:
                        num, t, r = a
                        img = r // TILES
                        pe.wait_ge(sem("c_exp"), num + 1)
                        if not (isinstance(num, int) and num < 1):
                            pe.wait_ge(sem("c_norm"), num)
                        for j in range(PAIRS):
                            last = mm(bank(5, TILE, 68, 68 * j), PC[r % 2][:, TILE * j:TILE * (j + 1)], VB[img][:, j, :], start=True, stop=True)
                        last.then_inc(sem("c_pv"), 1)
                    a = at(i, k, 4, CB, CT)
                    if a:
                        num, t, r = a
                        pe.wait_ge(sem("c_norm"), num + 1)
                        if not (isinstance(num, int) and num < 1):
                            pe.wait_ge(sem("c_ot"), 2 * num)
                        for ty in range(2):
                            tr(bank(6, C, TILE, TILE * ty), oc[r % 2][:, C * ty:C * (ty + 1)], ident[0:TILE, 0:TILE])
                        tr(bank(6, 3, TILE, 2 * TILE), oc[r % 2][:, 256:259], ident[0:TILE, 0:TILE]).then_inc(sem("c_tr"), 1)
                    a = at(i, k, 5, CB, CT)
                    if a:
                        num, t, r = a
                        pe.wait_ge(sem("c_ot"), 2 * num + 2)
                        if not (isinstance(num, int) and num < 1):
                            pe.wait_ge(sem("c_added"), num)
                        y = bank(7, C, TILE)
                        mm(y, w("pj0"), ot[r % 2][:, 0:TILE], start=True, stop=False)
                        mm(y, w("pj1"), ot[r % 2][:, TILE:2 * TILE], start=False, stop=False)
                        mm(y, pjrow[:], ot[r % 2][0:3, 2 * TILE:3 * TILE], start=False, stop=True)
                        mm(bank(7, C, TILE, TILE), cst[0:3, CG:CG + C], ot[r % 2][0:3, 2 * TILE:3 * TILE], start=True, stop=True).then_inc(sem("c_y"), 1)

            run_loop(pe, c_body, BANDS, True)

            pe.wait_ge(sem("c_added"), CT)
            pe.wait_ge(sem("stacks0"), 2)
            pe.wait_ge(sem("w_zeroed"), 3)

            def pslot(s, p=128):
                return PS[0:p, 2 * s:2 * s + 2, :]

            def w_body(i, ks):
                lst = pa_list(i, ks)
                for k in ks:
                    mine = [e for e in lst if e[0] == k]

                    def slot_free(last_use):
                        if not (isinstance(last_use, int) and last_use < 1):
                            pe.wait_ge(sem("w_slot_read"), last_use)

                    for _, kind, n, slot, before, last_use in mine:
                        if kind == "A":
                            num, t, r = wjob(i, n)
                            img, q = divmod(r, STEPJ)
                            c, hp = divmod(q, 4)
                            if q == 0:
                                pe.wait_ge(sem(f"band_loaded{img}"), (t + 1) * (16 * 3 * len(TERMS) // 2))
                                if isinstance(num, int) and num == STEPJ:
                                    pe.wait_ge(sem("stacks1"), 2)
                            slot_free(last_use)
                            for e in range(2):
                                h = 2 * hp + e
                                last = mm(pslot(slot, TILE)[:, e, 0:KROWS * TCOLS], Q[img][0:SHIFT0, h, c * TILE:(c + 1) * TILE],
                                          K[img][0:SHIFT0, h * KBAND + 14 * c * KROWS:h * KBAND + (14 * c + TCOLS) * KROWS], start=True, stop=True)
                            last.then_inc(sem("w_slot"), 1)
                        if kind == "S":
                            num, t, r = wjob(i, n, WB // 4, WTOT // 4)
                            pe.wait_ge(sem("w_split"), num + 1)
                            slot_free(last_use)
                            dst = PS[0:2 * HEADS, 2 * slot, 0:TILE // 2].bitcast(BF16)
                            tr(dst, wnb[r % 2][:].rearrange("p a h -> p (a h)"), identb[:]).then_inc(sem("w_slot"), 1)
                    jb = wjob(i, k)
                    if jb:
                        num, t, r = jb
                        img, q = divmod(r, STEPJ)
                        c, h2 = divmod(q, 2)
                        if q % 4 == 0:
                            par = (r // 4) % 2
                            pe.wait_ge(sem(f"w_shift{par}"), (t * (WB // 8) + (r // 8) + 1) * 16)
                        if not (isinstance(num, int) and num < 2):
                            pe.wait_ge(sem("w_exp"), num - 1)
                        for h in range(HEADS):
                            first = h * KBAND + (SUBC * c + HCOLS[0] * h2) * KROWS
                            last = mm(PS[:, 4 + r % 2, h * SUB:(h + 1) * SUB], K[img][:, first:first + 128],
                                      Q[img][:, h, c * SUB:(c + 1) * SUB], start=True, stop=True)
                        last.then_inc(sem("w_scores"), 1)
                    jb = wjob(i, k - 2)
                    if jb:
                        num, t, r = jb
                        s = r // 2
                        pe.wait_ge(sem("w_exp"), num + 1)
                        if r % 2 == 0:
                            pe.wait_ge(sem(f"w_values{s % 4}"), (t * (WB // 8) + s // 4 + 1) * 32)
                            if not (isinstance(num, int) and num < 4):
                                pe.wait_ge(sem("w_out"), t * (WB // 2) + s - 1)
                        for h in range(HEADS):
                            u, b = divmod(h, 4)
                            last = mm(PS[QUAD * b:QUAD * b + VH, 6 + s % 2, u * SUB:(u + 1) * SUB], Vw[s % 4][0:HKEYS[r % 2], r % 2, VH * h:VH * (h + 1)],
                                      P[r % 4][0:HKEYS[r % 2], SUB * h:SUB * (h + 1)], start=(r % 2 == 0 and u == 0),
                                      stop=(r % 2 == 1), skip_group_check=True)
                        last.then_inc(sem("w_products"), 1)
                    for _, kind, n, slot, before, last_use in mine:
                        if kind == "D":
                            num, t, r = wjob(i, n, 2, 2 * BANDS)
                            pe.wait_ge(sem(f"w_recips{r}"), 16 * (t + 1))
                            slot_free(last_use)
                            for u in range(2):
                                last = mm(PS[:, 2 * slot + u, 0:BAND], cst[0:4, CD:CD + C], RB[r][:, u, :], start=True, stop=True)
                            last.then_inc(sem("w_slot"), 1)
                        if kind == "Y":
                            num, t, r = wjob(i, n, 2, 2 * BANDS)
                            pe.wait_ge(sem("w_norm"), num + 1)
                            slot_free(last_use)
                            for u in range(2):
                                last = mm(PS[:, 2 * slot, 0:BAND], w("pj2", C, C * u), ON[r][:, u, :], start=(u == 0), stop=(u == 1))
                            last.then_inc(sem("w_slot"), 1)

            run_window(pe, w_body)

            pe.wait_ge(sem("w_y"), 2 * BANDS)
            job = 0

            def z_step(z):
                if z < ZB:
                    pe.wait_ge(sem("hidden"), 2 * z + 2)
                    if z == 1:
                        pe.wait_ge(sem("t_read"), 2 * IMAGES * BANDS)
                    if z >= 2:
                        pe.wait_ge(sem("z_sum"), z - 1)
                    for g2 in range(2):
                        last = mm(bank((5, 0)[z % 2], C, BAND), w("pout", C, C * g2), U[g2][:, z % URING, :], start=(g2 == 0), stop=(g2 == 1))
                    last.then_inc(sem("z_proj"), 1)
                q = z - 1
                if 0 <= q < ZB:
                    m, b = divmod(q, BANDS)
                    pe.wait_ge(sem("z_sum"), q + 1)
                    if q >= 2:
                        pe.wait_ge(sem("z_centred"), q - 1)
                    mm(bank((6, 1)[q % 2], C, BAND), meanw[:], X[:, m, b * BAND:(b + 1) * BAND], start=True, stop=True).then_inc(sem("z_mean"), 1)
                q = z - 2
                if 0 <= q < ZB:
                    pe.wait_ge(sem("z_square"), q + 1)
                    if q >= 1:
                        pe.wait_ge(sem("z_std"), q)
                    mm(bank(7, C, BAND), meanw[:], zq[q % 2][:], start=True, stop=True).then_inc(sem("z_var"), 1)

            for u in range(UNITS):
                for m, grp in PINS.get(u, []):
                    for b in range(BANDS):
                        if job >= 2:
                            pe.wait_ge(sem("t_read"), job - 1)
                        mm(bank(job % 2, C, BAND), w("pin", C, C * grp), X[:, m, b * BAND:(b + 1) * BAND], start=True, stop=True).then_inc(sem("t_proj"), 1)
                        job += 1
                n, grp = divmod(u, 2)
                m, b = divmod(n, BANDS)
                if u == 0:
                    pe.wait_ge(sem("taps"), 1)
                    pe.wait_ge(sem("y_border"), 2)
                pe.wait_ge(sem(f"y{m}_padded"), min(b + 2, BANDS))
                if u >= 3:
                    pe.wait_ge(sem("x2_read"), u - 2)
                dst = bank(2 + u % 3, C, BAND).rearrange("p (r c) -> p r c", c=SIDE)
                for t, (dy, dx) in enumerate(TAPS):
                    last = mm(dst, WT[:, t, C * grp:C * (grp + 1)], YP[:, m, BLOCK * b + 1 + dy:BLOCK * (b + 1) + 1 + dy, 1 + dx:1 + dx + SIDE],
                              start=(t == 0), stop=(t == 8))
                last.then_inc(sem("x2_conv"), 1)
                if u in ZSTEP:
                    z_step(ZSTEP[u])
            for z in range(ZLAST, ZSTEPS):
                z_step(z)

        @block.scalar
        def _(act):
            a = nc.scalar.activation
            act.wait_ge(sem("vec_loaded"), 16)
            act.wait_ge(sem("cst_loaded"), 16)
            act.wait_ge(sem("c1"), 1)
            for t in range(9):
                a(diag[:, t, :], cst[:, CI:CI + C], ACT.Copy, scale=c1[:, 0:1] if t == 4 else v(V_POSW + t)).then_inc(sem("diag"), 1)

            def tile_order(m):
                for b in range(BANDS):
                    src = FP[:, m, PAD + BLOCK * b:PAD + BLOCK * (b + 1), PAD:PAD + SIDE].rearrange("p r (s c) -> p s r c", c=SUBC)
                    dst = XT[:, m, b * BAND:(b + 1) * BAND].rearrange("p (s r c) -> p s r c", s=SUBS, c=SUBC)
                    a(dst, src, ACT.Copy).then_inc(sem("tile_order"), 1)

            for b in range(PEB):
                act.wait_ge(sem("pos_conv"), b + 1)
                dst = FP[:, 1, PAD + BLOCK * b:PAD + BLOCK * (b + 1), PAD:PAD + SIDE]
                a(dst, PS[:, 3 + b % 2, 0:BAND].rearrange("p (r c) -> p r c", c=SIDE), ACT.Identity, bias=v(V_POSB)).then_inc(sem("pos_read"), 1)
                if b == 3:
                    act.wait_ge(sem("conv_done"), 1)
                    tile_order(0)
            act.wait_ge(sem("pos_read"), PEB)
            act.wait_ge(sem("conv_last"), 1)
            tile_order(1)
            act.wait_ge(sem("p_hid"), 1)
            a(hs[:], PS[0:64, 0, 0:98], ACT.Gelu, bias=v(V_S1B, 1, 64)).then_inc(sem("hid"), 1)
            a(identb[:], cst[0:TILE, CI:CI + TILE], ACT.Copy).then_inc(sem("identb"), 1)
            for m in range(IMAGES):
                act.wait_ge(sem("tile_order"), BANDS * (m + 1))
                a(XH[:, m, :], xt(m), ACT.Copy).then_inc(sem("high"), 1)
            act.wait_ge(sem("c1"), 3)
            for n, (m, which, at0, cols) in enumerate(pjobs):
                act.wait_ge(sem("proj"), n + 1)
                if n >= RING:
                    act.wait_ge(sem("residual"), n - RING + 1)
                    act.wait_ge(sem(f"parts_stored{n % RING}"), 16 * (n // RING))
                ps = PS[:, PBANKS[n % 3], 0:cols]
                bias = v(V_BK + 2) if which == "k" else c1[:, 2:3]
                sc = 1.0 if which == "k" else SCALE
                a(pf[n % RING][:, 0:cols], ps, ACT.Identity, bias=bias, scale=sc).then_inc(sem("proj_full"), 1)
                a(pk[n % RING][:, SLOT[0], 0:cols], ps, ACT.Identity, bias=bias, scale=sc).then_inc(sem("proj_read"), 1)
                q, step = divmod(n, 3)
                if step == 0:
                    act.wait_ge(sem("g_centred"), q + 1)
                    if q >= 2:
                        act.wait_ge(sem("g_logits"), q - 1)
                    a(sq[q % 2][:], xc[q % 2][:], ACT.Square).then_inc(sem("g_square"), 1)
            act.wait_ge(sem("g_stored"), NGJ)
            g4 = G[:].rearrange("p i b s k -> p (i b s) k")
            a(gst[:], g4[:, :, 3], ACT.Sqrt, bias=epsc[0:TILE, :]).then_inc(sem("g_std"), 1)
            act.wait_ge(sem("g_shifted"), 1)
            a(g4[:, :, 0:3], g4[:, :, 0:3], ACT.Exp).then_inc(sem("g_exp"), 1)

            def c_body(i, tail):
                for k in range(CLAG if tail else CB):
                    s = at(i, k, 2, CB, CT)
                    if s:
                        num, t, r = s
                        act.wait_ge(sem("c_sb"), num + 1)
                        if not (isinstance(num, int) and num < 2):
                            act.wait_ge(sem("c_pv"), num - 1)
                        a(PC[r % 2][:], PS[0:KC, 3 + r % 2, 0:PAIRS * TILE], ACT.Exp).then_inc(sem("c_exp"), 1)
                    s = at(i, k, 4, CB, CT)
                    if s:
                        num, t, r = s
                        act.wait_ge(sem("c_tr"), num + 1)
                        if not (isinstance(num, int) and num < 2):
                            act.wait_ge(sem("c_y"), num - 1)
                        a(ot[r % 2][:, 0:2 * TILE], PS[:, 6, 0:2 * TILE], ACT.Copy).then_inc(sem("c_ot"), 1)
                        a(ot[r % 2][0:3, 2 * TILE:3 * TILE], PS[0:3, 6, 2 * TILE:3 * TILE], ACT.Copy).then_inc(sem("c_ot"), 1)

            act.wait_ge(sem("setup_done"), 2)
            run_loop(act, c_body, BANDS, True)

            act.wait_ge(sem("c_added"), CT)
            act.wait_ge(sem("stage_loaded"), 16)
            for m in range(IMAGES):
                kd = K[m][MASK0:128, 0:HEADS * KBAND].rearrange("p (h n) -> p h n", h=HEADS)
                a(kd, bc(stage[MASK0:128, 0:KBAND].unsqueeze(1), [32, HEADS, KBAND]), ACT.Copy).then_inc(sem(f"stacks{m}"), 1)

            def w_body(i, ks):
                for k in ks:
                    jb = wjob(i, k)
                    if jb:
                        num, t, r = jb
                        act.wait_ge(sem("w_scores"), num + 1)
                        if not (isinstance(num, int) and num < 4):
                            act.wait_ge(sem("w_products"), num - 3)
                        kn = HKEYS[r % 2]
                        a(P[r % 4][0:kn, :], PS[0:kn, 4 + r % 2, 0:HEADS * SUB], ACT.Exp).then_inc(sem("w_exp"), 1)
                    if k % 2 == 0:
                        s = wjob(i, k // 2 - 2, WB // 2, WTOT // 2)
                        if s:
                            num, t, r = s
                            img, c = divmod(r, SUBS)
                            act.wait_ge(sem("w_products"), 2 * num + 2)
                            if c == 0 and not (isinstance(num, int) and num < WB // 2):
                                act.wait_ge(sem("w_norm"), 2 * t + img - 1)
                            src = PS[:, 6 + r % 2, 0:2 * SUB].rearrange("p (u n) -> p u n", u=2)
                            a(OB[img][:, :, c * SUB:(c + 1) * SUB], src, ACT.Copy).then_inc(sem("w_out"), 1)

            run_window(act, w_body)

            job = 0
            act.wait_ge(sem("w_y"), 2 * BANDS)

            def z_step(z):
                q = z - 3
                if 0 <= q < ZB:
                    act.wait_ge(sem("z_scaled"), q + 1)
                    if q >= 2:
                        act.wait_ge(sem(f"z_stored{q % 2}"), 16 * (q // 2))
                    a(zo[q % 2][:], sd[q % 2][:], ACT.Identity, bias=v(V_N2B)).then_inc(sem("z_ready"), 1)
                q = z - 2
                if 0 <= q < ZB:
                    act.wait_ge(sem("z_var"), q + 1)
                    if q >= 2:
                        act.wait_ge(sem("z_ready"), q - 1)
                    a(sd[q % 2][:], PS[:, 7, 0:BAND], ACT.Sqrt, bias=epsc[:]).then_inc(sem("z_std"), 1)
                q = z - 1
                if 0 <= q < ZB:
                    act.wait_ge(sem("z_centred"), q + 1)
                    if q >= 2:
                        act.wait_ge(sem("z_var"), q - 1)
                    a(zq[q % 2][:], zc[q % 2][:], ACT.Square).then_inc(sem("z_square"), 1)

            for u in range(UNITS):
                for m, grp in PINS.get(u, []):
                    ac = AC[ACID[m, grp]]
                    if m == 1:
                        act.wait_ge(sem("conv2"), 1 + grp)
                    for b in range(BANDS):
                        act.wait_ge(sem("t_proj"), job + 1)
                        cols = slice(b * BAND, (b + 1) * BAND)
                        a(T[grp][:, cols], PS[:, job % 2, 0:BAND], ACT.Copy).then_inc(sem("t_full"), 1)
                        if (m, grp) == (1, 1):
                            act.wait_ge(sem("hidden"), 2 * b + 2)
                        a(ac[:, cols], PS[:, job % 2, 0:BAND], ACT.Copy, scale=v(V_DW + 9 * grp + 4)).then_inc(sem("t_read"), 1)
                        job += 1
                n, grp = divmod(u, 2)
                act.wait_ge(sem("x2_conv"), u + 1)
                if n >= URING:
                    act.wait_ge(sem("z_proj"), n - URING + 1)
                a(U[grp][:, n % URING, :], PS[:, 2 + u % 3, 0:BAND], ACT.Copy).then_inc(sem("x2_read"), 1)
                if u in ZSTEP:
                    z_step(ZSTEP[u])
                if u in GELUS:
                    m = GELUS[u]
                    for grp in range(2):
                        act.wait_ge(sem("conv2"), 2 * m + grp + 1)
                        ac = AC[ACID[m, grp]]
                        a(ac[:], ac[:], ACT.Gelu).then_inc(sem("gelu"), 1)
            for z in range(ZLAST, ZSTEPS):
                z_step(z)

        @block.vector
        def _(dve):
            ve = nc.vector
            chain = [0]

            def link(ins):
                chain[0] += 1
                ins.then_inc(sem("v_chain"), 1)
                dve.wait_ge(sem("v_chain"), chain[0])

            dve.wait_ge(sem("vec_loaded"), 16)
            ve.tensor_scalar(c1[:, 0:1], v(V_POSW + 4), 1.0, None, ALU.add).then_inc(sem("c1"), 1)
            ve.memset(gl[:], 0.0).then_inc(sem("c1"), 1)
            ve.tensor_scalar(c1[:, 2:3], v(V_BQ + 2), SCALE, None, ALU.mult).then_inc(sem("c1"), 1)
            dve.wait_ge(sem("c1"), 3)

            def tap(t, src, dst, wcol, first=0):
                dy, dx = TAPS[t]
                ro = max(first, -dy)
                rn = min(SIDE, SIDE - dy) - ro
                co, cn = max(0, -dx), SIDE - abs(dx)
                o = dst(ro, rn, co, cn)
                return ve.scalar_tensor_tensor(out=o, in0=src(ro + dy, rn, co + dx, cn), scalar=v(wcol + t), in1=o, op0=ALU.mult, op1=ALU.add)

            for m in range(IMAGES):
                inner = FP[:, m, PAD:PAD + SIDE, PAD:PAD + SIDE]
                first = BLOCK * PEB if m else 0
                dve.wait_ge(sem(f"x{m}_loaded"), 16)
                xi = X[:, m, :].rearrange("p (r c) -> p r c", c=SIDE)
                link(ve.tensor_scalar(inner[:, first:, :], xi[:, first:, :], c1[:, 0:1], v(V_POSB), ALU.mult, ALU.add))
                for t in SIDE_TAPS:
                    link(tap(t, lambda r, rn, c, cn: xi[:, r:r + rn, c:c + cn], lambda r, rn, c, cn: inner[:, r:r + rn, c:c + cn], V_POSW, first))
                if m:
                    ve.memset(c1[0:1, 3:4], 0.0).then_inc(sem("conv_last"), 1)
                    dve.wait_ge(sem("pos_read"), PEB)
                ve.tensor_reduce(bs1[:, m, :, :], inner.rearrange("p r (b c) -> p r b c", c=BLOCK), AX.X, ALU.add).then_inc(sem("conv_done"), 1)
            for m in range(IMAGES):
                dve.wait_ge(sem("conv_done"), m + 1)
                src = bs1[:, m, :, :].rearrange("p (y r) b -> p y b r", r=BLOCK)
                link(ve.tensor_reduce(blk[:, m, :].rearrange("p (y b) -> p y b", b=NBS), src, AX.X, ALU.add))
            ve.tensor_scalar(blk[:], blk[:], 1.0 / BLOCK ** 2, None, ALU.mult).then_inc(sem("blk_ready"), 1)
            dve.wait_ge(sem("loaded"), 16 * 3)
            dve.wait_ge(sem("cst_loaded"), 16)
            dve.wait_ge(sem("p_blkT"), 1)
            ve.tensor_copy(blkT[:], PS[0:NBLK, 1, 0:2 * C].rearrange("p (i c) -> p i c", i=IMAGES)).then_inc(sem("blkT"), 1)
            dve.wait_ge(sem("p_score"), 1)
            link(ve.tensor_scalar(score[:], PS[0:1, 0, 128:128 + 98].rearrange("p (i n) -> p i n", i=IMAGES), row[0:1, R_S2B:R_S2B + 1], None, ALU.add))
            for m in range(IMAGES):
                link(ve.max(top[:, m, :], score[:, m, :]))
            for m in range(IMAGES):
                link(ve.max_index(topi[:, m, :], top[:, m, :], score[:, m, :]))
            ve.tensor_copy(topf[:], topi[:]).then_inc(sem("topf"), 1)
            dve.wait_ge(sem("p_idx"), 1)
            ve.tensor_scalar(onehot[:], PS[0:NBLK, 0, 256:272].rearrange("p (i n) -> p i n", i=IMAGES), cst[0:NBLK, CIO:CIO + 1], None, ALU.is_equal).then_inc(sem("onehot"), 1)
            ve.tensor_scalar(gl[:, 0, 0:3], v(V_GW, 3), v(V_N1W), None, ALU.mult).then_inc(sem("c1"), 1)
            ve.memset(gl[:, 1, 3:4], 1.0 / C).then_inc(sem("c1"), 1)
            link(ve.tensor_copy(n1rep[:], bc(v(V_N1B), [128, TILE])))
            for n in range(2):
                link(ve.tensor_copy(bq35[:, n, :], bc(v(V_BQ + n), [128, 35])))
            r4 = R[:, :, 0:2 * NBLK].rearrange("p i (e n) -> p i e n", e=2)
            for e in range(2):
                link(ve.tensor_copy(r4[:, :, e, :], blk[:]))
            dve.wait_ge(sem("p_ksel"), 1)
            for e in range(2):
                ve.tensor_copy(R[:, :, 2 * NBLK + TOPK * e:2 * NBLK + TOPK * (e + 1)],
                               PS[:, 2, 0:16].rearrange("p (i n) -> p i n", i=IMAGES)[:, :, 0:TOPK]).then_inc(sem("rows_ready"), 1)
            for m in range(IMAGES):
                dve.wait_ge(sem("p_keys"), m + 1)
                link(ve.tensor_scalar(k0[:], PS[:, 0, 0:NBLK], v(V_BK), SCALE, ALU.add, ALU.mult))
                link(ve.tensor_scalar(k1[:], PS[:, 0, 64:64 + TOPK], v(V_BK + 1), SCALE, ALU.add, ALU.mult))
                hm = cst[:, CH:CH + HEADS].rearrange("p (j e) -> p j e", e=2)
                for e in range(2):
                    for kk, o, n in ((k0, NBLK * e, NBLK), (k1, 2 * NBLK + TOPK * e, TOPK)):
                        last = ve.tensor_tensor(KM[:, :, o:o + n], bc(kk[:].unsqueeze(1), [128, PAIRS, n]), bc(hm[:, :, e:e + 1], [128, PAIRS, n]), ALU.mult)
                        if (e, n) != (1, TOPK):
                            link(last)
                last.then_inc(sem("km_ready"), 1)
                dve.wait_ge(sem("p_vals"), m + 1)
                for n in range(2):
                    vf = PS[0:KC, 1, C * n:C * (n + 1)].rearrange("p (j d) -> p j d", j=PAIRS)
                    vm = cst[0:KC, CVM + 32 * n:CVM + 32 * (n + 1)]
                    ve.tensor_tensor(VB[m][:, :, 32 * n:32 * (n + 1)], vf, bc(vm.unsqueeze(1), [KC, PAIRS, 32]), ALU.mult).then_inc(sem("attn_ops"), 1)
                ve.tensor_copy(VB[m][:, :, 64:68], bc(cst[0:KC, CVM + 64:CVM + 68].unsqueeze(1), [KC, PAIRS, 4])).then_inc(sem("attn_ops"), 1)
                dve.wait_ge(sem("p_fold"), m + 1)
                link(ve.tensor_copy(Af[m][:], PS[:, 2, 0:SC]))
                link(ve.tensor_copy(Ah[m][:], Af[m][:]))
                link(ve.tensor_tensor(Al[m][:], Af[m][:], Ah[m][:], ALU.subtract))
                link(ve.tensor_copy(cs[:], PS[0:35, 3, 0:SC]))
                prev = cst[0:35, CE:CE + SC]
                for part in range(3):
                    link(ve.tensor_copy(chb[:], cs[:]))
                    dst = ES[m] if part == 2 else ch[part]
                    link(ve.scalar_tensor_tensor(out=dst[:], in0=chb[:], scalar=cst[0:35, CM + part:CM + part + 1], in1=prev, op0=ALU.mult, op1=ALU.add))
                    prev = ch[part][:]
                    if part < 2:
                        link(ve.tensor_tensor(cs[:], cs[:], chb[:], ALU.subtract))
                ve.memset(c1[:, 4 + m:5 + m], 0.0).then_inc(sem("attn_ops"), 1)
            dve.wait_ge(sem("p_rows"), 1)
            link(ve.tensor_copy(BV2[:], PS[0:124, 4, 0:C]))
            ve.tensor_copy(cg[:], PS[0:TILE, 4, 256:259]).then_inc(sem("rows_read"), 1)
            for n in range(NPJ + 1):
                if n < NPJ:
                    cols = pjobs[n][3]
                    dve.wait_ge(sem("proj_read"), n + 1)
                    dve.wait_ge(sem("proj_full"), n + 1)
                    if n >= 3:
                        dve.wait_ge(sem("parts_ready"), n - 2)
                    ve.tensor_tensor(pr[n % 3][:, 0:cols], pf[n % RING][:, 0:cols], pk[n % RING][:, SLOT[0], 0:cols], ALU.subtract).then_inc(sem("residual"), 1)
                    q, step = divmod(n, 3)
                    gm, b = gjobs[q]
                    if step == 0:
                        dve.wait_ge(sem("g_mean"), q + 1)
                        if q >= 2:
                            dve.wait_ge(sem("g_logits"), q - 1)
                        ve.tensor_tensor(xc[q % 2][:], xt(gm)[:, b * BAND:(b + 1) * BAND], PS[:, 0, 0:BAND], ALU.subtract).then_inc(sem("g_centred"), 1)
                if n >= 1:
                    cols = pjobs[n - 1][3]
                    dve.wait_ge(sem("residual"), n)
                    ve.tensor_copy(pk[(n - 1) % RING][:, SLOT[1], 0:cols], pr[(n - 1) % 3][:, 0:cols]).then_inc(sem("second_part"), 1)
                if n < NPJ:
                    if n in VPLACES:
                        j = VPLACES.index(n)
                        vm, g, k = vjobs[j]
                        dve.wait_ge(sem("vals"), j + 1)
                        if j >= 2:
                            dve.wait_ge(sem(f"v_stored{j % 2}"), 16 * (j // 2))
                        o = vst[j % 2][:, 0:k, :].rearrange("p t (j d) -> p (t j) d", d=VH)[:, :, 0:DH]
                        i0 = PS[0:124, 7, 0:C * k].rearrange("p (t d) -> p t d", d=DH)
                        for t in range(k):
                            last = ve.tensor_tensor(o[:, HEADS * t:HEADS * (t + 1), :], i0[:, HEADS * t:HEADS * (t + 1), :],
                                                    BV2[:].rearrange("p (j d) -> p j d", j=HEADS), ALU.add)
                        last.then_inc(sem("v_ready"), 1)
                    if step == 1:
                        dve.wait_ge(sem("g_logits"), q + 1)
                        ve.tensor_copy(ls[q % 2][:], PS[0:4, 1, 0:BAND])
                        ve.tensor_copy(ls2[q % 2][:], bc(PS[0:4, 1, 0:BAND].rearrange("p (s n) -> p s n", n=SUB).unsqueeze(2), [4, SUBS, 2, SUB])).then_inc(sem("g_logits_read"), 1)
                if n % 3 == 0 and n >= 3:
                    gm, b = gjobs[n // 3 - 1]
                    dve.wait_ge(sem("g_byquery"), n // 3)
                    ve.tensor_copy(G[:, gm, b, :, :], PS[0:TILE, 2, 0:48].rearrange("p (s k) -> p s k", k=4)).then_inc(sem("g_stored"), 1)
            g4 = G[:].rearrange("p i b s k -> p (i b s) k")
            g3 = g4[:, :, 0:3]
            dve.wait_ge(sem("g_stored"), NGJ)
            dve.wait_ge(sem("g_std"), 1)
            link(ve.reciprocal(gst[:], gst[:]))
            link(ve.tensor_tensor(g3, g3, bc(gst[:].unsqueeze(2), [TILE, NG, 3]), ALU.mult))
            link(ve.tensor_tensor(g3, g3, bc(cg[:].unsqueeze(1), [TILE, NG, 3]), ALU.add))
            link(ve.tensor_reduce(gmx[:], g3, AX.X, ALU.max))
            ve.tensor_tensor(g3, g3, bc(gmx[:].unsqueeze(2), [TILE, NG, 3]), ALU.subtract).then_inc(sem("g_shifted"), 1)
            dve.wait_ge(sem("g_exp"), 1)
            link(ve.tensor_reduce(gst[:], g3, AX.X, ALU.add))
            link(ve.reciprocal(gmx[:], gst[:]))
            link(ve.tensor_tensor(g3, g3, bc(gmx[:].unsqueeze(2), [TILE, NG, 3]), ALU.mult))
            ve.memset(c1[:, 6:7], 0.0).then_inc(sem("gates"), 1)
            ve.memset(c1[:, 7:8], 0.0).then_inc(sem("setup_done"), 2)

            def c_body(i, tail):
                for k in range(CLAG if tail else CB):
                    s = at(i, k, 0, CB, CT)
                    if s:
                        num, t, r = s
                        dve.wait_ge(sem("c_sa"), num + 1)
                        if not (isinstance(num, int) and num < 1):
                            dve.wait_ge(sem("c_shift"), num)
                        s4 = PS[0:TILE, r % 2, 0:SC].rearrange("p (j k) -> p j k", j=PAIRS)
                        o = nm[:].rearrange("p (t j e) -> p t j e", t=2, e=2)
                        ve.tensor_reduce(o[:, 0, :, :], s4[:, :, 0:2 * NBLK].rearrange("p j (e n) -> p j e n", e=2), AX.X, ALU.max, negate=True).then_inc(sem("c_max1"), 1)
                        ve.tensor_reduce(o[:, 1, :, :], s4[:, :, 2 * NBLK:KC].rearrange("p j (e n) -> p j e n", e=2), AX.X, ALU.max, negate=True).then_inc(sem("c_maxed"), 1)
                        dve.wait_ge(sem("c_maxed"), num + 1)
                        dve.wait_ge(sem("c_max1"), num + 1)
                        if not (isinstance(num, int) and num < 2):
                            dve.wait_ge(sem("c_shiftT"), num - 1)
                        ve.tensor_copy(nmb[r % 2][:, 0:16], nm[:]).then_inc(sem("c_high"), 1)
                        dve.wait_ge(sem("c_high"), num + 1)
                        ve.tensor_tensor(nmb[r % 2][:, 16:32], nm[:], nmb[r % 2][:, 0:16], ALU.subtract).then_inc(sem("c_shift"), 1)
                    s = at(i, k, 1, CB, CT)
                    if s:
                        num, t, r = s
                        dve.wait_ge(sem("c_shiftT"), num + 1)
                        if not (isinstance(num, int) and num < 2):
                            dve.wait_ge(sem("c_sb"), num - 1)
                        ve.tensor_copy(MV[r % 2][0:32, :], PS[0:32, 2, 0:TILE // 2].bitcast(BF16)).then_inc(sem("c_shift_used"), 1)
                    s = at(i, k, 3, CB, CT)
                    if s:
                        num, t, r = s
                        img, c = divmod(r, TILES)
                        dve.wait_ge(sem("c_pv"), num + 1)
                        if not (isinstance(num, int) and num < 1):
                            dve.wait_ge(sem("c_norm"), num)
                        if not (isinstance(num, int) and num < 2):
                            dve.wait_ge(sem("c_tr"), num - 1)
                        pv = PS[0:TILE, 5, 0:68 * PAIRS].rearrange("p (j k) -> p j k", j=PAIRS)
                        gg = G[:, img, ds(t, 1), 8 + c, 0:2] if not isinstance(t, int) else G[:, img, t:t + 1, 8 + c, 0:2]
                        ve.reciprocal(rd[:].rearrange("p a j e -> p j a e"), pv[:, :, 64:68].rearrange("p j (a e) -> p j a e", e=2)).then_inc(sem("c_recip"), 1)
                        dve.wait_ge(sem("c_recip"), num + 1)
                        for ty in range(2):
                            ve.tensor_scalar(rg[:, ty, :, :], rd[:, ty, :, :], gg[:, 0, ty:ty + 1], None, ALU.mult).then_inc(sem("c_gated"), 1)
                        dve.wait_ge(sem("c_gated"), 2 * num + 2)
                        ve.tensor_scalar(oc[r % 2][:, 256:259], G[:, img, ds(t, 1), 8 + c, 0:3].rearrange("p a k -> p (a k)") if not isinstance(t, int) else G[:, img, t, 8 + c, 0:3], 1.0, None, ALU.mult).then_inc(sem("c_gcol"), 1)
                        dve.wait_ge(sem("c_gcol"), num + 1)
                        for ty in range(2):
                            o = oc[r % 2][:, C * ty:C * (ty + 1)].rearrange("p (j e d) -> p j e d", e=2, d=DH)
                            last = ve.tensor_tensor(o, pv[:, :, 32 * ty:32 * (ty + 1)].rearrange("p j (e d) -> p j e d", e=2),
                                                    bc(rg[:, ty, :, :].unsqueeze(3), [TILE, PAIRS, 2, DH]), ALU.mult)
                        last.then_inc(sem("c_norm"), 1)
                    s = at(i, k, 5, CB, CT)
                    if s:
                        num, t, r = s
                        img, c = divmod(r, TILES)
                        dve.wait_ge(sem("c_y"), num + 1)
                        xs = XT[:, img, ds(t * BAND + c * TILE, TILE)]
                        ve.tensor_copy(GB[:, img, ds(t * BAND + c * TILE, TILE)], PS[:, 7, TILE:2 * TILE])
                        ve.tensor_tensor(xs, PS[:, 7, 0:TILE], xs, ALU.add).then_inc(sem("c_added"), 1)

            run_loop(dve, c_body, BANDS, True)

            dve.wait_ge(sem("c_added"), CT)
            for b in (6, 7):
                ve.memset(PS[:, b, 0:2 * SUB], 0.0).then_inc(sem("w_zeroed"), 1)
            dve.wait_ge(sem("stage_loaded"), 16)
            for m in range(IMAGES):
                ve.tensor_copy(Q[m][MASK0:128, :, :], bc(stage[MASK0:128, KBAND:KBAND + BAND].unsqueeze(1), [32, HEADS, BAND])).then_inc(sem(f"stacks{m}"), 1)

            def w_body(i, ks):
                lst = pa_list(i, ks)
                for k in ks:
                    mine = [e for e in lst if e[0] == k]

                    def paj(kinds):
                        for _, kind, n, slot, before, last_use in mine:
                            if kind not in kinds:
                                continue
                            dve.wait_ge(sem("w_slot"), before + 1)
                            if kind == "A":
                                num, t, r = wjob(i, n)
                                tl, hp = divmod(r, 4)
                                if hp == 0 and not (isinstance(num, int) and num < 8):
                                    dve.wait_ge(sem("w_split"), t * (WB // 4) + tl - 1)
                                src = PS[0:TILE, 2 * slot:2 * slot + 2, 0:KROWS * TCOLS]
                                ve.tensor_reduce(wn[tl % 2][:, 2 * hp:2 * hp + 2], src, AX.X, ALU.max, negate=True).then_inc(sem("w_slot_read"), 1)
                                if hp == 3:
                                    dve.wait_ge(sem("w_slot_read"), before + 1)
                                    if not (isinstance(num, int) and num < 8):
                                        dve.wait_ge(sem("w_slot"), before - 5)
                                    ve.tensor_copy(wnb[tl % 2][:, 0, :], wn[tl % 2][:]).then_inc(sem("w_high"), 1)
                                    dve.wait_ge(sem("w_high"), t * (WB // 4) + tl + 1)
                                    ve.tensor_tensor(wnb[tl % 2][:, 1, :], wn[tl % 2][:], wnb[tl % 2][:, 0, :], ALU.subtract).then_inc(sem("w_split"), 1)
                            if kind == "S":
                                num, t, r = wjob(i, n, WB // 4, WTOT // 4)
                                if not (isinstance(num, int) and num < 2):
                                    dve.wait_ge(sem(f"w_shift{r % 2}"), (t * (WB // 8) + r // 2) * 16)
                                src = PS[0:2 * HEADS, 2 * slot, 0:TILE // 2].bitcast(BF16)
                                ve.tensor_copy(nT[r % 2][:], src).then_inc(sem("w_slot_read"), 1)
                            if kind == "D":
                                num, t, r = wjob(i, n, 2, 2 * BANDS)
                                if not (isinstance(num, int) and num < 2):
                                    dve.wait_ge(sem("w_y"), num - 1)
                                dve.wait_ge(sem("w_out"), SUBS * num + SUBS)
                                ve.tensor_tensor(ON[r][:], OB[r][:], PS[:, 2 * slot:2 * slot + 2, 0:BAND], ALU.mult).then_inc(sem("w_norm"), 1)
                                dve.wait_ge(sem("w_norm"), num + 1)
                                ve.memset(c1[0:1, 5:6], 0.0).then_inc(sem("w_slot_read"), 1)
                            if kind == "Y":
                                num, t, r = wjob(i, n, 2, 2 * BANDS)
                                if not (isinstance(num, int) and num < 1):
                                    dve.wait_ge(sem("w_y"), num)
                                ve.tensor_tensor(yt[:], PS[:, 2 * slot, 0:BAND], GB[:, r, ds(t * BAND, BAND)], ALU.mult).then_inc(sem("w_slot_read"), 1)
                                o = X[:, r, ds(t * BAND, BAND)].rearrange("p (r s c) -> p s r c", s=SUBS, c=SUBC)
                                xs = XT[:, r, ds(t * BAND, BAND)].rearrange("p (s r c) -> p s r c", s=SUBS, c=SUBC)
                                dve.wait_ge(sem("w_slot_read"), before + 1)
                                ve.tensor_tensor(o, yt[:].rearrange("p (s r c) -> p s r c", s=SUBS, c=SUBC), xs, ALU.add).then_inc(sem("w_y"), 1)

                    if k % 16 == 7:
                        s = wjob(i, (k - 23) // 16, 2, 2 * BANDS)
                        if s is not None:
                            num, t, r = s
                            dve.wait_ge(sem(f"w_sums{r}"), 16 * (t + 1))
                            ve.reciprocal(SR[r][:], SR[r][:]).then_inc(sem("w_recip"), 1)
                    paj("ASDY")

            run_window(dve, w_body)

            dve.wait_ge(sem("w_y"), 2 * BANDS)
            for b in range(BANDS):
                xs = X[:, 0, b * BAND:(b + 1) * BAND].rearrange("p (r c) -> p r c", c=SIDE)
                ve.tensor_copy(YP[:, 0, 1 + BLOCK * b:1 + BLOCK * (b + 1), 1:1 + SIDE], xs).then_inc(sem("y0_padded"), 1)
            dve.wait_ge(sem("taps_loaded"), 16)
            ve.tensor_tensor(WT[:], WT[:], bc(w("pin", HID, HID).unsqueeze(1), [128, 9, HID]), ALU.mult).then_inc(sem("taps"), 1)

            def product(n):
                m, b = divmod(n, BANDS)
                dve.wait_ge(sem("gelu"), 2 * m + 2)
                dve.wait_ge(sem("x2_read"), 2 * n + 2)
                for grp in range(2):
                    un = U[grp][:, n % URING, :]
                    ve.tensor_tensor(un, AC[ACID[m, grp]][:, b * BAND:(b + 1) * BAND], un, ALU.mult).then_inc(sem("hidden"), 1)

            def z_step(z):
                if z < ZB:
                    m, b = divmod(z, BANDS)
                    dve.wait_ge(sem("z_proj"), z + 1)
                    xs = X[:, m, b * BAND:(b + 1) * BAND]
                    ve.tensor_tensor(xs, PS[:, (5, 0)[z % 2], 0:BAND], xs, ALU.add).then_inc(sem("z_sum"), 1)
                q = z - 2
                if 0 <= q < ZB:
                    dve.wait_ge(sem("z_std"), q + 1)
                    ve.reciprocal(sd[q % 2][:], sd[q % 2][:]).then_inc(sem("z_rstd"), 1)
                    dve.wait_ge(sem("z_rstd"), q + 1)
                    dve.wait_ge(sem("z_centred"), q + 1)
                    ve.scalar_tensor_tensor(out=sd[q % 2][:], in0=zc[q % 2][:], scalar=v(V_N2W), in1=sd[q % 2][:], op0=ALU.mult, op1=ALU.mult).then_inc(sem("z_scaled"), 1)
                q = z - 1
                if 0 <= q < ZB:
                    m, b = divmod(q, BANDS)
                    dve.wait_ge(sem("z_mean"), q + 1)
                    if q >= 2:
                        dve.wait_ge(sem("z_scaled"), q - 1)
                        dve.wait_ge(sem("z_square"), q - 1)
                    ve.tensor_tensor(zc[q % 2][:], X[:, m, b * BAND:(b + 1) * BAND], PS[:, (6, 1)[q % 2], 0:BAND], ALU.subtract).then_inc(sem("z_centred"), 1)

            PRODUCTS = {0: [0, 1, 2, 3], 4: [4], 7: [5, 6]}
            for q in range(2 * IMAGES):
                m, grp = divmod(q, 2)
                dve.wait_ge(sem("t_read"), BANDS * (q + 1))
                dve.wait_ge(sem("t_full"), BANDS * (q + 1))
                ti = T[grp][:].rearrange("p (r c) -> p r c", c=SIDE)
                ai = AC[ACID[m, grp]][:].rearrange("p (r c) -> p r c", c=SIDE)
                for n, t in enumerate(SIDE_TAPS):
                    ins = tap(t, lambda r, rn, c, cn: ti[:, r:r + rn, c:c + cn], lambda r, rn, c, cn: ai[:, r:r + rn, c:c + cn], V_DW + 9 * grp)
                    if n == len(SIDE_TAPS) - 1:
                        ins.then_inc(sem("conv2"), 1)
                    else:
                        link(ins)
                    step = 8 * grp + n
                    if m:
                        for p in PRODUCTS.get(step, []):
                            product(p)
                        if step >= 9:
                            z_step(step - 9)
            product(BANDS)
            for z in range(BANDS, ZSTEPS):
                if z + 1 < ZB:
                    product(z + 1)
                z_step(z)


_OUT = (IMAGES, C, SIDE, SIDE)


def kernel(**inputs):
    import concourse.bacc as _bacc
    from concourse.bass_utils import run_bass_kernel_spmd as _run

    a = {n.replace("L0_conv_", ""): np.ascontiguousarray(t) for n, t in inputs.items()}
    def dh(t):
        return t.reshape(HEADS, DH, -1).transpose(1, 0, 2).reshape(t.shape)

    pj2 = np.zeros((4, QUAD, 2, C), np.float32)
    pj2[:, 0:DH] = a["pj_w"][2].T.reshape(2, 4, DH, C).transpose(1, 2, 0, 3)
    wts = np.concatenate(
        [a["wq_w"][0], a["wq_w"][1], dh(a["wq_w"][2]).T, a["wk_w"][0].T, a["wk_w"][1].T, dh(a["wk_w"][2]).T,
         a["wv_w"][0].T, a["wv_w"][1].T, a["wv_w"][2].T, a["pj_w"][0].T, a["pj_w"][1].T,
         a["s1_w"].T, a["pin_w"].T, a["pout_w"].T[0:C], a["pout_w"].T[C:], pj2.reshape(C, 2 * C)], 1)
    vecs = np.zeros((128, NV), np.float32)
    vecs[:, V_POSW:V_POSW + 9] = a["pos_w"].reshape(C, 9)
    for col, name in ((V_POSB, "pos_b"), (V_N1W, "n1_w"), (V_N1B, "n1_b"), (V_N2W, "n2_w"), (V_N2B, "n2_b")):
        vecs[:, col] = a[name]
    vecs[:, V_BQ:V_BQ + 3] = a["wq_b"].T
    vecs[:, V_BK:V_BK + 3] = a["wk_b"].T
    vecs[:, V_BQ + 2], vecs[:, V_BK + 2] = dh(a["wq_b"][2]), dh(a["wk_b"][2])
    for g in range(4):
        vecs[:, V_DW + 9 * g:V_DW + 9 * (g + 1)] = a["dw_w"].reshape(9, 2 * HID)[:, C * g:C * (g + 1)].T
    vecs[0:64, V_S1B] = a["s1_b"]
    vecs[0:64, V_S2] = a["s2_w"][0]
    vecs[:, V_GW:V_GW + 3] = a["g_w"].T
    rows = np.concatenate([a["wv_b"].reshape(-1), a["g_b"], a["s2_b"]])[None]
    dwr = np.ascontiguousarray(a["dw_w"].reshape(9, 2 * HID)[:, HID:]).reshape(1, 9 * HID)
    c32, cmask = shape_constants()
    arrays = {"x": a["x"].reshape(IMAGES, C, PIX), "wts": wts, "vecs": vecs, "rows": rows, "pjb": a["pj_b"], "dwr": dwr, "c32": c32, "cmask": cmask}
    nc = _bacc.Bacc("TRN2", target_bir_lowering=False, num_devices=1)
    args = {n: nc.dram_tensor(f"in_{n}", t.shape, mybir.dt.from_np(t.dtype), kind="ExternalInput").ap() for n, t in arrays.items()}
    out = nc.dram_tensor("out_y", (IMAGES, C, PIX), F32, kind="ExternalOutput").ap()
    build(nc, out=out, **args)
    r = _run(nc, [{f"in_{n}": np.ascontiguousarray(t) for n, t in arrays.items()}], core_ids=[0])
    return r.results[0]["out_y"].reshape(_OUT)
```
